# Optimizing a Trainium2 kernel written in Bass

```python
import numpy as np
import jax
import jax.numpy as jnp

def _softmax(x, axis=-1):
    return jax.nn.softmax(x, axis=axis)

def _gelu(x):
    return jax.nn.gelu(x, approximate=True)

def _silu(x):
    return jax.nn.silu(x)

def _sigmoid(x):
    return jax.nn.sigmoid(x)

def _layernorm(x, axis=-1, eps=1e-05):
    m = jnp.mean(x, axis=axis, keepdims=True)
    v = jnp.var(x, axis=axis, keepdims=True)
    return (x - m) / jnp.sqrt(v + eps)

def _scatter_add(tgt, idx, src, axis=0):
    return tgt.at[idx].add(src)

def _segment_sum(src, seg, n):
    return jax.ops.segment_sum(src, seg, n)
kernel_name = 'mk_cond_seq_d2_seqx_r2_0f648b'

def setup_inputs(seed: int=0):
    np.random.seed(seed)
    _w = jnp.asarray

    def _rec_inputs():
        import jax
        import jax.numpy as jnp
        _rk = jax.random.key(seed)
        x = 3.843e-05 + 0.9999 * jax.random.normal(jax.random.fold_in(_rk, 1), (8, 512, 512), jnp.float32)
        _lenS = 512 - jax.random.randint(jax.random.fold_in(_rk, 7), (8,), 0, max(1, 512 // 4) + 1, jnp.int32)
        _lenS2 = 512 - jax.random.randint(jax.random.fold_in(_rk, 8), (8,), 0, max(1, 512 // 4) + 1, jnp.int32)
        fside_BxS_0 = 0.0125939 + 0.993166 * jax.random.normal(jax.random.fold_in(_rk, 11), (8, 512), jnp.float32)
        cond_1024 = 0.00516053 + 0.988656 * jax.random.normal(jax.random.fold_in(_rk, 12), (8, 512), jnp.float32)
        return (x, fside_BxS_0, cond_1024)
    x, fside_BxS_0, cond_1024 = _rec_inputs()

    def _L0_cond_setup():
        import jax, jax.numpy as jnp
        import numpy as np
        B, S, D = (8, 512, 512)
        EPS = 1e-05

        def _layernorm(h, g, b):
            mu = jnp.mean(h, axis=-1, keepdims=True)
            var = jnp.mean((h - mu) ** 2, axis=-1, keepdims=True)
            return (h - mu) * jax.lax.rsqrt(var + EPS) * g + b
        key = jax.random.key(seed)
        ks = jax.random.split(key, 16)

        def lin(k, fan_in, fan_out):
            bound = 1.0 / np.sqrt(fan_in)
            k1, k2 = jax.random.split(k)
            W = jax.random.uniform(k1, (fan_in, fan_out), jnp.float32, -bound, bound)
            b = jax.random.uniform(k2, (fan_out,), jnp.float32, -bound, bound)
            return (W, b)
        Wq, bq = lin(ks[0], D, D)
        Wk, bk = lin(ks[1], D, D)
        Wv, bv = lin(ks[2], D, D)
        W1, b1 = lin(ks[3], D, 4 * D)
        W2, b2 = lin(ks[4], 4 * D, D)
        Wc, bc = lin(ks[5], 2 * D, 6 * D)
        return {'x': jax.random.normal(ks[6], (B, S, D), jnp.float32), 't': jax.random.normal(ks[7], (B, D), jnp.float32), 'c': jax.random.normal(ks[8], (B, D), jnp.float32), 'Wq': Wq, 'bq': bq, 'Wk': Wk, 'bk': bk, 'Wv': Wv, 'bv': bv, 'W1': W1, 'b1': b1, 'W2': W2, 'b2': b2, 'Wc': Wc, 'bc': bc, 'ln1_g': jnp.ones((D,), jnp.float32), 'ln1_b': jnp.zeros((D,), jnp.float32), 'ln2_g': jnp.ones((D,), jnp.float32), 'ln2_b': jnp.zeros((D,), jnp.float32)}
    _L0_cond_all = _L0_cond_setup()
    _L0_cond_in = {k: v for k, v in _L0_cond_all.items() if k in ('Wq', 'bq', 'Wk', 'bk', 'Wv', 'bv', 'W1', 'b1', 'W2', 'b2', 'Wc', 'bc', 'ln1_g', 'ln1_b', 'ln2_g', 'ln2_b')}
    del _L0_cond_all

    def _L1_cond_setup():
        import jax, jax.numpy as jnp
        import numpy as np
        DIM = 512
        HEADS = 16
        HEAD_DIM = DIM // HEADS
        MLP = 4 * DIM
        EPS = 1e-05

        def layer_norm(x, g, b):
            mu = jnp.mean(x, axis=-1, keepdims=True)
            var = jnp.var(x, axis=-1, keepdims=True)
            return (x - mu) * jax.lax.rsqrt(var + EPS) * g + b

        def rope_cos_sin(n, d):
            inv_freq = 1.0 / 10000.0 ** (jnp.arange(0, d, 2, dtype=jnp.float32) / d)
            t = jnp.arange(n, dtype=jnp.float32)
            freqs = jnp.outer(t, inv_freq)
            emb = jnp.concatenate([freqs, freqs], -1)
            return (jnp.cos(emb), jnp.sin(emb))

        def rotate_half(x):
            x1, x2 = (x[..., ::2], x[..., 1::2])
            return jnp.concatenate([-x2, x1], axis=-1)
        key = jax.random.key(seed)
        ks = jax.random.split(key, 16)
        B, N = (2, 1024)
        s = lambda fan_in: 1.0 / np.sqrt(fan_in)
        inp = {'x': jax.random.normal(ks[0], (B, N, DIM), jnp.float32), 't_emb': jax.random.normal(ks[1], (B, DIM), jnp.float32), 'norm1_g': jnp.ones((DIM,), jnp.float32), 'norm1_b': jnp.zeros((DIM,), jnp.float32), 'Wq': jax.random.normal(ks[2], (DIM, DIM), jnp.float32) * s(DIM), 'Wk': jax.random.normal(ks[3], (DIM, DIM), jnp.float32) * s(DIM), 'Wv': jax.random.normal(ks[4], (DIM, DIM), jnp.float32) * s(DIM), 'Wo': jax.random.normal(ks[5], (DIM, DIM), jnp.float32) * s(DIM), 'norm2_g': jnp.ones((DIM,), jnp.float32), 'norm2_b': jnp.zeros((DIM,), jnp.float32), 'W1': jax.random.normal(ks[6], (DIM, MLP), jnp.float32) * s(DIM), 'W2': jax.random.normal(ks[7], (MLP, DIM), jnp.float32) * s(MLP), 'ada_W': jax.random.normal(ks[8], (DIM, 6 * DIM), jnp.float32) * s(DIM), 'ada_b': jnp.zeros((6 * DIM,), jnp.float32)}
        return inp
    _L1_cond_all = _L1_cond_setup()
    _L1_cond_in = {k: v for k, v in _L1_cond_all.items() if k in ('norm1_g', 'norm1_b', 'Wq', 'Wk', 'Wv', 'Wo', 'norm2_g', 'norm2_b', 'W1', 'W2', 'ada_W', 'ada_b')}
    del _L1_cond_all
    return {'x': x, 'fside_BxS_0': fside_BxS_0, 'cond_1024': cond_1024, 'L0_cond_Wq': _L0_cond_in['Wq'], 'L0_cond_bq': _L0_cond_in['bq'], 'L0_cond_Wk': _L0_cond_in['Wk'], 'L0_cond_bk': _L0_cond_in['bk'], 'L0_cond_Wv': _L0_cond_in['Wv'], 'L0_cond_bv': _L0_cond_in['bv'], 'L0_cond_W1': _L0_cond_in['W1'], 'L0_cond_b1': _L0_cond_in['b1'], 'L0_cond_W2': _L0_cond_in['W2'], 'L0_cond_b2': _L0_cond_in['b2'], 'L0_cond_Wc': _L0_cond_in['Wc'], 'L0_cond_bc': _L0_cond_in['bc'], 'L0_cond_ln1_g': _L0_cond_in['ln1_g'], 'L0_cond_ln1_b': _L0_cond_in['ln1_b'], 'L0_cond_ln2_g': _L0_cond_in['ln2_g'], 'L0_cond_ln2_b': _L0_cond_in['ln2_b'], 'L1_cond_norm1_g': _L1_cond_in['norm1_g'], 'L1_cond_norm1_b': _L1_cond_in['norm1_b'], 'L1_cond_Wq': _L1_cond_in['Wq'], 'L1_cond_Wk': _L1_cond_in['Wk'], 'L1_cond_Wv': _L1_cond_in['Wv'], 'L1_cond_Wo': _L1_cond_in['Wo'], 'L1_cond_norm2_g': _L1_cond_in['norm2_g'], 'L1_cond_norm2_b': _L1_cond_in['norm2_b'], 'L1_cond_W1': _L1_cond_in['W1'], 'L1_cond_W2': _L1_cond_in['W2'], 'L1_cond_ada_W': _L1_cond_in['ada_W'], 'L1_cond_ada_b': _L1_cond_in['ada_b']}

def reference(x, fside_BxS_0, cond_1024, L0_cond_Wq, L0_cond_bq, L0_cond_Wk, L0_cond_bk, L0_cond_Wv, L0_cond_bv, L0_cond_W1, L0_cond_b1, L0_cond_W2, L0_cond_b2, L0_cond_Wc, L0_cond_bc, L0_cond_ln1_g, L0_cond_ln1_b, L0_cond_ln2_g, L0_cond_ln2_b, L1_cond_norm1_g, L1_cond_norm1_b, L1_cond_Wq, L1_cond_Wk, L1_cond_Wv, L1_cond_Wo, L1_cond_norm2_g, L1_cond_norm2_b, L1_cond_W1, L1_cond_W2, L1_cond_ada_W, L1_cond_ada_b):
    import jax
    import jax.numpy as jnp

    def _L0_cond_ref(x, t, c, Wq, bq, Wk, bk, Wv, bv, W1, b1, W2, b2, Wc, bc, ln1_g, ln1_b, ln2_g, ln2_b):
        import jax, jax.numpy as jnp
        import numpy as np
        B, S, D = (8, 512, 512)
        EPS = 1e-05

        def _layernorm(h, g, b):
            mu = jnp.mean(h, axis=-1, keepdims=True)
            var = jnp.mean((h - mu) ** 2, axis=-1, keepdims=True)
            return (h - mu) * jax.lax.rsqrt(var + EPS) * g + b
        dim = x.shape[-1]
        cond = jnp.concatenate([t, c], axis=-1) @ Wc + bc
        a1, g1, be1, a2, g2, be2 = jnp.split(cond[:, None, :], 6, axis=-1)
        h = _layernorm(x, ln1_g, ln1_b) * (1.0 + g1) + be1
        Q = h @ Wq + bq
        K = h @ Wk + bk
        V = h @ Wv + bv
        scores = jnp.einsum('bsd,btd->bst', Q, K) / jnp.sqrt(jnp.float32(dim))
        attn = jax.nn.softmax(scores, axis=-1) @ V
        x = x + a1 * attn
        h = _layernorm(x, ln2_g, ln2_b) * (1.0 + g2) + be2
        h = jax.nn.gelu(h @ W1 + b1, approximate=False)
        h = jax.nn.gelu(h @ W2 + b2, approximate=False)
        x = x + a2 * h
        return x

    def _L1_cond_ref(x, t_emb, norm1_g, norm1_b, Wq, Wk, Wv, Wo, norm2_g, norm2_b, W1, W2, ada_W, ada_b):
        import jax, jax.numpy as jnp
        import numpy as np
        DIM = 512
        HEADS = 16
        HEAD_DIM = DIM // HEADS
        MLP = 4 * DIM
        EPS = 1e-05

        def layer_norm(x, g, b):
            mu = jnp.mean(x, axis=-1, keepdims=True)
            var = jnp.var(x, axis=-1, keepdims=True)
            return (x - mu) * jax.lax.rsqrt(var + EPS) * g + b

        def rope_cos_sin(n, d):
            inv_freq = 1.0 / 10000.0 ** (jnp.arange(0, d, 2, dtype=jnp.float32) / d)
            t = jnp.arange(n, dtype=jnp.float32)
            freqs = jnp.outer(t, inv_freq)
            emb = jnp.concatenate([freqs, freqs], -1)
            return (jnp.cos(emb), jnp.sin(emb))

        def rotate_half(x):
            x1, x2 = (x[..., ::2], x[..., 1::2])
            return jnp.concatenate([-x2, x1], axis=-1)
        B, N, C = x.shape
        H, D = (HEADS, HEAD_DIM)
        scale = D ** (-0.5)
        mod = jax.nn.silu(t_emb) @ ada_W + ada_b
        shift_msa, scale_msa, gate_msa, shift_mlp, scale_mlp, gate_mlp = jnp.split(mod, 6, axis=-1)
        xn = layer_norm(x, norm1_g, norm1_b) * (1 + scale_msa[:, None, :]) + shift_msa[:, None, :]
        q = (xn @ Wq).reshape(B, N, H, D).transpose(0, 2, 1, 3)
        k = (xn @ Wk).reshape(B, N, H, D).transpose(0, 2, 1, 3)
        v = (xn @ Wv).reshape(B, N, H, D).transpose(0, 2, 1, 3)
        cos, sin = rope_cos_sin(N, D)
        q = q * cos + rotate_half(q) * sin
        k = k * cos + rotate_half(k) * sin
        attn = jnp.einsum('bhnd,bhmd->bhnm', q, k) * scale
        attn = jax.nn.softmax(attn, axis=-1)
        out = jnp.einsum('bhnm,bhmd->bhnd', attn, v)
        out = out.transpose(0, 2, 1, 3).reshape(B, N, C) @ Wo
        x = x + gate_msa[:, None, :] * out
        xn = layer_norm(x, norm2_g, norm2_b) * (1 + scale_mlp[:, None, :]) + shift_mlp[:, None, :]
        mlp = jax.nn.gelu(xn @ W1, approximate=False) @ W2
        x = x + gate_mlp[:, None, :] * mlp
        return x
    x = _L0_cond_ref(x, fside_BxS_0, cond_1024, L0_cond_Wq, L0_cond_bq, L0_cond_Wk, L0_cond_bk, L0_cond_Wv, L0_cond_bv, L0_cond_W1, L0_cond_b1, L0_cond_W2, L0_cond_b2, L0_cond_Wc, L0_cond_bc, L0_cond_ln1_g, L0_cond_ln1_b, L0_cond_ln2_g, L0_cond_ln2_b)
    x = _L1_cond_ref(x, cond_1024, L1_cond_norm1_g, L1_cond_norm1_b, L1_cond_Wq, L1_cond_Wk, L1_cond_Wv, L1_cond_Wo, L1_cond_norm2_g, L1_cond_norm2_b, L1_cond_W1, L1_cond_W2, L1_cond_ada_W, L1_cond_ada_b)
    return x

_drawn_inputs = setup_inputs


def setup_inputs(seed=0):
    import zlib

    import numpy as np

    out = dict(_drawn_inputs(seed))
    spreads = {'L0_cond_ln1_g': (1.0, 0.6),
     'L0_cond_ln1_b': (0.0, 0.1),
     'L0_cond_ln2_g': (1.0, 0.6),
     'L0_cond_ln2_b': (0.0, 0.8),
     'L1_cond_norm1_g': (1.0, 0.2),
     'L1_cond_norm1_b': (0.0, 0.1),
     'L1_cond_norm2_g': (1.0, 0.2),
     'L1_cond_norm2_b': (0.0, 0.1),
     'L1_cond_ada_b': (0.0, 0.1)}
    factors = {'L0_cond_Wq': 3.433,
     'L0_cond_bq': 8.0,
     'L0_cond_Wk': 3.399,
     'L0_cond_bk': 8.0,
     'L0_cond_bv': 3.356,
     'L0_cond_b1': 8.0,
     'L0_cond_b2': 8.0,
     'L0_cond_bc': 5.898}
    for name, (base, spread) in spreads.items():
        noise = np.random.default_rng([zlib.crc32(name.encode()), seed]).standard_normal(out[name].shape)
        drawn = base * np.exp(spread * noise) if base else spread * noise
        out[name] = jnp.asarray(drawn.astype(out[name].dtype))
    for name, factor in factors.items():
        out[name] = (out[name] * factor).astype(out[name].dtype)
    return out
```

```python
from contextlib import ExitStack

import concourse.bass as bass
import numpy as np
from concourse import mybir

F32 = mybir.dt.float32
F32R = mybir.dt.float32r
ACT = mybir.ActivationFunctionType
ALU = mybir.AluOpType
AX = mybir.AxisListType

B, S, D = 8, 512, 512
P = 128
KC = D // P
TT = S // P
FF = 4 * D
FC = FF // P
H = 16
HD = D // H
HG = P // HD
EPS = 1e-5
SCALE0 = float(D) ** -0.5
SCALE1 = float(HD) ** -0.5
PA, PB, PC, PD = range(4)
TURN_TRANSPOSES = [KC, KC, KC + 3 * H, KC]
W_UNITS = [6, FC, 8, FC]
W_FIRST = [0, 6, 6 + FC, 14 + FC]


def seq(phase, n):
    return n + B * phase


def transposes_before(phase, n):
    return KC + sum([KC * B, KC * B, (KC + 3 * H) * B][:phase]) + TURN_TRANSPOSES[phase] * n


N_CONST = 21
LN_STEPS = 14
MOD_STEPS = 16
T_ORDER = [(0, 0), (0, 1), (0, 2), (1, 0), (1, 1)]
for _h in range(H):
    T_ORDER += [x for x in ((_h + 2, 0), (_h + 2, 1), (_h + 1, 2)) if x[0] < H]
T_USE = {x: i for i, x in enumerate(T_ORDER)}


def build(nc, a):
    ctx = ExitStack()
    with ctx:
        def sb(name, shape, dt=F32):
            return ctx.enter_context(nc.sbuf_tensor(name, shape, dt))

        def sem(name):
            return ctx.enter_context(nc.semaphore(name))

        R = sb("pe_operands", [P, 40960], F32R)
        W_SLOT = 2048

        def r(at, *shape):
            ap = R[:, at:at + int(np.prod(shape))]
            return ap if len(shape) == 1 else ap.rearrange("p (a b) -> p a b", b=shape[-1])

        XH, XL = r(32768, KC, S), r(34816, KC, S)
        A_W = [[r(W_SLOT * (2 * w + part), KC, D) for part in range(2)] for w in range(3)]
        A_QH, A_QL, A_KH, A_KL, A_VH, A_VL, A_PH, A_PL = [r(12288 + 2048 * i, 4, 512) for i in range(8)]
        SLOT_OF = {PB: [(j + 14) % FC for j in range(FC)], PD: list(range(FC))}

        def w_chunk(phase, j):
            base = W_SLOT * SLOT_OF[phase][j]
            return (r(base, KC, P), r(base + 1024, KC, P)), (r(base + 512, D), r(base + 1536, D))

        HH = [r(36864 + 1024 * i, 512) for i in range(4)]
        HL = [r(36864 + 1024 * i + 512, 512) for i in range(4)]
        C_W = [[r(W_SLOT * (2 * w + part), KC, D) for part in range(2)] for w in range(4)]
        VS = r(16384, TT, H * 96)
        VSH = VS.rearrange("p t (h c) -> p t h c", c=96)
        QS = [r(22528 + 384 * i, TT, 96) for i in range(2)]
        KS = [r(23296 + 384 * i, TT, 96) for i in range(2)]
        QT = [r(24064 + 1024 * i, S) for i in range(3)]
        KT = [r(24576 + 1024 * i, S) for i in range(3)]
        PTH = [r(at, TT, S) for at in (27136, 36864)]
        PTL = [r(at, TT, S) for at in (29184, 38912)]
        OTH, OTL = XH, XL
        MM = sb("minus_max_split", [P, 3, TT, 2], F32R)
        ID_R = sb("identity_r", [P, P], F32R)

        F = sb("work", [P, 12288])

        def f(at, *shape):
            ap = F[:, at:at + int(np.prod(shape))]
            return ap if len(shape) == 1 else ap.rearrange("p (a b) -> p a b", b=shape[-1])

        XLN, Y, XRES = f(0, TT, D), f(2048, KC, S), f(4096, TT, D)
        TMP = [f(6144, 512), f(6656, 512)]
        GATE = f(7168, 512)
        A_P = f(7680, TT, S)
        A_VT = [f(9728, 512), f(10240, 512)]
        BV = f(10752, 512)
        HID = [f(7680 + 512 * i, 512) for i in range(4)]
        B2 = f(9728, 512)
        KF, QF = XLN, Y
        PE = [f(7680 + 512 * i, 512) for i in range(3)]
        DEN = [f(9216, 512), f(9728, 512)]
        OA = [f(10240, 512), f(10752, 512)]
        SL, RC = f(11264, 512), f(11776, 512)
        ROT = [SL, RC]
        STAGE = sb("weight_stage", [P, 2, 1024])
        STAGE_W = [F[:, 4096 * i:4096 * (i + 1)] for i in range(2)]
        GROW, GBIAS = F[0:B, 8192:10240], F[0:B, 10240:12288]
        COND_ROWS = F[0:B, 0:1024]
        VEC_ROWS = F[0:104, 1024:1152]
        ID_F = sb("identity", [P, P])
        MINUS_HALF = sb("minus_half", [P, TT])
        COS, SIN = sb("cos", [P, TT, HD]), sb("sin", [P, TT, HD])
        CT = sb("cond_T", [P, 8, B])
        ST_ = sb("silu_T", [P, 4, B])
        SE = sb("silu_exp", [P, 4, B])
        VEC = sb("vectors_T", [P, 104])
        MOD = sb("mod_T", [P, 4, 4, B])
        LN_SCALE = sb("ln_scale", [P, 4, KC, B])
        LN_SHIFT = sb("ln_shift", [P, 4, KC, B])
        STATS = sb("bn_stats", [P, TT, 6])
        MV = sb("mean_var", [P, TT, 2])
        VEPS, RSTD = sb("var_eps", [P, TT]), sb("rstd", [P, TT])
        MX, NB, SM, RS = sb("row_max", [P, 4]), sb("minus_scaled_max", [P, 4]), sb("row_sum", [P, 4]), sb("row_sum_inv", [P, 4])
        MX1 = sb("row_max_heads", [P, 3, TT])

        PS = ctx.enter_context(nc.psum_tensor("psum", [P, 8, 512], F32))
        VECQ, VECK, VECB1 = 80, 84, 88

        x_mid = [nc.dram_tensor(f"x_after_{c}", (B, S, D), F32, kind="Internal").ap() for c in "abc"]
        gates_d = nc.dram_tensor("gates", (4, B, D), F32, kind="Internal").ap()
        x_in = [a["x"], *x_mid]
        x_out = [*x_mid, a["out"]]

        def tokens(ap, n):
            return ap[bass.ds(n, 1)].rearrange("o (t p) d -> p (o t) d", p=P)

        const_ld, vec_done, const_evac, consts = sem("const_loaded"), sem("const_transposed"), sem("const_evacuated"), sem("pool_consts")
        idr_rdy, silu_a = sem("identity_r_ready"), sem("silu_steps")
        modw_ld, modw_done = [sem("mod_weights_0"), sem("mod_weights_1")], sem("mod_products")
        mod_steps, gates_st = sem("mod_steps"), sem("gates_stored")
        gate_evac = sem("gate_evacuated")
        w_ld, w_split = [sem("weights_0"), sem("weights_1")], sem("weights_split")
        xln_ld, ln_v, ln_rstd = sem("ln_input_loaded"), sem("ln_steps"), sem("rstd_ready")
        t_done, t_evac = sem("transposed"), sem("transpose_evacuated")
        y_rdy, xh_rdy, xl_rdy = sem("y_ready"), sem("xh_ready"), sem("xl_ready")
        res_ld, gate_ld, tmp_rdy, res_step, res_done, stored = (
            sem("residual_loaded"), sem("gate_loaded"), sem("branch_ready"), sem("gated"), sem("residual_added"), sem("stored"))
        row_ld = sem("bias_rows_loaded")
        a_qkv, a_qkh, a_evac, a_vhi, a_vlo = sem("a_qkv_done"), sem("a_qk_hi"), sem("a_qkv_evacuated"), sem("a_v_hi"), sem("a_v_lo")
        a_s, a_mx, a_exp, a_pp, a_ppa, a_ppe, a_rs = (sem("a_scores"), sem("a_max"), sem("a_exp"), sem("a_probs_T"),
                                                     sem("a_probs_T_hi"), sem("a_probs_T_lo"), sem("a_row_sum_inv"))
        a_pv = sem("a_attn")
        m_up = {ph: sem(f"up_done_{ph}") for ph in (PB, PD)}
        m_gelu = {ph: sem(f"gelu_{ph}") for ph in (PB, PD)}
        m_hi = {ph: sem(f"hidden_hi_{ph}") for ph in (PB, PD)}
        m_lo = {ph: sem(f"hidden_lo_{ph}") for ph in (PB, PD)}
        m_down = {ph: sem(f"down_done_{ph}") for ph in (PB, PD)}
        b_gelu = sem("b_out_gelu")
        c_ones, c_qkv, c_rot, c_evac, c_rope, c_vhi = sem("c_ones"), sem("c_qkv_done"), sem("c_rot_steps"), sem("c_qkv_evacuated"), sem("c_rope"), sem("c_v_hi")
        c_stack, c_s, c_max, c_mm, c_st, c_exp = sem("c_stacks"), sem("c_scores"), sem("c_max"), sem("c_minus_max"), sem("c_scores_T"), sem("c_exp")
        c_phd, c_pha, c_pl = sem("c_probs_hi_dve"), sem("c_probs_hi_act"), sem("c_probs_lo")
        c_o, c_ocp, c_oadd, c_rc, c_on, c_oh, c_ol = (sem("c_attn"), sem("c_attn_copied"), sem("c_attn_summed"), sem("c_denominator_inv"),
                                                     sem("c_attn_normalised"), sem("c_attn_hi"), sem("c_attn_lo"))
        c_wo, c_woe = sem("c_out_done"), sem("c_out_evacuated")

        def since(eng, semaphore, value):
            if not isinstance(value, int) or value > 0:
                eng.wait_ge(semaphore, value)

        def operand_free(eng, phase, n):
            if phase < 0:
                return
            s, per = [(a_qkv, 12), (m_up[PB], FC), (c_wo, TT), (m_up[PD], FC)][phase]
            since(eng, s, per * n + per)

        def transposes_c(n, h, what):
            return transposes_before(PC, n) + (T_USE[h, what] + 1 if h >= 0 else 0)

        def after(phase, n, last):
            if not last:
                return phase, n + 1
            return (phase + 1, 0) if phase < PD else None

        def over_sequences(eng, body, phase):
            body(phase, 0, True, False)
            with eng.Fori(1, B - 1) as n:
                body(phase, n, False, False)
            body(phase, B - 1, False, True)

        block = ctx.enter_context(nc.Block())

        @block.sync
        def _(sp):
            sp.dma_start(COND_ROWS[:, 0:512], a["fside"]).then_inc(const_ld, 16)
            sp.dma_start(COND_ROWS[:, 512:1024], a["cond"]).then_inc(const_ld, 16)
            at = 0
            for name in ("bc", "ada_b", "ln1_g", "ln1_b", "ln2_g", "ln2_b", "n1_g", "n1_b", "n2_g", "n2_b", "bq", "bk", "b1"):
                rows = a[name].shape[0] // P
                sp.dma_start(VEC_ROWS[at:at + rows, :], a[name].rearrange("(r c) -> r c", c=P)).then_inc(const_ld, 16)
                at += rows
            sp.dma_start(COS[:], a["cos"].rearrange("(t p) d -> p t d", p=P)).then_inc(const_ld, 16)
            sp.dma_start(SIN[:], a["sin"].rearrange("(t p) d -> p t d", p=P)).then_inc(const_ld, 16)
            for g in range(4):
                src = a[("bc", "ada_b")[g // 2]][(0, 3, 2, 5)[g] * D:((0, 3, 2, 5)[g] + 1) * D]
                sp.dma_start(GBIAS[:, g * D:(g + 1) * D], src.partition_broadcast(B)).then_inc(const_ld, 16)

            def load_unit(u):
                slot = u % 2
                since(sp, w_split, 2 * (u - 1))
                phase = max(p for p in range(4) if W_FIRST[p] <= u)
                j = u - W_FIRST[phase]
                if phase in (PA, PC):
                    w = a[(("Wq0", "Wk0", "Wv0"), ("Wq1", "Wk1", "Wv1", "Wo1"))[phase == PC][j // 2]]
                    src = w.rearrange("(k p) n -> p k n", p=P)[:, 2 * (j % 2):2 * (j % 2) + 2, :]
                    sp.dma_start(STAGE[:, slot, :].rearrange("p (k n) -> p k n", n=D), src).then_inc(w_ld[slot], 16)
                else:
                    w1, w2 = (a["W1_0"], a["W2_0"]) if phase == PB else (a["W1_1"], a["W2_1"])
                    sp.dma_start(STAGE[:, slot, 0:512].rearrange("p (k n) -> p k n", n=P),
                                 w1.rearrange("(k p) n -> p k n", p=P)[:, :, j * P:(j + 1) * P]).then_inc(w_ld[slot], 16)
                    sp.dma_start(STAGE[:, slot, 512:1024], w2[j * P:(j + 1) * P, :]).then_inc(w_ld[slot], 16)

            for blk in range(12):
                slot = blk % 2
                if blk == 0:
                    sp.wait_ge(const_evac, 3)
                since(sp, modw_done, blk - 1)
                w = a["Wc"] if blk < 6 else a["ada_W"]
                k = 8 if blk < 6 else 4
                sp.dma_start(STAGE_W[slot][:, 0:k * D].rearrange("p (k n) -> p k n", n=D),
                             w.rearrange("(k p) n -> p k n", p=P)[:, :, (blk % 6) * D:(blk % 6 + 1) * D]).then_inc(modw_ld[slot], 16)
                if blk < 2:
                    load_unit(blk)
            sp.wait_ge(gate_evac, 4)
            sp.dma_start(gates_d.rearrange("g b d -> b g d"), GROW.rearrange("b (g d) -> b g d", d=D)).then_inc(gates_st, 16)

            def load_ln(phase, n):
                if phase > PA:
                    since(sp, stored, 16 * (seq(phase - 1, n) + 1))
                first = isinstance(n, int) and n == 0
                if phase == PC and not first:
                    sp.wait_ge(c_stack, 4 * H * n)
                elif phase == PD and first:
                    sp.wait_ge(c_stack, 4 * H * B)
                elif first:
                    sp.wait_ge(t_done, transposes_before(phase - 1, B - 1))
                else:
                    sp.wait_ge(t_done, transposes_before(phase, n) - TURN_TRANSPOSES[phase])
                sp.dma_start(XLN, tokens(x_in[phase], n)).then_inc(xln_ld, 16)

            def load_residual(phase, n):
                turn = seq(phase, n)
                since(sp, stored, 16 * turn)
                sp.dma_start(XRES, tokens(x_in[phase], n)).then_inc(res_ld, 16)
                sp.dma_start(GATE, gates_d[phase, bass.ds(n, 1), :].rearrange("o d -> (o d)").partition_broadcast(P)).then_inc(gate_ld, 16)

            sp.wait_ge(modw_done, 12)
            for u in range(2, 6):
                load_unit(u)
            sp.dma_start(XLN, tokens(x_in[PA], 0)).then_inc(xln_ld, 16)
            sp.wait_ge(gates_st, 16)
            load_residual(PA, 0)
            sp.dma_start(BV, a["bv"].partition_broadcast(P)).then_inc(row_ld, 16)

            def body(phase, n, first, last):
                if first and phase in (PB, PD):
                    for j in range(2, 6):
                        load_unit(W_FIRST[phase] + j)
                nxt = after(phase, n, last)
                if nxt:
                    load_ln(*nxt)
                if first and phase in (PB, PD):
                    for j in range(6, FC):
                        load_unit(W_FIRST[phase] + j)
                if last and phase < PD:
                    for j in range(8 if phase == PB else 2):
                        load_unit(W_FIRST[phase + 1] + j)
                sp.wait_ge(res_done, TT * (seq(phase, n) + 1))
                sp.dma_start(tokens(x_out[phase], n), XRES).then_inc(stored, 16)
                if nxt:
                    load_residual(*nxt)
                if last and phase == PA:
                    sp.dma_start(B2, a["b2"].partition_broadcast(P)).then_inc(row_ld, 16)

            for phase in range(4):
                over_sequences(sp, body, phase)
            sp.wait_ge(stored, 16 * 4 * B)

        @block.gpsimd
        def _(pool):
            pool.memset(ID_F[:], 0.0).then_inc(consts, 1)
            pool.memset(MINUS_HALF[:], -0.5).then_inc(consts, 1)
            pool.wait_ge(consts, 2)
            pool.affine_select(out=ID_F[:], in_=ID_F[:], compare_op=ALU.not_equal, fill=1.0, base=0,
                               pattern=[[-1, P]], channel_multiplier=1).then_inc(consts, 1)

            def rstd(turn):
                pool.wait_ge(ln_v, LN_STEPS * turn + 10)
                pool.tensor_tensor(RSTD[:], VEPS[:], MINUS_HALF[:], ALU.pow).then_inc(ln_rstd, 1)

            def add_residual(phase, n):
                turn = seq(phase, n)
                pool.wait_ge(res_ld, 16 * (turn + 1))
                for t in range(TT):
                    if phase == PB:
                        pool.wait_ge(gate_ld, 16 * (turn + 1))
                        pool.wait_ge(b_gelu, TT * n + t + 1)
                        pool.tensor_tensor(TMP[t % 2], TMP[t % 2], GATE, ALU.mult).then_inc(res_step, 1)
                        pool.wait_ge(res_step, TT * n + t + 1)
                    else:
                        pool.wait_ge(tmp_rdy, TT * (turn) + t + 1)
                    pool.tensor_tensor(XRES[:, t], XRES[:, t], TMP[t % 2], ALU.add).then_inc(res_done, 1)

            rstd(0)

            def plain_body(phase, n, first, last):
                nxt = after(phase, n, last)
                if nxt:
                    rstd(seq(*nxt))
                add_residual(phase, n)

            def c_body(phase, n, first, last):
                for u in range(2 * TT):
                    dst = (QF, KF)[u // TT][:, u % TT]
                    pool.wait_ge(c_evac, 12 * n + u + 1)
                    pool.tensor_tensor(dst, dst, ROT[u % 2], ALU.add).then_inc(c_rope, 1)
                for h in range(H + 1):
                    if h >= HG and (h % HG == 1 or h == H):
                        g = (h - 1) // HG - 1 if h < H else KC - 1
                        pool.wait_ge(c_rc, KC * n + g + 1)
                        pool.tensor_tensor(OA[g % 2], OA[g % 2], RC, ALU.mult).then_inc(c_on, 1)
                    if h < H:
                        for t in range(TT):
                            if t < 3:
                                pool.wait_ge(c_phd, 48 * n + 3 * h + t + 1)
                            else:
                                pool.wait_ge(c_pha, H * n + h + 1)
                            pool.tensor_tensor(PTL[h % 2][:, t], PE[(TT * h + t) % 3], PTH[h % 2][:, t].bitcast(F32),
                                               ALU.subtract).then_inc(c_pl, 1)
                    if h == 14:
                        nxt = after(phase, n, last)
                        if nxt:
                            rstd(seq(*nxt))
                    if h >= HG and (h % HG == 1 or h == H):
                        g = (h - 1) // HG - 1 if h < H else KC - 1
                        pool.wait_ge(c_oh, KC * n + g + 1)
                        pool.tensor_tensor(OTL[:, g], OA[g % 2], OTH[:, g].bitcast(F32), ALU.subtract).then_inc(c_ol, 1)
                add_residual(phase, n)

            for phase in range(4):
                over_sequences(pool, c_body if phase == PC else plain_body, phase)

        @block.vector
        def _(dve):
            dve.wait_ge(consts, 3)
            dve.tensor_copy(ID_R[:], ID_F[:]).then_inc(idr_rdy, 1)
            dve.wait_ge(vec_done, 1)
            dve.tensor_copy(CT[:], PS[:, 0, 0:64].rearrange("p (k b) -> p k b", b=B)).then_inc(const_evac, 1)
            dve.tensor_copy(VEC[:], PS[:, 0, 64:168]).then_inc(const_evac, 1)
            dve.wait_ge(const_evac, 2)
            dve.wait_ge(silu_a, 1)
            dve.tensor_scalar(SE[:], SE[:], 1.0, None, ALU.add).then_inc(silu_a, 1)
            dve.wait_ge(silu_a, 2)
            dve.reciprocal(SE[:], SE[:]).then_inc(silu_a, 1)
            dve.wait_ge(silu_a, 3)
            dve.tensor_tensor(ST_[:], CT[:, 4:8], SE[:], ALU.mult).then_inc(const_evac, 1)

            def split_unit(u, dst_hi, dst_lo, w_count):
                slot = u % 2
                dve.wait_ge(w_ld[slot], w_count)
                dve.tensor_copy(dst_hi, STAGE[:, slot, :]).then_inc(w_split, 1)
                dve.wait_ge(w_split, 2 * u + 1)
                dve.tensor_tensor(dst_lo, STAGE[:, slot, :], dst_hi.bitcast(F32), ALU.subtract).then_inc(w_split, 1)

            arrived = []
            count = [0, 0]
            for u in range(sum(W_UNITS)):
                phase = max(p for p in range(4) if W_FIRST[p] <= u)
                count[u % 2] += 16 if phase in (PA, PC) else 32
                arrived.append(count[u % 2])

            def split_square(phase, j):
                u = W_FIRST[phase] + j
                base = W_SLOT * 2 * (j // 2) + 1024 * (j % 2)
                split_unit(u, R[:, base:base + 1024], R[:, base + W_SLOT:base + W_SLOT + 1024], arrived[u])

            def split_chunk(phase, j):
                u = W_FIRST[phase] + j
                base = W_SLOT * SLOT_OF[phase][j]
                split_unit(u, R[:, base:base + 1024], R[:, base + 1024:base + 2048], arrived[u])

            for j in range(2):
                split_square(PA, j)
            steps = 0
            for layer in range(2):
                dve.wait_ge(modw_done, 6 * layer + 6)
                for half in range(2):
                    v0 = ((1, 4), (0, 3))[layer][half]
                    bias = VEC[:, 24 * layer + 4 * v0:24 * layer + 4 * v0 + 8]
                    dst = MOD[:, 2 * half:2 * half + 2].rearrange("p v f b -> p (v f) b")
                    src = PS[:, 1 + layer, 64 * half:64 * half + 64].rearrange("p (v b) -> p v b", b=B)
                    since(dve, mod_steps, steps)
                    dve.tensor_tensor(dst, src, bias.unsqueeze(2).broadcast_to([P, 8, B]), ALU.add).then_inc(mod_steps, 1)
                    steps += 1
                dve.wait_ge(mod_steps, steps)
                for half in range(2):
                    ln = 2 * layer + half
                    m_g, m_b = ((MOD[:, 2 * half], MOD[:, 2 * half + 1]), (MOD[:, 2 * half + 1], MOD[:, 2 * half]))[layer]
                    gain = VEC[:, 48 + 8 * ln:52 + 8 * ln].unsqueeze(2).broadcast_to([P, KC, B])
                    offset = VEC[:, 52 + 8 * ln:56 + 8 * ln].unsqueeze(2).broadcast_to([P, KC, B])
                    dve.scalar_tensor_tensor(LN_SCALE[:, ln], m_g, 1.0, gain, ALU.add, ALU.mult).then_inc(mod_steps, 1)
                    dve.scalar_tensor_tensor(LN_SHIFT[:, ln], m_g, 1.0, offset, ALU.add, ALU.mult).then_inc(mod_steps, 1)
                    steps += 2
                    dve.wait_ge(mod_steps, steps)
                    dve.tensor_tensor(LN_SHIFT[:, ln], LN_SHIFT[:, ln], m_b, ALU.add).then_inc(mod_steps, 1)
                    steps += 1
                for half in range(2):
                    g = 2 * layer + half
                    dve.tensor_tensor(GROW[:, g * D:(g + 1) * D], PS[0:B, 3 + g, :], GBIAS[:, g * D:(g + 1) * D],
                                      ALU.add).then_inc(gate_evac, 1)
            assert steps == MOD_STEPS
            for j in range(2, 6):
                split_square(PA, j)

            def ln_stats(turn):
                dve.wait_ge(xln_ld, 16 * (turn + 1))
                since(dve, ln_v, LN_STEPS * turn)
                for t in range(TT):
                    dve.bn_stats(STATS[:, t], XLN[:, t]).then_inc(ln_v, 1)
                dve.wait_ge(ln_v, LN_STEPS * turn + 4)
                dve.memset(VEPS[:], EPS).then_inc(ln_v, 1)
                for t in range(TT):
                    dve.bn_aggr(MV[:, t], STATS[:, t]).then_inc(ln_v, 1)
                dve.wait_ge(ln_v, LN_STEPS * turn + 9)
                dve.tensor_tensor(VEPS[:], MV[:, :, 1], VEPS[:], ALU.add).then_inc(ln_v, 1)

            def ln_norm(turn):
                dve.wait_ge(ln_rstd, turn + 1)
                for t in range(TT):
                    dve.tensor_scalar(XLN[:, t], XLN[:, t], MV[:, t, 0:1], RSTD[:, t:t + 1], ALU.subtract, ALU.mult).then_inc(ln_v, 1)

            def split_x(turn):
                for k in range(KC):
                    dve.wait_ge(xh_rdy, KC * turn + k + 1)
                    dve.tensor_tensor(XL[:, k], Y[:, k], XH[:, k].bitcast(F32), ALU.subtract).then_inc(xl_rdy, 1)

            def tmp_free(turn, t):
                since(dve, res_done, TT * turn + t - 1)

            ln_stats(0)
            ln_norm(0)
            split_x(0)

            def a_body(phase, n, first, last):
                turn = seq(phase, n)
                nxt = after(phase, n, last)
                for u in range(2 * KC):
                    hi, lo, vec = ((A_QH, A_QL, VECQ), (A_KH, A_KL, VECK))[u // KC]
                    k = u % KC
                    dve.wait_ge(a_qkh, 8 * n + u + 1)
                    dve.scalar_tensor_tensor(lo[:, k], PS[:, u % 4, :], VEC[:, vec + k:vec + k + 1], hi[:, k].bitcast(F32),
                                             ALU.add, ALU.subtract).then_inc(a_evac, 1)
                    if u == 2 and nxt:
                        ln_stats(seq(*nxt))
                    if u == 4 and nxt:
                        ln_norm(seq(*nxt))
                if first:
                    dve.wait_ge(row_ld, 16)
                for t in range(TT + 1):
                    if t < TT:
                        dve.wait_ge(a_qkv, 12 * n + 8 + t + 1)
                        since(dve, a_vlo, TT * n + t - 1)
                        dve.tensor_tensor(A_VT[t % 2], PS[:, t, :], BV, ALU.add).then_inc(a_evac, 1)
                    if t >= 1:
                        dve.wait_ge(a_vhi, TT * n + t)
                        dve.tensor_tensor(A_VL[:, t - 1], A_VT[(t - 1) % 2], A_VH[:, t - 1].bitcast(F32), ALU.subtract).then_inc(a_vlo, 1)
                since(dve, a_exp, TT * n)
                since(dve, a_mx, 8 * n)
                for s in range(TT):
                    dve.wait_ge(a_s, TT * n + s + 1)
                    dve.reduce_max(MX[:, s:s + 1], PS[:, s, :], AX.X).then_inc(a_mx, 1)
                    dve.wait_ge(a_mx, 8 * n + 2 * s + 1)
                    dve.tensor_scalar(NB[:, s:s + 1], MX[:, s:s + 1], -SCALE0, None, ALU.mult).then_inc(a_mx, 1)
                dve.wait_ge(a_exp, TT * n + TT)
                since(dve, tmp_rdy, TT * turn)
                dve.reciprocal(RS[:], SM[:]).then_inc(a_rs, 1)
                for s in range(TT):
                    dve.wait_ge(a_ppa, TT * n + s + 1)
                    dve.tensor_tensor(A_PL[:, s], PS[:, 4 + s % 2, :], A_PH[:, s].bitcast(F32), ALU.subtract).then_inc(a_ppe, 1)
                if last:
                    for j in range(2):
                        split_chunk(PB, j)
                if nxt:
                    split_x(seq(*nxt))
                dve.wait_ge(gate_ld, 16 * (turn + 1))
                dve.wait_ge(a_rs, n + 1)
                for s in range(TT):
                    dve.wait_ge(a_pv, TT * n + s + 1)
                    tmp_free(turn, s)
                    dve.scalar_tensor_tensor(TMP[s % 2], PS[:, s, :], RS[:, s:s + 1], GATE, ALU.mult, ALU.mult).then_inc(tmp_rdy, 1)

            def mlp_body(phase, n, first, last):
                turn = seq(phase, n)
                nxt = after(phase, n, last)
                for j in range(FC):
                    if first and j + 2 < FC:
                        if j == 0:
                            dve.wait_ge(*((a_pv, TT * B) if phase == PB else (c_wo, TT * B)))
                        split_chunk(phase, j + 2)
                    dve.wait_ge(m_hi[phase], FC * n + j + 1)
                    dve.tensor_tensor(HL[j % 4], HID[j % 4], HH[j % 4].bitcast(F32), ALU.subtract).then_inc(m_lo[phase], 1)
                    if j == 7 and nxt:
                        ln_stats(seq(*nxt))
                    if j == 8 and nxt:
                        ln_norm(seq(*nxt))
                    if last and phase == PB and j >= 12:
                        if j == 12:
                            dve.wait_ge(m_down[PB], FC * n + 10)
                        for i in range(2):
                            split_square(PC, 2 * (j - 12) + i)
                if nxt:
                    split_x(seq(*nxt))
                if first and phase == PB:
                    dve.wait_ge(row_ld, 32)
                if phase == PD:
                    dve.wait_ge(gate_ld, 16 * (turn + 1))
                dve.wait_ge(m_down[phase], FC * n + FC)
                for t in range(TT):
                    tmp_free(turn, t)
                    if phase == PB:
                        dve.tensor_tensor(TMP[t % 2], PS[:, t, :], B2, ALU.add).then_inc(tmp_rdy, 1)
                    else:
                        dve.tensor_tensor(TMP[t % 2], PS[:, t, :], GATE, ALU.mult).then_inc(tmp_rdy, 1)

            def c_body(phase, n, first, last):
                turn = seq(phase, n)
                nxt = after(phase, n, last)
                if first:
                    dve.wait_ge(const_ld, 16 * N_CONST)
                    dve.wait_ge(m_down[PB], FC * B)
                    for i in range(3):
                        dve.memset(KT[i][96:98].bitcast(F32), 1.0).then_inc(c_ones, 1)
                    for t in range(TT):
                        dve.memset(VSH[:, t, :, 64:96].bitcast(F32), 1.0).then_inc(c_ones, 1)
                since(dve, c_on, KC * n)
                for u in range(2 * TT):
                    t = u % TT
                    dst = (QF, KF)[u // TT][:, t].rearrange("p (h d) -> p h d", d=HD)
                    src = PS[:, u % 4, :].rearrange("p (h d) -> p h d", d=HD)
                    rot = ROT[u % 2].rearrange("p (h d) -> p h d", d=HD)
                    dve.wait_ge(c_qkv, 12 * n + u + 1)
                    since(dve, c_rope, 8 * n + u - 1)
                    if u == 0:
                        since(dve, c_oadd, H * n)
                    dve.tensor_tensor(dst, src, COS[:, t].unsqueeze(1).broadcast_to([P, H, HD]), ALU.mult).then_inc(c_rot, 1)
                    dve.tensor_tensor(rot[:, :, 0:HD // 2], src[:, :, 1::2],
                                      SIN[:, t, 0:HD // 2].unsqueeze(1).broadcast_to([P, H, HD // 2]), ALU.mult).then_inc(c_rot, 1)
                    dve.wait_ge(c_rot, 16 * n + 2 * u + 2)
                    dve.tensor_tensor(rot[:, :, HD // 2:HD], src[:, :, 0::2],
                                      SIN[:, t, HD // 2:HD].unsqueeze(1).broadcast_to([P, H, HD // 2]), ALU.mult).then_inc(c_evac, 1)

                def stack(h):
                    i = h % 2
                    dve.wait_ge(t_done, transposes_c(n, h - 2, 1))
                    cols = slice(h * HD, (h + 1) * HD)
                    for x, (src, st, hi2, lo) in enumerate(((QF, QS[i], slice(0, 2), slice(64, 96)), (KF, KS[i], slice(0, 3, 2), slice(32, 64)))):
                        out = st.rearrange("p t (c d) -> p t c d", d=HD)[:, :, hi2, :]
                        dve.tensor_copy(out, src[:, :, cols].unsqueeze(2).broadcast_to([P, TT, 2, HD])).then_inc(c_stack, 1)
                        dve.wait_ge(c_stack, 4 * (H * n + h) + 2 * x + 1)
                        dve.tensor_tensor(st[:, :, lo], src[:, :, cols], st[:, :, 0:HD].bitcast(F32), ALU.subtract).then_inc(c_stack, 1)

                def maxima(h):
                    since(dve, c_mm, 2 * (H * n + max(h - 2, 0)))
                    for s in range(TT):
                        e = TT * h + s
                        dve.wait_ge(c_s, 64 * n + e + 1)
                        dve.reduce_max(MX1[:, h % 3, s:s + 1], PS[:, e % 2, :], AX.X).then_inc(c_max, 1)

                def minus_max(h):
                    dve.wait_ge(c_max, 64 * n + TT * h + TT)
                    dve.wait_ge(t_done, transposes_c(n, h - 3, 2))
                    dve.tensor_scalar(MM[:, h % 3, :, 0], MX1[:, h % 3], -1.0, None, ALU.mult).then_inc(c_mm, 1)
                    dve.wait_ge(c_mm, 2 * (H * n + h) + 1)
                    dve.scalar_tensor_tensor(MM[:, h % 3, :, 1], MX1[:, h % 3], -1.0, MM[:, h % 3, :, 0].bitcast(F32),
                                             ALU.mult, ALU.subtract).then_inc(c_mm, 1)

                def sum_head(h):
                    g, q = h // HG, h % HG
                    rows = slice(HD * q, HD * (q + 1))
                    dve.wait_ge(c_ocp, 2 * (H * n + h) + 2)
                    if q == 0:
                        since(dve, c_ol, KC * n + g - 1)
                    dve.tensor_tensor(OA[g % 2][rows], PS[0:HD, 5, :], SL[rows], ALU.add).then_inc(c_oadd, 1)
                    if q == HG - 1:
                        since(dve, c_on, KC * n + g)
                        dve.reciprocal(RC, DEN[g % 2]).then_inc(c_rc, 1)

                dve.wait_ge(c_rope, 8 * n + 8)
                stack(0)
                stack(1)
                for t in range(TT):
                    dve.wait_ge(c_vhi, TT * n + t + 1)
                    dve.tensor_tensor(VSH[:, t, :, HD:2 * HD], PS[:, t, :].rearrange("p (h d) -> p h d", d=HD),
                                      VSH[:, t, :, 0:HD].bitcast(F32), ALU.subtract).then_inc(c_evac, 1)
                maxima(0)
                minus_max(0)
                stack(2)
                maxima(1)
                for h in range(H + 1):
                    if h + 1 < H:
                        minus_max(h + 1)
                    if h + 3 < H:
                        stack(h + 3)
                    if h < H:
                        for t in range(3):
                            e = TT * h + t
                            dve.wait_ge(c_exp, 64 * n + e + 1)
                            if t == 0:
                                since(dve, c_o, H * n + h - 1)
                            dve.tensor_copy(PTH[h % 2][:, t], PE[e % 3]).then_inc(c_phd, 1)
                    if h + 2 < H:
                        maxima(h + 2)
                    if h >= 1:
                        sum_head(h - 1)
                    if h == 14 and nxt:
                        ln_stats(seq(*nxt))
                    if h == 15 and nxt:
                        ln_norm(seq(*nxt))
                if last:
                    for j in range(2):
                        split_chunk(PD, j)
                if nxt:
                    split_x(seq(*nxt))
                dve.wait_ge(gate_ld, 16 * (turn + 1))
                for t in range(TT):
                    dve.wait_ge(c_wo, TT * n + t + 1)
                    tmp_free(turn, t)
                    dve.tensor_tensor(TMP[t % 2], PS[:, t, :], GATE, ALU.mult).then_inc(tmp_rdy, 1)

            for phase in range(4):
                over_sequences(dve, (a_body, mlp_body, c_body, mlp_body)[phase], phase)

        @block.scalar
        def _(act):
            act.wait_ge(const_evac, 1)
            act.activation(SE[:], CT[:, 4:8], ACT.Exp, scale=-1.0).then_inc(silu_a, 1)

            def evacuate_y(phase, n):
                turn = seq(phase, n)
                since(act, xl_rdy, KC * turn)
                for k in range(KC):
                    act.wait_ge(t_done, transposes_before(phase, n) - KC + k + 1)
                    act.activation(Y[:, k], PS[:, 6 + k % 2, :], ACT.Identity,
                                   scale=LN_SCALE[:, phase, k, bass.ds(n, 1)], bias=LN_SHIFT[:, phase, k, bass.ds(n, 1)]).then_inc(y_rdy, 1)

            def split_x(phase, n, prev):
                turn = seq(phase, n)
                if prev:
                    operand_free(act, *prev)
                for k in range(KC):
                    act.wait_ge(y_rdy, KC * turn + k + 1)
                    act.activation(XH[:, k], Y[:, k], ACT.Identity).then_inc(xh_rdy, 1)

            act.wait_ge(mod_steps, MOD_STEPS)
            evacuate_y(PA, 0)
            split_x(PA, 0, None)

            def a_body(phase, n, first, last):
                nxt = after(phase, n, last)
                since(act, a_s, TT * n)
                for u in range(2 * KC):
                    hi, vec = ((A_QH, VECQ), (A_KH, VECK))[u // KC]
                    k = u % KC
                    act.wait_ge(a_qkv, 12 * n + u + 1)
                    act.activation(hi[:, k], PS[:, u % 4, :], ACT.Identity, bias=VEC[:, vec + k:vec + k + 1]).then_inc(a_qkh, 1)
                since(act, a_pv, TT * n)
                for t in range(TT):
                    act.wait_ge(a_evac, 12 * n + 8 + t + 1)
                    act.activation(A_VH[:, t], A_VT[t % 2], ACT.Identity).then_inc(a_vhi, 1)
                if nxt:
                    evacuate_y(*nxt)
                since(act, a_rs, n)
                for s in range(TT):
                    act.wait_ge(a_mx, 8 * n + 2 * s + 2)
                    act.activation(A_P[:, s], PS[:, s, :], ACT.Exp, bias=NB[:, s:s + 1], scale=SCALE0,
                                   accum_out=SM[:, s:s + 1]).then_inc(a_exp, 1)
                for s in range(TT):
                    act.wait_ge(a_pp, TT * n + s + 1)
                    act.activation(A_PH[:, s], PS[:, 4 + s % 2, :], ACT.Identity).then_inc(a_ppa, 1)
                if nxt:
                    split_x(*nxt, (phase, n))

            def mlp_body(phase, n, first, last):
                nxt = after(phase, n, last)
                for j in range(FC):
                    act.wait_ge(m_up[phase], FC * n + j + 1)
                    since(act, m_lo[phase], FC * n + j - 3)
                    if first and phase == PD and j == 0:
                        act.wait_ge(c_pl, 64 * B)
                        act.wait_ge(c_rc, KC * B)
                    bias = VEC[:, VECB1 + j:VECB1 + j + 1] if phase == PB else 0.0
                    act.activation(HID[j % 4], PS[:, 4 + j % 2, :], ACT.Gelu, bias=bias).then_inc(m_gelu[phase], 1)
                    act.wait_ge(m_gelu[phase], FC * n + j + 1)
                    since(act, m_down[phase], FC * n + j - 3)
                    act.activation(HH[j % 4], HID[j % 4], ACT.Identity).then_inc(m_hi[phase], 1)
                    if j == 10 and nxt:
                        evacuate_y(*nxt)
                if nxt:
                    split_x(*nxt, (phase, n))
                if phase == PB:
                    for t in range(TT):
                        act.wait_ge(tmp_rdy, TT * seq(phase, n) + t + 1)
                        act.activation(TMP[t % 2], TMP[t % 2], ACT.Gelu).then_inc(b_gelu, 1)

            def c_body(phase, n, first, last):
                nxt = after(phase, n, last)
                if first:
                    act.wait_ge(m_down[PB], FC * B)
                since(act, c_o, H * n)
                for t in range(TT):
                    act.wait_ge(c_qkv, 12 * n + 8 + t + 1)
                    act.activation(VSH[:, t, :, 0:HD], PS[:, t, :].rearrange("p (h d) -> p h d", d=HD), ACT.Identity).then_inc(c_vhi, 1)

                def evacuate(h, what, rows, dst):
                    act.wait_ge(t_done, transposes_c(n, h, what))
                    act.activation(dst, PS[0:rows, 6 + T_USE[h, what] % 2, :], ACT.Identity).then_inc(t_evac, 1)

                def evacuate_q(h):
                    since(act, c_st, 64 * n + TT * max(h - 2, 0))
                    evacuate(h, 0, 96, QT[h % 3][0:96])

                def evacuate_k(h):
                    evacuate(h, 1, 96, KT[h % 3][0:96])

                def evacuate_m(h):
                    evacuate(h, 2, 2, QT[h % 3][96:98])

                def copy_out(h):
                    g, q = h // HG, h % HG
                    rows = slice(HD * q, HD * (q + 1))
                    act.wait_ge(c_o, H * n + h + 1)
                    if q == 0:
                        since(act, c_rc, KC * n + g - 1)
                    act.activation(DEN[g % 2][rows], PS[64:96, 5, :], ACT.Identity).then_inc(c_ocp, 1)
                    since(act, c_oadd, H * n + h - 3)
                    if h == 0:
                        act.wait_ge(c_rope, 8 * n + 8)
                    act.activation(SL[rows], PS[HD:2 * HD, 5, :], ACT.Identity).then_inc(c_ocp, 1)

                def normalised_hi(g):
                    act.wait_ge(c_on, KC * n + g + 1)
                    act.activation(OTH[:, g], OA[g % 2], ACT.Identity).then_inc(c_oh, 1)

                evacuate_q(0)
                evacuate_k(0)
                evacuate_m(0)
                evacuate_q(1)
                evacuate_k(1)
                for h in range(H + 1):
                    if h < H:
                        for t in range(TT):
                            if t == 0 and h + 2 < H:
                                evacuate_q(h + 2)
                            if t == 1 and h + 2 < H:
                                evacuate_k(h + 2)
                            if t == 2 and h + 1 < H:
                                evacuate_m(h + 1)
                            e = TT * h + t
                            act.wait_ge(c_st, 64 * n + e + 1)
                            since(act, c_pl, 64 * n + max(e - 2, 0))
                            if h == 0 and t == 0 and first:
                                act.wait_ge(m_lo[PB], FC * B)
                            act.activation(PE[e % 3], PS[:, 2 + e % 3, :], ACT.Exp, scale=SCALE1).then_inc(c_exp, 1)
                    if h >= 1:
                        copy_out(h - 1)
                    if h < H:
                        act.wait_ge(c_exp, 64 * n + TT * h + TT)
                        since(act, c_o, H * n + h - 1)
                        act.activation(PTH[h % 2][:, 3], PE[(TT * h + 3) % 3], ACT.Identity).then_inc(c_pha, 1)
                    if h >= HG and h % HG == 1:
                        normalised_hi(h // HG - 1)
                normalised_hi(KC - 1)
                if nxt:
                    evacuate_y(*nxt)
                    split_x(*nxt, (phase, n))

            for phase in range(4):
                over_sequences(act, (a_body, mlp_body, c_body, mlp_body)[phase], phase)

        @block.tensor
        def _(pe):
            def product(out, x, w, start, stop):
                (xh, xl), (wh, wl) = x, w
                pe.matmul(out, xh, wh, start=start, stop=False)
                pe.matmul(out, xh, wl, start=False, stop=False)
                return pe.matmul(out, xl, wh, start=False, stop=stop)

            pe.wait_ge(const_ld, 16 * N_CONST)
            pe.wait_ge(consts, 3)
            for k in range(8):
                pe.transpose(PS[:, 0, B * k:B * k + B], COND_ROWS[:, P * k:P * k + P], ID_F[0:B, 0:B])
            pe.transpose(PS[:, 0, 64:168], VEC_ROWS, ID_F[0:104, 0:104]).then_inc(vec_done, 1)
            pe.wait_ge(const_evac, 3)
            seen = [0, 0]
            for blk in range(12):
                layer, v = blk // 6, blk % 6
                slot, kn = blk % 2, (8, 4)[layer]
                seen[slot] += 16
                pe.wait_ge(modw_ld[slot], seen[slot])
                c = CT if layer == 0 else ST_
                w = STAGE_W[slot][:, 0:kn * D].rearrange("p (k n) -> p k n", n=D)
                is_gate = v in ((0, 3), (2, 5))[layer]
                if is_gate:
                    g = 2 * layer + (v > 2)
                    for k in range(kn):
                        mm = pe.matmul(PS[0:B, 3 + g, :], c[:, k, :], w[:, k, :], start=k == 0, stop=k == kn - 1)
                else:
                    at = [x for x in range(6) if x not in ((0, 3), (2, 5))[layer]].index(v)
                    for fc in range(KC):
                        o = PS[:, 1 + layer, 32 * at + B * fc:32 * at + B * fc + B]
                        for k in range(kn):
                            mm = pe.matmul(o, w[:, k, P * fc:P * fc + P], c[:, k, :], start=k == 0, stop=k == kn - 1)
                mm.then_inc(modw_done, 1)

            def transpose_x(phase, n):
                turn = seq(phase, n)
                pe.wait_ge(ln_v, LN_STEPS * (turn + 1))
                for k in range(KC):
                    since(pe, y_rdy, KC * turn + k - 1)
                    for t in range(TT):
                        mm = pe.transpose(PS[:, 6 + k % 2, P * t:P * t + P], XLN[:, t, P * k:P * k + P], ID_F[:])
                    mm.then_inc(t_done, 1)

            pe.wait_ge(gate_evac, 4)
            transpose_x(PA, 0)

            def a_body(phase, n, first, last):
                turn = seq(phase, n)
                nxt = after(phase, n, last)
                if first:
                    pe.wait_ge(w_split, 2 * W_FIRST[PB])
                for u in range(2 * KC):
                    fc = u % KC
                    if u < 4:
                        since(pe, tmp_rdy, TT * (turn - 1) + u + 1)
                    else:
                        pe.wait_ge(a_evac, 12 * n + u - 3)
                    wh, wl = A_W[u // KC]
                    for k in range(KC):
                        if u == 0:
                            pe.wait_ge(xl_rdy, KC * turn + k + 1)
                        cols = slice(P * fc, P * fc + P)
                        mm = product(PS[:, u % 4, :], (wh[:, k, cols], wl[:, k, cols]), (XH[:, k], XL[:, k]), k == 0, k == KC - 1)
                    mm.then_inc(a_qkv, 1)
                for t in range(TT):
                    pe.wait_ge(a_evac, 12 * n + 8 + t - 3)
                    wh, wl = A_W[2]
                    for k in range(KC):
                        cols = slice(P * t, P * t + P)
                        mm = product(PS[:, t, :], (XH[:, k, cols], XL[:, k, cols]), (wh[:, k], wl[:, k]), k == 0, k == KC - 1)
                    mm.then_inc(a_qkv, 1)
                for s in range(TT):
                    pe.wait_ge(a_evac, 12 * n + 8 + s + 1)
                    for k in range(KC):
                        cols = slice(P * s, P * s + P)
                        mm = product(PS[:, s, :], (A_QH[:, k, cols], A_QL[:, k, cols]), (A_KH[:, k], A_KL[:, k]), k == 0, k == KC - 1)
                    mm.then_inc(a_s, 1)
                    if s == 1 and nxt:
                        transpose_x(*nxt)

                def transpose_p(s):
                    pe.wait_ge(a_exp, TT * n + s + 1)
                    since(pe, a_ppe, TT * n + s - 1)
                    for t in range(TT):
                        mm = pe.transpose(PS[:, 4 + s % 2, P * t:P * t + P], A_P[:, s, P * t:P * t + P], ID_F[:])
                    mm.then_inc(a_pp, 1)

                def attend(s):
                    pe.wait_ge(a_ppe, TT * n + s + 1)
                    if s == 0:
                        pe.wait_ge(a_vlo, TT * n + TT)
                    for t in range(TT):
                        cols = slice(P * t, P * t + P)
                        mm = product(PS[:, s, :], (A_PH[:, s, cols], A_PL[:, s, cols]), (A_VH[:, t], A_VL[:, t]), t == 0, t == TT - 1)
                    mm.then_inc(a_pv, 1)

                transpose_p(0)
                transpose_p(1)
                for s in range(TT):
                    attend(s)
                    if s + 2 < TT:
                        transpose_p(s + 2)

            def mlp_body(phase, n, first, last):
                turn = seq(phase, n)
                nxt = after(phase, n, last)

                def up(j):
                    if first:
                        pe.wait_ge(w_split, 2 * (W_FIRST[phase] + j + 1))
                        if j < 2:
                            pe.wait_ge(*((a_ppe, TT * B) if phase == PB else (c_oadd, H * B)))
                    since(pe, m_gelu[phase], FC * n + j - 1)
                    (wh, wl), _ = w_chunk(phase, j)
                    for k in range(KC):
                        if j == 0:
                            pe.wait_ge(xl_rdy, KC * turn + k + 1)
                        mm = product(PS[:, 4 + j % 2, :], (wh[:, k], wl[:, k]), (XH[:, k], XL[:, k]), k == 0, k == KC - 1)
                    mm.then_inc(m_up[phase], 1)

                def down(j):
                    pe.wait_ge(m_lo[phase], FC * n + j + 1)
                    _, w = w_chunk(phase, j)
                    for t in range(TT):
                        if j == 0:
                            pe.wait_ge(tmp_rdy, TT * (turn - 1) + t + 1)
                        cols = slice(P * t, P * t + P)
                        mm = product(PS[:, t, :], (HH[j % 4][:, cols], HL[j % 4][:, cols]), w, j == 0, j == FC - 1)
                    mm.then_inc(m_down[phase], 1)

                up(0)
                for j in range(FC):
                    if j + 1 < FC:
                        up(j + 1)
                    down(j)
                    if j == 9 and nxt:
                        transpose_x(*nxt)

            def c_body(phase, n, first, last):
                turn = seq(phase, n)
                nxt = after(phase, n, last)
                if first:
                    pe.wait_ge(w_split, 2 * W_FIRST[PD])
                for u in range(3 * TT):
                    t = u % TT
                    if u >= 4:
                        pe.wait_ge(c_evac, 12 * n + u - 3)
                    else:
                        pe.wait_ge(tmp_rdy, TT * (turn - 1) + t + 1)
                    wh, wl = C_W[u // TT]
                    for k in range(KC):
                        if u == 0:
                            pe.wait_ge(xl_rdy, KC * turn + k + 1)
                        cols = slice(P * t, P * t + P)
                        mm = product(PS[:, t, :], (XH[:, k, cols], XL[:, k, cols]), (wh[:, k], wl[:, k]), k == 0, k == KC - 1)
                    mm.then_inc(c_qkv, 1)

                def transpose_bank(h, what):
                    use = T_USE[h, what]
                    if use < 2:
                        since(pe, y_rdy, KC * (turn + 1))
                    else:
                        pe.wait_ge(t_evac, 48 * n + use - 1)
                    return PS[:, 6 + use % 2, :].bitcast(F32R)

                def transpose_qk(h, what):
                    bank = transpose_bank(h, what)
                    pe.wait_ge(c_stack, 4 * (H * n + h) + 2 * what + 2)
                    st = (QS, KS)[what][h % 2]
                    for t in range(TT):
                        mm = pe.transpose(bank[0:96, P * t:P * t + P], st[:, t], ID_R[:])
                    mm.then_inc(t_done, 1)

                def transpose_m(h):
                    bank = transpose_bank(h, 2)
                    pe.wait_ge(c_mm, 2 * (H * n + h) + 2)
                    for t in range(TT):
                        mm = pe.transpose(bank[0:2, P * t:P * t + P], MM[:, h % 3, t], ID_R[:])
                    mm.then_inc(t_done, 1)

                def scores(h, s):
                    e = TT * h + s
                    if s == 0:
                        pe.wait_ge(t_evac, 48 * n + T_USE[h, 1] + 1)
                    if e < 2:
                        pe.wait_ge(c_evac, 12 * n + 12)
                    else:
                        pe.wait_ge(c_max, 64 * n + e - 1)
                    pe.matmul(PS[:, e % 2, :], QT[h % 3][0:96, P * s:P * s + P], KT[h % 3][0:96], start=True, stop=True).then_inc(c_s, 1)

                def scores_t(h, t):
                    e = TT * h + t
                    if t == 0:
                        pe.wait_ge(t_evac, 48 * n + T_USE[h, 2] + 1)
                    since(pe, c_exp, 64 * n + max(e - 2, 0))
                    pe.matmul(PS[:, 2 + e % 3, :], KT[h % 3][0:98, P * t:P * t + P], QT[h % 3][0:98], start=True, stop=True).then_inc(c_st, 1)

                def attend(h, t):
                    if t == 0:
                        since(pe, c_oadd, H * n + h)
                    pe.wait_ge(c_pl, 64 * n + TT * h + t + 1)
                    v = VS[:, t, 96 * h:96 * h + 96]
                    pe.matmul(PS[0:96, 5, :], v, PTH[h % 2][:, t], start=t == 0, stop=False)
                    mm = pe.matmul(PS[0:96, 5, :], v, PTL[h % 2][:, t], start=False, stop=t == TT - 1)
                    if t == TT - 1:
                        mm.then_inc(c_o, 1)

                if first:
                    pe.wait_ge(c_ones, 7)
                transpose_qk(0, 0)
                transpose_qk(0, 1)
                for s in range(TT):
                    scores(0, s)
                transpose_m(0)
                transpose_qk(1, 0)
                transpose_qk(1, 1)
                for s in range(TT):
                    scores(1, s)
                for h in range(H):
                    if h + 2 < H:
                        transpose_qk(h + 2, 0)
                    scores_t(h, 0)
                    if h + 2 < H:
                        transpose_qk(h + 2, 1)
                    scores_t(h, 1)
                    if h + 1 < H:
                        transpose_m(h + 1)
                    scores_t(h, 2)
                    if h + 2 < H:
                        scores(h + 2, 0)
                    scores_t(h, 3)
                    if h + 2 < H:
                        scores(h + 2, 1)
                    if h >= 1:
                        attend(h - 1, 0)
                        attend(h - 1, 1)
                    if h + 2 < H:
                        scores(h + 2, 2)
                    if h >= 1:
                        attend(h - 1, 2)
                        attend(h - 1, 3)
                    if h + 2 < H:
                        scores(h + 2, 3)
                for t in range(TT):
                    attend(H - 1, t)
                if nxt:
                    pe.wait_ge(t_evac, 48 * n + 48)
                    transpose_x(*nxt)
                pe.wait_ge(c_exp, 64 * n + 64)
                wh, wl = C_W[3]
                for t in range(TT):
                    for k in range(KC):
                        if t == 0:
                            pe.wait_ge(c_ol, KC * n + k + 1)
                        cols = slice(P * t, P * t + P)
                        mm = product(PS[:, t, :], (OTH[:, k, cols], OTL[:, k, cols]), (wh[:, k], wl[:, k]), k == 0, k == KC - 1)
                    mm.then_inc(c_wo, 1)

            for phase in range(4):
                over_sequences(pe, (a_body, mlp_body, c_body, mlp_body)[phase], phase)


_INS = {
    "x": "x", "fside": "fside_BxS_0", "cond": "cond_1024",
    "Wq0": "L0_cond_Wq", "bq": "L0_cond_bq", "Wk0": "L0_cond_Wk", "bk": "L0_cond_bk", "Wv0": "L0_cond_Wv", "bv": "L0_cond_bv",
    "W1_0": "L0_cond_W1", "b1": "L0_cond_b1", "W2_0": "L0_cond_W2", "b2": "L0_cond_b2", "Wc": "L0_cond_Wc", "bc": "L0_cond_bc",
    "ln1_g": "L0_cond_ln1_g", "ln1_b": "L0_cond_ln1_b", "ln2_g": "L0_cond_ln2_g", "ln2_b": "L0_cond_ln2_b",
    "n1_g": "L1_cond_norm1_g", "n1_b": "L1_cond_norm1_b", "n2_g": "L1_cond_norm2_g", "n2_b": "L1_cond_norm2_b",
    "Wq1": "L1_cond_Wq", "Wk1": "L1_cond_Wk", "Wv1": "L1_cond_Wv", "Wo1": "L1_cond_Wo",
    "W1_1": "L1_cond_W1", "W2_1": "L1_cond_W2", "ada_W": "L1_cond_ada_W", "ada_b": "L1_cond_ada_b",
}


def rope_tables():
    inv = (1.0 / 10000.0 ** (np.arange(0, HD, 2, dtype=np.float32) / np.float32(HD))).astype(np.float32)
    freqs = np.outer(np.arange(S, dtype=np.float32), inv).astype(np.float32)
    emb = np.concatenate([freqs, freqs], -1)
    sign = np.where(np.arange(HD) < HD // 2, -1.0, 1.0).astype(np.float32)
    return np.cos(emb).astype(np.float32), (np.sin(emb).astype(np.float32) * sign).astype(np.float32)


def kernel(**inputs):
    import concourse.bacc as bacc
    from concourse.bass_utils import run_bass_kernel_spmd

    nc = bacc.Bacc("TRN2", target_bir_lowering=False, num_devices=1, dynamic_dma_scratch_size=1024)
    arrays = {f"in_{k}": np.ascontiguousarray(inputs[name]) for k, name in _INS.items()}
    arrays["in_cos"], arrays["in_sin"] = rope_tables()
    a = {n[3:]: nc.dram_tensor(n, v.shape, F32, kind="ExternalInput").ap() for n, v in arrays.items()}
    a["out"] = nc.dram_tensor("out_x", (B, S, D), F32, kind="ExternalOutput").ap()
    build(nc, a)
    r = run_bass_kernel_spmd(nc, [arrays], core_ids=[0])
    return r.results[0]["out_x"]
```

```python
from contextlib import ExitStack

import concourse.bass as bass
import numpy as np
from concourse import mybir

F32 = mybir.dt.float32
F32R = mybir.dt.float32r
ACT = mybir.ActivationFunctionType
ALU = mybir.AluOpType
AX = mybir.AxisListType

B, S, D = 8, 512, 512
P = 128
KC = D // P
TT = S // P
FF = 4 * D
FC = FF // P
H = 16
HD = D // H
HG = P // HD
EPS = 1e-5
SCALE0 = float(D) ** -0.5
SCALE1 = float(HD) ** -0.5
PA, PB, PC, PD = range(4)
TURN_TRANSPOSES = [KC, KC, KC + 3 * H, KC]
W_UNITS = [6, FC, 8, FC]
W_FIRST = [0, 6, 6 + FC, 14 + FC]


def seq(phase, n):
    return n + B * phase


def transposes_before(phase, n):
    return KC + sum([KC * B, KC * B, (KC + 3 * H) * B][:phase]) + TURN_TRANSPOSES[phase] * n


QKV_BANK = [4, 5, 6, 7] + 2 * [4, 5, 2, 3]
N_CONST = 21
LN_STEPS = 14
MOD_STEPS = 16
T_ORDER = [(0, 0), (0, 1), (0, 2), (1, 0), (1, 1)]
for _h in range(H):
    T_ORDER += [x for x in ((_h + 2, 0), (_h + 2, 1), (_h + 1, 2)) if x[0] < H]
T_USE = {x: i for i, x in enumerate(T_ORDER)}


def build(nc, a):
    ctx = ExitStack()
    with ctx:
        def sb(name, shape, dt=F32):
            return ctx.enter_context(nc.sbuf_tensor(name, shape, dt))

        def sem(name):
            return ctx.enter_context(nc.semaphore(name))

        R = sb("pe_operands", [P, 40960], F32R)
        W_SLOT = 2048

        def r(at, *shape):
            ap = R[:, at:at + int(np.prod(shape))]
            return ap if len(shape) == 1 else ap.rearrange("p (a b) -> p a b", b=shape[-1])

        XH, XL = r(32768, KC, S), r(34816, KC, S)
        A_W = [[r(W_SLOT * (2 * w + part), KC, D) for part in range(2)] for w in range(3)]
        A_QH, A_QL, A_KH, A_KL, A_VH, A_VL, A_PH, A_PL = [r(12288 + 2048 * i, 4, 512) for i in range(8)]
        SLOT_OF = {PB: [(j + 14) % FC for j in range(FC)], PD: list(range(FC))}

        def w_chunk(phase, j):
            base = W_SLOT * SLOT_OF[phase][j]
            return (r(base, KC, P), r(base + 1024, KC, P)), (r(base + 512, D), r(base + 1536, D))

        HH = [r(36864 + 1024 * i, 512) for i in range(4)]
        HL = [r(36864 + 1024 * i + 512, 512) for i in range(4)]
        C_W = [[r(W_SLOT * (2 * w + part), KC, D) for part in range(2)] for w in range(4)]
        VS = r(16384, TT, H * 96)
        VSH = VS.rearrange("p t (h c) -> p t h c", c=96)
        QS = [r(22528 + 384 * i, TT, 96) for i in range(2)]
        KS = [r(23296 + 384 * i, TT, 96) for i in range(2)]
        QT = [r(24064 + 1024 * i, S) for i in range(3)]
        KT = [r(24576 + 1024 * i, S) for i in range(3)]
        PTH = [r(at, TT, S) for at in (27136, 36864)]
        PTL = [r(at, TT, S) for at in (29184, 38912)]
        OTH = [XH[:, k] for k in range(KC - 1)] + [r(31232, S)]
        OTL = [XL[:, k] for k in range(KC - 1)] + [r(31744, S)]
        MM = sb("minus_max_r", [P, 3, TT], F32R)
        ID_R = sb("identity_r", [P, P], F32R)

        F = sb("work", [P, 12288])

        def f(at, *shape):
            ap = F[:, at:at + int(np.prod(shape))]
            return ap if len(shape) == 1 else ap.rearrange("p (a b) -> p a b", b=shape[-1])

        XLN, Y, XRES = f(0, TT, D), f(2048, KC, S), f(4096, TT, D)
        TMP = [f(6144, 512), f(6656, 512)]
        GATE = f(7168, 512)
        A_P = f(7680, TT, S)
        A_VT = [f(9728, 512), f(10240, 512)]
        BV = f(10752, 512)
        HID = [f(7680 + 512 * i, 512) for i in range(4)]
        B2 = f(9728, 512)
        KF, QF = XLN, Y
        PE = [f(7680 + 512 * i, 512) for i in range(TT)]
        OA = [f(9728, 512), f(10240, 512)]
        ROT = [f(10752, 512), f(11264, 512)]
        SLD = [F[64 * (i % 2):64 * (i % 2) + 64, 10752 + 512 * (i // 2):11264 + 512 * (i // 2)] for i in range(4)]
        RC = f(11776, 512)
        STAGE = sb("weight_stage", [P, 2, 1024])
        STAGE_W = [F[:, 4096 * i:4096 * (i + 1)] for i in range(2)]
        GROW, GBIAS = F[0:B, 8192:10240], F[0:B, 10240:12288]
        COND_ROWS = F[0:B, 0:1024]
        VEC_ROWS = F[0:104, 1024:1152]
        ID_F = sb("identity", [P, P])
        MINUS_HALF = sb("minus_half", [P, TT])
        COS, SIN = sb("cos", [P, TT, HD]), sb("sin", [P, TT, HD])
        CT = sb("cond_T", [P, 8, B])
        ST_ = sb("silu_T", [P, 4, B])
        SE = sb("silu_exp", [P, 4, B])
        VEC = sb("vectors_T", [P, 104])
        MOD = sb("mod_T", [P, 4, 4, B])
        LN_SCALE = sb("ln_scale", [P, 4, KC, B])
        LN_SHIFT = sb("ln_shift", [P, 4, KC, B])
        STATS = sb("bn_stats", [P, TT, 6])
        MV = sb("mean_var", [P, TT, 2])
        VEPS, RSTD = sb("var_eps", [P, TT]), sb("rstd", [P, TT])
        MX, NB, SM, RS = sb("row_max", [P, 4]), sb("minus_scaled_max", [P, 4]), sb("row_sum", [P, 4]), sb("row_sum_inv", [P, 4])
        DEN = sb("denominators", [P, 2, HG, S // P])
        DENI = sb("denominators_inv", [P, 2, HG, S // P])
        MX1 = sb("row_max_heads", [P, 3, TT])

        PS = ctx.enter_context(nc.psum_tensor("psum", [P, 8, 512], F32))
        VECQ, VECK, VECB1 = 80, 84, 88

        x_mid = [nc.dram_tensor(f"x_after_{c}", (B, S, D), F32, kind="Internal").ap() for c in "abc"]
        gates_d = nc.dram_tensor("gates", (4, B, D), F32, kind="Internal").ap()
        den_rows, inv_rows = (nc.dram_tensor(x, (2, HG, S), F32, kind="Internal").ap() for x in ("denominator_rows", "inverse_rows"))
        x_in = [a["x"], *x_mid]
        x_out = [*x_mid, a["out"]]

        def tokens(ap, n):
            return ap[bass.ds(n, 1)].rearrange("o (t p) d -> p (o t) d", p=P)

        const_ld, vec_done, const_evac, consts = sem("const_loaded"), sem("const_transposed"), sem("const_evacuated"), sem("pool_consts")
        idr_rdy, silu_a = sem("identity_r_ready"), sem("silu_steps")
        modw_ld, modw_done = [sem("mod_weights_0"), sem("mod_weights_1")], sem("mod_products")
        mod_steps, gates_st = sem("mod_steps"), sem("gates_stored")
        gate_evac = sem("gate_evacuated")
        w_ld, w_split = [sem("weights_0"), sem("weights_1")], sem("weights_split")
        xln_ld, ln_v, ln_rstd = sem("ln_input_loaded"), sem("ln_steps"), sem("rstd_ready")
        t_done, t_evac = sem("transposed"), sem("transpose_evacuated")
        y_rdy, xh_rdy, xl_rdy = sem("y_ready"), sem("xh_ready"), sem("xl_ready")
        res_ld, gate_ld, tmp_rdy, res_step, res_done, stored = (
            sem("residual_loaded"), sem("gate_loaded"), sem("branch_ready"), sem("gated"), sem("residual_added"), sem("stored"))
        row_ld = sem("bias_rows_loaded")
        a_qkv, a_qkh, a_evac, a_vhi, a_vlo = sem("a_qkv_done"), sem("a_qk_hi"), sem("a_qkv_evacuated"), sem("a_v_hi"), sem("a_v_lo")
        a_s, a_mx, a_exp, a_pp, a_ppa, a_ppe, a_rs = (sem("a_scores"), sem("a_max"), sem("a_exp"), sem("a_probs_T"),
                                                     sem("a_probs_T_hi"), sem("a_probs_T_lo"), sem("a_row_sum_inv"))
        a_pv = sem("a_attn")
        m_up = {ph: sem(f"up_done_{ph}") for ph in (PB, PD)}
        m_gelu = {ph: sem(f"gelu_{ph}") for ph in (PB, PD)}
        m_hi = {ph: sem(f"hidden_hi_{ph}") for ph in (PB, PD)}
        m_lo = {ph: sem(f"hidden_lo_{ph}") for ph in (PB, PD)}
        m_down = {ph: sem(f"down_done_{ph}") for ph in (PB, PD)}
        b_gelu = sem("b_out_gelu")
        c_ones, c_qkv, c_rot, c_evac, c_rope, c_vhi = sem("c_ones"), sem("c_qkv_done"), sem("c_rot_steps"), sem("c_qkv_evacuated"), sem("c_rope"), sem("c_v_hi")
        c_stack, c_s, c_max, c_mm, c_st, c_exp = sem("c_stacks"), sem("c_scores"), sem("c_max"), sem("c_minus_max"), sem("c_scores_T"), sem("c_exp")
        c_phd, c_pha, c_pl = sem("c_probs_hi_dve"), sem("c_probs_hi_act"), sem("c_probs_lo")
        c_o, c_ocp, c_oadd, c_on, c_oh, c_ol = (sem("c_attn"), sem("c_attn_copied"), sem("c_attn_summed"), sem("c_attn_normalised"), sem("c_attn_hi"), sem("c_attn_lo"))
        c_wo, c_wok = sem("c_out_done"), sem("c_out_chunk_done")
        c_den, c_dencp, c_deni, c_denst, c_rcld = ([sem(f"c_denominators_stored_{q}") for q in range(HG)], sem("c_denominators_compact"), sem("c_denominators_inverted"),
                                          sem("c_denominators_inv_stored"), sem("c_denominators_inv_rows"))

        def since(eng, semaphore, value):
            if not isinstance(value, int) or value > 0:
                eng.wait_ge(semaphore, value)

        def operand_free(eng, phase, n, k):
            if phase == PC and k < KC - 1:
                since(eng, c_wok, (KC - 1) * n + k + 1)
            else:
                s, per = [(a_qkv, 12), (m_up[PB], FC), (c_qkv, 12), (m_up[PD], FC)][phase]
                since(eng, s, per * n + per)

        def transposes_c(n, h, what):
            return transposes_before(PC, n) + (T_USE[h, what] + 1 if h >= 0 else 0)

        def after(phase, n, last):
            if not last:
                return phase, n + 1
            return (phase + 1, 0) if phase < PD else None

        def over_sequences(eng, body, phase):
            body(phase, 0, True, False)
            with eng.Fori(1, B - 1) as n:
                body(phase, n, False, False)
            body(phase, B - 1, False, True)

        block = ctx.enter_context(nc.Block())

        @block.sync
        def _(sp):
            sp.dma_start(COND_ROWS[:, 0:512], a["fside"]).then_inc(const_ld, 16)
            sp.dma_start(COND_ROWS[:, 512:1024], a["cond"]).then_inc(const_ld, 16)
            at = 0
            for name in ("bc", "ada_b", "ln1_g", "ln1_b", "ln2_g", "ln2_b", "n1_g", "n1_b", "n2_g", "n2_b", "bq", "bk", "b1"):
                rows = a[name].shape[0] // P
                sp.dma_start(VEC_ROWS[at:at + rows, :], a[name].rearrange("(r c) -> r c", c=P)).then_inc(const_ld, 16)
                at += rows
            sp.dma_start(COS[:], a["cos"].rearrange("(t p) d -> p t d", p=P)).then_inc(const_ld, 16)
            sp.dma_start(SIN[:], a["sin"].rearrange("(t p) d -> p t d", p=P)).then_inc(const_ld, 16)
            for g in range(4):
                src = a[("bc", "ada_b")[g // 2]][(0, 3, 2, 5)[g] * D:((0, 3, 2, 5)[g] + 1) * D]
                sp.dma_start(GBIAS[:, g * D:(g + 1) * D], src.partition_broadcast(B)).then_inc(const_ld, 16)

            def load_unit(u):
                slot = u % 2
                since(sp, w_split, 2 * (u - 1))
                phase = max(p for p in range(4) if W_FIRST[p] <= u)
                j = u - W_FIRST[phase]
                if phase in (PA, PC):
                    w = a[(("Wq0", "Wk0", "Wv0"), ("Wq1", "Wk1", "Wv1", "Wo1"))[phase == PC][j // 2]]
                    src = w.rearrange("(k p) n -> p k n", p=P)[:, 2 * (j % 2):2 * (j % 2) + 2, :]
                    sp.dma_start(STAGE[:, slot, :].rearrange("p (k n) -> p k n", n=D), src).then_inc(w_ld[slot], 16)
                else:
                    w1, w2 = (a["W1_0"], a["W2_0"]) if phase == PB else (a["W1_1"], a["W2_1"])
                    sp.dma_start(STAGE[:, slot, 0:512].rearrange("p (k n) -> p k n", n=P),
                                 w1.rearrange("(k p) n -> p k n", p=P)[:, :, j * P:(j + 1) * P]).then_inc(w_ld[slot], 16)
                    sp.dma_start(STAGE[:, slot, 512:1024], w2[j * P:(j + 1) * P, :]).then_inc(w_ld[slot], 16)

            for blk in range(12):
                slot = blk % 2
                if blk == 0:
                    sp.wait_ge(const_evac, 3)
                since(sp, modw_done, blk - 1)
                w = a["Wc"] if blk < 6 else a["ada_W"]
                k = 8 if blk < 6 else 4
                sp.dma_start(STAGE_W[slot][:, 0:k * D].rearrange("p (k n) -> p k n", n=D),
                             w.rearrange("(k p) n -> p k n", p=P)[:, :, (blk % 6) * D:(blk % 6 + 1) * D]).then_inc(modw_ld[slot], 16)
                if blk < 2:
                    load_unit(blk)
            sp.wait_ge(gate_evac, 4)
            sp.dma_start(gates_d.rearrange("g b d -> b g d"), GROW.rearrange("b (g d) -> b g d", d=D)).then_inc(gates_st, 16)

            def load_ln(phase, n):
                if phase > PA:
                    since(sp, stored, 16 * (seq(phase - 1, n) + 1))
                first = isinstance(n, int) and n == 0
                if phase == PC and not first:
                    sp.wait_ge(c_stack, 4 * H * n)
                elif phase == PD and first:
                    sp.wait_ge(c_stack, 4 * H * B)
                elif first:
                    sp.wait_ge(t_done, transposes_before(phase - 1, B - 1))
                else:
                    sp.wait_ge(t_done, transposes_before(phase, n) - TURN_TRANSPOSES[phase])
                sp.dma_start(XLN, tokens(x_in[phase], n)).then_inc(xln_ld, 16)

            def load_residual(phase, n):
                turn = seq(phase, n)
                since(sp, stored, 16 * turn)
                sp.dma_start(XRES, tokens(x_in[phase], n)).then_inc(res_ld, 16)
                sp.dma_start(GATE, gates_d[phase, bass.ds(n, 1), :].rearrange("o d -> (o d)").partition_broadcast(P)).then_inc(gate_ld, 16)

            sp.wait_ge(modw_done, 12)
            for u in range(2, 6):
                load_unit(u)
            sp.dma_start(XLN, tokens(x_in[PA], 0)).then_inc(xln_ld, 16)
            sp.wait_ge(gates_st, 16)
            load_residual(PA, 0)
            sp.dma_start(BV, a["bv"].partition_broadcast(P)).then_inc(row_ld, 16)

            def denominators(n, h):
                g, q = h // HG, h % HG
                sp.wait_ge(c_ocp, H * n + h + 1)
                sp.dma_start(den_rows[g % 2, q:q + 1, :], SLD[h % 4][32:33, :]).then_inc(c_den[q], 16)
                if q == HG - 1:
                    since(sp, c_deni, KC * n + g - 1)
                    for s_ in c_den:
                        sp.wait_ge(s_, 16 * (KC * n + g + 1))
                    sp.dma_start(DEN[:, g % 2], den_rows[g % 2].rearrange("q (p i) -> p q i", i=S // P)).then_inc(c_dencp, 16)
                    sp.wait_ge(c_deni, KC * n + g + 1)
                    sp.dma_start(inv_rows[g % 2].rearrange("q (p i) -> p q i", i=S // P), DENI[:, g % 2]).then_inc(c_denst, 16)
                    sp.wait_ge(c_denst, 16 * (KC * n + g + 1))
                    since(sp, c_on, KC * n + g)
                    for r_ in range(HG):
                        sp.dma_start(RC[HD * r_:HD * r_ + HD], inv_rows[g % 2, r_].partition_broadcast(HD)).then_inc(c_rcld, 16)

            def body(phase, n, first, last):
                if first and phase in (PB, PD):
                    for j in range(2, 6):
                        load_unit(W_FIRST[phase] + j)
                nxt = after(phase, n, last)
                if phase == PC:
                    for h in range(11):
                        denominators(n, h)
                if nxt:
                    load_ln(*nxt)
                if phase == PC:
                    for h in range(11, H):
                        denominators(n, h)
                if first and phase in (PB, PD):
                    for j in range(6, FC):
                        load_unit(W_FIRST[phase] + j)
                if last and phase < PD:
                    for j in range(8 if phase == PB else 2):
                        load_unit(W_FIRST[phase + 1] + j)
                sp.wait_ge(res_done, TT * (seq(phase, n) + 1))
                sp.dma_start(tokens(x_out[phase], n), XRES).then_inc(stored, 16)
                if nxt:
                    load_residual(*nxt)
                if last and phase == PA:
                    sp.dma_start(B2, a["b2"].partition_broadcast(P)).then_inc(row_ld, 16)

            for phase in range(4):
                over_sequences(sp, body, phase)
            sp.wait_ge(stored, 16 * 4 * B)

        @block.gpsimd
        def _(pool):
            pool.memset(ID_F[:], 0.0).then_inc(consts, 1)
            pool.memset(MINUS_HALF[:], -0.5).then_inc(consts, 1)
            pool.wait_ge(consts, 2)
            pool.affine_select(out=ID_F[:], in_=ID_F[:], compare_op=ALU.not_equal, fill=1.0, base=0,
                               pattern=[[-1, P]], channel_multiplier=1).then_inc(consts, 1)

            def rstd(turn):
                pool.wait_ge(ln_v, LN_STEPS * turn + 10)
                pool.tensor_tensor(RSTD[:], VEPS[:], MINUS_HALF[:], ALU.pow).then_inc(ln_rstd, 1)

            def add_residual(phase, n):
                turn = seq(phase, n)
                pool.wait_ge(res_ld, 16 * (turn + 1))
                for t in range(TT):
                    if phase == PB:
                        pool.wait_ge(gate_ld, 16 * (turn + 1))
                        pool.wait_ge(b_gelu, TT * n + t + 1)
                        pool.tensor_tensor(TMP[t % 2], TMP[t % 2], GATE, ALU.mult).then_inc(res_step, 1)
                        pool.wait_ge(res_step, TT * n + t + 1)
                    else:
                        pool.wait_ge(tmp_rdy, TT * (turn) + t + 1)
                    pool.tensor_tensor(XRES[:, t], XRES[:, t], TMP[t % 2], ALU.add).then_inc(res_done, 1)

            rstd(0)

            def plain_body(phase, n, first, last):
                nxt = after(phase, n, last)
                if nxt:
                    rstd(seq(*nxt))
                add_residual(phase, n)

            def c_body(phase, n, first, last):
                def rope(n, us):
                    for u in us:
                        dst = (QF, KF)[u // TT][:, u % TT]
                        pool.wait_ge(c_evac, 12 * n + u + 1)
                        pool.tensor_tensor(dst, dst, ROT[u % 2], ALU.add).then_inc(c_rope, 1)

                if first:
                    rope(n, range(TT))
                rope(n, range(TT, 2 * TT))
                for h in range(H):
                    for t in range(TT):
                        if t % 2 == 0:
                            pool.wait_ge(c_exp, 64 * n + TT * h + t + 1)
                        else:
                            pool.wait_ge(c_phd, 32 * n + 2 * h + t // 2 + 1)
                        pool.tensor_tensor(PTL[h % 2][:, t], PE[t], PTH[h % 2][:, t].bitcast(F32), ALU.subtract).then_inc(c_pl, 1)
                    if h == H - 2:
                        nxt = after(phase, n, last)
                        if nxt:
                            rstd(seq(*nxt))
                if not last:
                    rope(n + 1, range(TT))
                add_residual(phase, n)

            for phase in range(4):
                over_sequences(pool, c_body if phase == PC else plain_body, phase)

        @block.vector
        def _(dve):
            dve.wait_ge(consts, 3)
            dve.tensor_copy(ID_R[:], ID_F[:]).then_inc(idr_rdy, 1)
            dve.wait_ge(vec_done, 1)
            dve.tensor_copy(CT[:], PS[:, 0, 0:64].rearrange("p (k b) -> p k b", b=B)).then_inc(const_evac, 1)
            dve.tensor_copy(VEC[:], PS[:, 0, 64:168]).then_inc(const_evac, 1)
            dve.wait_ge(const_evac, 2)
            dve.wait_ge(silu_a, 1)
            dve.tensor_scalar(SE[:], SE[:], 1.0, None, ALU.add).then_inc(silu_a, 1)
            dve.wait_ge(silu_a, 2)
            dve.reciprocal(SE[:], SE[:]).then_inc(silu_a, 1)
            dve.wait_ge(silu_a, 3)
            dve.tensor_tensor(ST_[:], CT[:, 4:8], SE[:], ALU.mult).then_inc(const_evac, 1)

            def split_unit(u, dst_hi, dst_lo, w_count):
                slot = u % 2
                dve.wait_ge(w_ld[slot], w_count)
                dve.tensor_copy(dst_hi, STAGE[:, slot, :]).then_inc(w_split, 1)
                dve.wait_ge(w_split, 2 * u + 1)
                dve.tensor_tensor(dst_lo, STAGE[:, slot, :], dst_hi.bitcast(F32), ALU.subtract).then_inc(w_split, 1)

            arrived = []
            count = [0, 0]
            for u in range(sum(W_UNITS)):
                phase = max(p for p in range(4) if W_FIRST[p] <= u)
                count[u % 2] += 16 if phase in (PA, PC) else 32
                arrived.append(count[u % 2])

            def split_square(phase, j):
                u = W_FIRST[phase] + j
                base = W_SLOT * 2 * (j // 2) + 1024 * (j % 2)
                split_unit(u, R[:, base:base + 1024], R[:, base + W_SLOT:base + W_SLOT + 1024], arrived[u])

            def split_chunk(phase, j):
                u = W_FIRST[phase] + j
                base = W_SLOT * SLOT_OF[phase][j]
                split_unit(u, R[:, base:base + 1024], R[:, base + 1024:base + 2048], arrived[u])

            for j in range(2):
                split_square(PA, j)
            steps = 0
            for layer in range(2):
                dve.wait_ge(modw_done, 6 * layer + 6)
                for half in range(2):
                    v0 = ((1, 4), (0, 3))[layer][half]
                    bias = VEC[:, 24 * layer + 4 * v0:24 * layer + 4 * v0 + 8]
                    dst = MOD[:, 2 * half:2 * half + 2].rearrange("p v f b -> p (v f) b")
                    src = PS[:, 1 + layer, 64 * half:64 * half + 64].rearrange("p (v b) -> p v b", b=B)
                    since(dve, mod_steps, steps)
                    dve.tensor_tensor(dst, src, bias.unsqueeze(2).broadcast_to([P, 8, B]), ALU.add).then_inc(mod_steps, 1)
                    steps += 1
                dve.wait_ge(mod_steps, steps)
                for half in range(2):
                    ln = 2 * layer + half
                    m_g, m_b = ((MOD[:, 2 * half], MOD[:, 2 * half + 1]), (MOD[:, 2 * half + 1], MOD[:, 2 * half]))[layer]
                    gain = VEC[:, 48 + 8 * ln:52 + 8 * ln].unsqueeze(2).broadcast_to([P, KC, B])
                    offset = VEC[:, 52 + 8 * ln:56 + 8 * ln].unsqueeze(2).broadcast_to([P, KC, B])
                    dve.scalar_tensor_tensor(LN_SCALE[:, ln], m_g, 1.0, gain, ALU.add, ALU.mult).then_inc(mod_steps, 1)
                    dve.scalar_tensor_tensor(LN_SHIFT[:, ln], m_g, 1.0, offset, ALU.add, ALU.mult).then_inc(mod_steps, 1)
                    steps += 2
                    dve.wait_ge(mod_steps, steps)
                    dve.tensor_tensor(LN_SHIFT[:, ln], LN_SHIFT[:, ln], m_b, ALU.add).then_inc(mod_steps, 1)
                    steps += 1
                for half in range(2):
                    g = 2 * layer + half
                    dve.tensor_tensor(GROW[:, g * D:(g + 1) * D], PS[0:B, 3 + g, :], GBIAS[:, g * D:(g + 1) * D],
                                      ALU.add).then_inc(gate_evac, 1)
            assert steps == MOD_STEPS
            for j in range(2, 6):
                split_square(PA, j)

            def ln_moments(turn, tiles):
                if tiles[0] == 0:
                    dve.wait_ge(xln_ld, 16 * (turn + 1))
                    since(dve, ln_v, LN_STEPS * turn)
                for t in tiles:
                    dve.bn_stats(STATS[:, t], XLN[:, t]).then_inc(ln_v, 1)

            def ln_variance(turn):
                dve.wait_ge(ln_v, LN_STEPS * turn + 4)
                dve.memset(VEPS[:], EPS).then_inc(ln_v, 1)
                for t in range(TT):
                    dve.bn_aggr(MV[:, t], STATS[:, t]).then_inc(ln_v, 1)
                dve.wait_ge(ln_v, LN_STEPS * turn + 9)
                dve.tensor_tensor(VEPS[:], MV[:, :, 1], VEPS[:], ALU.add).then_inc(ln_v, 1)

            def ln_stats(turn):
                ln_moments(turn, range(TT))
                ln_variance(turn)

            def ln_norm(turn):
                dve.wait_ge(ln_rstd, turn + 1)
                for t in range(TT):
                    dve.tensor_scalar(XLN[:, t], XLN[:, t], MV[:, t, 0:1], RSTD[:, t:t + 1], ALU.subtract, ALU.mult).then_inc(ln_v, 1)

            def split_x(turn):
                for k in range(KC):
                    dve.wait_ge(xh_rdy, KC * turn + k + 1)
                    dve.tensor_tensor(XL[:, k], Y[:, k], XH[:, k].bitcast(F32), ALU.subtract).then_inc(xl_rdy, 1)

            def tmp_free(turn, t):
                since(dve, res_done, TT * turn + t - 1)

            ln_stats(0)
            ln_norm(0)
            split_x(0)

            def a_body(phase, n, first, last):
                turn = seq(phase, n)
                nxt = after(phase, n, last)
                for u in range(2 * KC):
                    hi, lo, vec = ((A_QH, A_QL, VECQ), (A_KH, A_KL, VECK))[u // KC]
                    k = u % KC
                    dve.wait_ge(a_qkh, 8 * n + u + 1)
                    dve.scalar_tensor_tensor(lo[:, k], PS[:, u % 4, :], VEC[:, vec + k:vec + k + 1], hi[:, k].bitcast(F32),
                                             ALU.add, ALU.subtract).then_inc(a_evac, 1)
                    if u == 2 and nxt:
                        ln_stats(seq(*nxt))
                    if u == 4 and nxt:
                        ln_norm(seq(*nxt))
                if first:
                    dve.wait_ge(row_ld, 16)
                for t in range(TT + 1):
                    if t < TT:
                        dve.wait_ge(a_qkv, 12 * n + 8 + t + 1)
                        since(dve, a_vlo, TT * n + t - 1)
                        dve.tensor_tensor(A_VT[t % 2], PS[:, t, :], BV, ALU.add).then_inc(a_evac, 1)
                    if t >= 1:
                        dve.wait_ge(a_vhi, TT * n + t)
                        dve.tensor_tensor(A_VL[:, t - 1], A_VT[(t - 1) % 2], A_VH[:, t - 1].bitcast(F32), ALU.subtract).then_inc(a_vlo, 1)
                since(dve, a_exp, TT * n)
                since(dve, a_mx, 8 * n)
                for s in range(TT):
                    dve.wait_ge(a_s, TT * n + s + 1)
                    dve.reduce_max(MX[:, s:s + 1], PS[:, s, :], AX.X).then_inc(a_mx, 1)
                    dve.wait_ge(a_mx, 8 * n + 2 * s + 1)
                    dve.tensor_scalar(NB[:, s:s + 1], MX[:, s:s + 1], -SCALE0, None, ALU.mult).then_inc(a_mx, 1)
                dve.wait_ge(a_exp, TT * n + TT)
                since(dve, tmp_rdy, TT * turn)
                dve.reciprocal(RS[:], SM[:]).then_inc(a_rs, 1)
                for s in range(TT):
                    dve.wait_ge(a_ppa, TT * n + s + 1)
                    dve.tensor_tensor(A_PL[:, s], PS[:, 4 + s % 2, :], A_PH[:, s].bitcast(F32), ALU.subtract).then_inc(a_ppe, 1)
                if last:
                    for j in range(2):
                        split_chunk(PB, j)
                if nxt:
                    split_x(seq(*nxt))
                dve.wait_ge(gate_ld, 16 * (turn + 1))
                dve.wait_ge(a_rs, n + 1)
                for s in range(TT):
                    dve.wait_ge(a_pv, TT * n + s + 1)
                    tmp_free(turn, s)
                    dve.scalar_tensor_tensor(TMP[s % 2], PS[:, s, :], RS[:, s:s + 1], GATE, ALU.mult, ALU.mult).then_inc(tmp_rdy, 1)

            def mlp_body(phase, n, first, last):
                turn = seq(phase, n)
                nxt = after(phase, n, last)
                for j in range(FC):
                    if first and j + 2 < FC:
                        if j == 0:
                            dve.wait_ge(*((a_pv, TT * B) if phase == PB else (c_wo, TT * B)))
                        split_chunk(phase, j + 2)
                    dve.wait_ge(m_hi[phase], FC * n + j + 1)
                    dve.tensor_tensor(HL[j % 4], HID[j % 4], HH[j % 4].bitcast(F32), ALU.subtract).then_inc(m_lo[phase], 1)
                    if j == 7 and nxt:
                        ln_stats(seq(*nxt))
                    if j == 8 and nxt:
                        ln_norm(seq(*nxt))
                    if last and phase == PB and j >= 12:
                        if j == 12:
                            dve.wait_ge(m_down[PB], FC * n + 10)
                        for i in range(2):
                            split_square(PC, 2 * (j - 12) + i)
                if nxt:
                    split_x(seq(*nxt))
                if first and phase == PB:
                    dve.wait_ge(row_ld, 32)
                if phase == PD:
                    dve.wait_ge(gate_ld, 16 * (turn + 1))
                dve.wait_ge(m_down[phase], FC * n + FC)
                for t in range(TT):
                    tmp_free(turn, t)
                    if phase == PB:
                        dve.tensor_tensor(TMP[t % 2], PS[:, t, :], B2, ALU.add).then_inc(tmp_rdy, 1)
                    else:
                        dve.tensor_tensor(TMP[t % 2], PS[:, t, :], GATE, ALU.mult).then_inc(tmp_rdy, 1)

            def c_body(phase, n, first, last):
                turn = seq(phase, n)
                nxt = after(phase, n, last)
                if first:
                    dve.wait_ge(const_ld, 16 * N_CONST)
                    dve.wait_ge(m_down[PB], FC * B)
                    for i in range(3):
                        dve.memset(KT[i][96:97].bitcast(F32), 1.0).then_inc(c_ones, 1)
                    for t in range(TT):
                        dve.memset(VSH[:, t, :, HD:64].bitcast(F32), 1.0).then_inc(c_ones, 1)

                def rope(n, us):
                    for u in us:
                        t = u % TT
                        dst = (QF, KF)[u // TT][:, t].rearrange("p (h d) -> p h d", d=HD)
                        src = PS[:, QKV_BANK[u], :].rearrange("p (h d) -> p h d", d=HD)
                        rot = ROT[u % 2].rearrange("p (h d) -> p h d", d=HD)
                        dve.wait_ge(c_qkv, 12 * n + u + 1)
                        since(dve, c_rope, 8 * n + u - 1)
                        if u == 0:
                            since(dve, c_oadd, H * n)
                        dve.tensor_tensor(dst, src, COS[:, t].unsqueeze(1).broadcast_to([P, H, HD]), ALU.mult).then_inc(c_rot, 1)
                        dve.tensor_tensor(rot[:, :, 0:HD // 2], src[:, :, 1::2],
                                          SIN[:, t, 0:HD // 2].unsqueeze(1).broadcast_to([P, H, HD // 2]), ALU.mult).then_inc(c_rot, 1)
                        dve.wait_ge(c_rot, 16 * n + 2 * u + 2)
                        dve.tensor_tensor(rot[:, :, HD // 2:HD], src[:, :, 0::2],
                                          SIN[:, t, HD // 2:HD].unsqueeze(1).broadcast_to([P, H, HD // 2]), ALU.mult).then_inc(c_evac, 1)

                if first:
                    rope(n, range(TT))
                rope(n, range(TT, 2 * TT))

                def stack(h):
                    i = h % 2
                    dve.wait_ge(t_done, transposes_c(n, h - 2, 1))
                    cols = slice(h * HD, (h + 1) * HD)
                    halves = ((QF, QS[i], slice(0, 2), slice(64, 96)), (KF, KS[i], slice(0, 3, 2), slice(32, 64)))
                    for src, st, hi2, _ in halves:
                        out = st.rearrange("p t (c d) -> p t c d", d=HD)[:, :, hi2, :]
                        dve.tensor_copy(out, src[:, :, cols].unsqueeze(2).broadcast_to([P, TT, 2, HD])).then_inc(c_stack, 1)
                    for x, (src, st, _, lo) in enumerate(halves):
                        dve.wait_ge(c_stack, 4 * (H * n + h) + x + 1)
                        dve.tensor_tensor(st[:, :, lo], src[:, :, cols], st[:, :, 0:HD].bitcast(F32), ALU.subtract).then_inc(c_stack, 1)

                def maximum(h, s):
                    if s == 0:
                        since(dve, c_mm, H * n + max(h - 2, 0))
                    e = TT * h + s
                    dve.wait_ge(c_s, 64 * n + e + 1)
                    dve.reduce_max(MX1[:, h % 3, s:s + 1], PS[:, e % 2, :], AX.X).then_inc(c_max, 1)

                def minus_max(h):
                    dve.wait_ge(c_max, 64 * n + TT * h + TT)
                    dve.wait_ge(t_done, transposes_c(n, h - 3, 2))
                    dve.tensor_scalar(MM[:, h % 3], MX1[:, h % 3], -1.0, None, ALU.mult).then_inc(c_mm, 1)

                def sum_head(h):
                    g, q = h // HG, h % HG
                    if q == 0:
                        since(dve, c_ol, KC * n + g - 1)
                    dve.wait_ge(c_ocp, H * n + h + 1)
                    dve.tensor_tensor(OA[g % 2][HD * q:HD * (q + 1)], PS[64:96, 5, :], SLD[h % 4][0:HD], ALU.add).then_inc(c_oadd, 1)

                def invert(g):
                    dve.wait_ge(c_dencp, 16 * (KC * n + g + 1))
                    since(dve, c_denst, 16 * (KC * n + g - 1))
                    dve.reciprocal(DENI[:, g % 2], DEN[:, g % 2]).then_inc(c_deni, 1)

                def normalise(g):
                    dve.wait_ge(c_rcld, 64 * (KC * n + g + 1))
                    dve.wait_ge(c_oadd, H * n + HG * (g + 1))
                    dve.tensor_tensor(OA[g % 2], OA[g % 2], RC, ALU.mult).then_inc(c_on, 1)

                def low(g):
                    dve.wait_ge(c_oh, KC * n + g + 1)
                    dve.tensor_tensor(OTL[g], OA[g % 2], OTH[g].bitcast(F32), ALU.subtract).then_inc(c_ol, 1)

                def v_low(t):
                    dve.wait_ge(c_vhi, TT * n + t + 1)
                    dve.tensor_tensor(VSH[:, t, :, 0:HD], PS[:, QKV_BANK[8 + t], :].rearrange("p (h d) -> p h d", d=HD),
                                      VSH[:, t, :, 64:96].bitcast(F32), ALU.subtract).then_inc(c_evac, 1)

                def prob_hi(h, t):
                    dve.wait_ge(c_exp, 64 * n + TT * h + t + 1)
                    if t == 1:
                        since(dve, c_o, H * n + h - 1)
                    dve.tensor_copy(PTH[h % 2][:, t], PE[t]).then_inc(c_phd, 1)

                dve.wait_ge(c_rope, 8 * n + 8)
                stack(0)
                v_low(0)
                stack(1)
                v_low(1)
                maximum(0, 0)
                maximum(0, 1)
                v_low(2)
                maximum(0, 2)
                maximum(0, 3)
                minus_max(0)
                v_low(3)
                stack(2)
                for s in range(TT):
                    maximum(1, s)
                minus_max(1)
                for h in range(H + 1):
                    if h + 3 < H:
                        stack(h + 3)
                    if h < H:
                        prob_hi(h, 1)
                    if h in (8, 12, 16):
                        low((h - 8) // HG)
                    if h == H - 2 and nxt:
                        ln_moments(seq(*nxt), range(2))
                    if h + 2 < H:
                        maximum(h + 2, 0)
                        maximum(h + 2, 1)
                    if h in (7, 11, 15):
                        normalise((h - 7) // HG)
                    if h < H:
                        prob_hi(h, 3)
                    if h >= 1:
                        sum_head(h - 1)
                    if h + 2 < H:
                        maximum(h + 2, 2)
                        maximum(h + 2, 3)
                        minus_max(h + 2)
                    if h in (5, 9, 13):
                        invert((h - 5) // HG)
                    if h == H - 2 and nxt:
                        ln_moments(seq(*nxt), range(2, TT))
                        ln_variance(seq(*nxt))
                    if h == H - 1 and nxt:
                        ln_norm(seq(*nxt))
                if nxt:
                    split_x(seq(*nxt))
                invert(KC - 1)
                if last:
                    for j in range(2):
                        split_chunk(PD, j)
                if not last:
                    rope(n + 1, range(2))
                normalise(KC - 1)
                low(KC - 1)
                if not last:
                    rope(n + 1, range(2, TT))
                dve.wait_ge(gate_ld, 16 * (turn + 1))
                for t in range(TT):
                    dve.wait_ge(c_wo, TT * n + t + 1)
                    tmp_free(turn, t)
                    dve.tensor_tensor(TMP[t % 2], PS[:, t, :], GATE, ALU.mult).then_inc(tmp_rdy, 1)

            for phase in range(4):
                over_sequences(dve, (a_body, mlp_body, c_body, mlp_body)[phase], phase)

        @block.scalar
        def _(act):
            act.wait_ge(const_evac, 1)
            act.activation(SE[:], CT[:, 4:8], ACT.Exp, scale=-1.0).then_inc(silu_a, 1)

            def evacuate_y(phase, n):
                turn = seq(phase, n)
                since(act, xl_rdy, KC * turn)
                for k in range(KC):
                    act.wait_ge(t_done, transposes_before(phase, n) - KC + k + 1)
                    act.activation(Y[:, k], PS[:, 6 + k % 2, :], ACT.Identity,
                                   scale=LN_SCALE[:, phase, k, bass.ds(n, 1)], bias=LN_SHIFT[:, phase, k, bass.ds(n, 1)]).then_inc(y_rdy, 1)

            def split_x(phase, n, prev):
                turn = seq(phase, n)
                for k in range(KC):
                    if prev:
                        operand_free(act, *prev, k)
                    act.wait_ge(y_rdy, KC * turn + k + 1)
                    act.activation(XH[:, k], Y[:, k], ACT.Identity).then_inc(xh_rdy, 1)

            act.wait_ge(mod_steps, MOD_STEPS)
            evacuate_y(PA, 0)
            split_x(PA, 0, None)

            def a_body(phase, n, first, last):
                nxt = after(phase, n, last)
                since(act, a_s, TT * n)
                for u in range(2 * KC):
                    hi, vec = ((A_QH, VECQ), (A_KH, VECK))[u // KC]
                    k = u % KC
                    act.wait_ge(a_qkv, 12 * n + u + 1)
                    act.activation(hi[:, k], PS[:, u % 4, :], ACT.Identity, bias=VEC[:, vec + k:vec + k + 1]).then_inc(a_qkh, 1)
                since(act, a_pv, TT * n)
                for t in range(TT):
                    act.wait_ge(a_evac, 12 * n + 8 + t + 1)
                    act.activation(A_VH[:, t], A_VT[t % 2], ACT.Identity).then_inc(a_vhi, 1)
                if nxt:
                    evacuate_y(*nxt)
                since(act, a_rs, n)
                for s in range(TT):
                    act.wait_ge(a_mx, 8 * n + 2 * s + 2)
                    act.activation(A_P[:, s], PS[:, s, :], ACT.Exp, bias=NB[:, s:s + 1], scale=SCALE0,
                                   accum_out=SM[:, s:s + 1]).then_inc(a_exp, 1)
                for s in range(TT):
                    act.wait_ge(a_pp, TT * n + s + 1)
                    act.activation(A_PH[:, s], PS[:, 4 + s % 2, :], ACT.Identity).then_inc(a_ppa, 1)
                if nxt:
                    split_x(*nxt, (phase, n))

            def mlp_body(phase, n, first, last):
                nxt = after(phase, n, last)
                for j in range(FC):
                    act.wait_ge(m_up[phase], FC * n + j + 1)
                    since(act, m_lo[phase], FC * n + j - 3)
                    if first and phase == PD and j == 0:
                        act.wait_ge(c_pl, 64 * B)
                    bias = VEC[:, VECB1 + j:VECB1 + j + 1] if phase == PB else 0.0
                    act.activation(HID[j % 4], PS[:, 4 + j % 2, :], ACT.Gelu, bias=bias).then_inc(m_gelu[phase], 1)
                    act.wait_ge(m_gelu[phase], FC * n + j + 1)
                    since(act, m_down[phase], FC * n + j - 3)
                    act.activation(HH[j % 4], HID[j % 4], ACT.Identity).then_inc(m_hi[phase], 1)
                    if j == 10 and nxt:
                        evacuate_y(*nxt)
                if nxt:
                    split_x(*nxt, (phase, n))
                if phase == PB:
                    for t in range(TT):
                        act.wait_ge(tmp_rdy, TT * seq(phase, n) + t + 1)
                        act.activation(TMP[t % 2], TMP[t % 2], ACT.Gelu).then_inc(b_gelu, 1)

            def c_body(phase, n, first, last):
                nxt = after(phase, n, last)
                if first:
                    act.wait_ge(m_down[PB], FC * B)
                since(act, c_o, H * n)

                def v_hi(t):
                    act.wait_ge(c_qkv, 12 * n + 8 + t + 1)
                    act.activation(VSH[:, t, :, 64:96], PS[:, QKV_BANK[8 + t], :].rearrange("p (h d) -> p h d", d=HD), ACT.Identity).then_inc(c_vhi, 1)

                def evacuate(h, what, rows, dst):
                    act.wait_ge(t_done, transposes_c(n, h, what))
                    act.activation(dst, PS[0:rows, 6 + T_USE[h, what] % 2, :], ACT.Identity).then_inc(t_evac, 1)

                def evacuate_q(h):
                    since(act, c_st, 64 * n + TT * max(h - 2, 0))
                    evacuate(h, 0, 96, QT[h % 3][0:96])

                def evacuate_k(h):
                    evacuate(h, 1, 96, KT[h % 3][0:96])

                def evacuate_m(h):
                    evacuate(h, 2, 1, QT[h % 3][96:97])

                def copy_out(h):
                    act.wait_ge(c_o, H * n + h + 1)
                    since(act, c_oadd, H * n + h - 3)
                    since(act, c_den[h % HG], 16 * (KC * n + h // HG))
                    if h == 0:
                        act.wait_ge(c_rope, 8 * n + 8)
                    act.activation(SLD[h % 4], PS[0:64, 5, :], ACT.Identity).then_inc(c_ocp, 1)

                def normalised_hi(g):
                    act.wait_ge(c_on, KC * n + g + 1)
                    act.activation(OTH[g], OA[g % 2], ACT.Identity).then_inc(c_oh, 1)

                def exponential(h, t):
                    e = TT * h + t
                    act.wait_ge(c_st, 64 * n + e + 1)
                    since(act, c_pl, 64 * n + e - 3)
                    if h == 0 and t == 0 and first:
                        act.wait_ge(m_lo[PB], FC * B)
                    if t == 0:
                        since(act, c_o, H * n + h - 1)
                    if t % 2 == 0:
                        act.activation(PTH[h % 2][:, t], PS[:, 2 + e % 3, :], ACT.Exp, scale=SCALE1).then_inc(c_pha, 1)
                    act.activation(PE[t], PS[:, 2 + e % 3, :], ACT.Exp, scale=SCALE1).then_inc(c_exp, 1)

                v_hi(0)
                v_hi(1)
                evacuate_q(0)
                evacuate_k(0)
                v_hi(2)
                v_hi(3)
                evacuate_m(0)
                evacuate_q(1)
                evacuate_k(1)
                for h in range(H + 1):
                    if h + 2 < H:
                        evacuate_q(h + 2)
                    if h < H:
                        exponential(h, 0)
                    if h + 2 < H:
                        evacuate_k(h + 2)
                    if h < H:
                        exponential(h, 1)
                        exponential(h, 2)
                        exponential(h, 3)
                    if h == H and nxt:
                        evacuate_y(*nxt)
                    if h + 1 < H:
                        evacuate_m(h + 1)
                    if h >= 1:
                        copy_out(h - 1)
                    if h in (7, 11, 15):
                        normalised_hi((h - 7) // HG)
                if nxt:
                    split_x(*nxt, (phase, n))
                normalised_hi(KC - 1)

            for phase in range(4):
                over_sequences(act, (a_body, mlp_body, c_body, mlp_body)[phase], phase)

        @block.tensor
        def _(pe):
            def product(out, x, w, start, stop):
                (xh, xl), (wh, wl) = x, w
                pe.matmul(out, xh, wh, start=start, stop=False)
                pe.matmul(out, xh, wl, start=False, stop=False)
                return pe.matmul(out, xl, wh, start=False, stop=stop)

            pe.wait_ge(const_ld, 16 * N_CONST)
            pe.wait_ge(consts, 3)
            for k in range(8):
                pe.transpose(PS[:, 0, B * k:B * k + B], COND_ROWS[:, P * k:P * k + P], ID_F[0:B, 0:B])
            pe.transpose(PS[:, 0, 64:168], VEC_ROWS, ID_F[0:104, 0:104]).then_inc(vec_done, 1)
            pe.wait_ge(const_evac, 3)
            seen = [0, 0]
            for blk in range(12):
                layer, v = blk // 6, blk % 6
                slot, kn = blk % 2, (8, 4)[layer]
                seen[slot] += 16
                pe.wait_ge(modw_ld[slot], seen[slot])
                c = CT if layer == 0 else ST_
                w = STAGE_W[slot][:, 0:kn * D].rearrange("p (k n) -> p k n", n=D)
                is_gate = v in ((0, 3), (2, 5))[layer]
                if is_gate:
                    g = 2 * layer + (v > 2)
                    for k in range(kn):
                        mm = pe.matmul(PS[0:B, 3 + g, :], c[:, k, :], w[:, k, :], start=k == 0, stop=k == kn - 1)
                else:
                    at = [x for x in range(6) if x not in ((0, 3), (2, 5))[layer]].index(v)
                    for fc in range(KC):
                        o = PS[:, 1 + layer, 32 * at + B * fc:32 * at + B * fc + B]
                        for k in range(kn):
                            mm = pe.matmul(o, w[:, k, P * fc:P * fc + P], c[:, k, :], start=k == 0, stop=k == kn - 1)
                mm.then_inc(modw_done, 1)

            def transpose_x(phase, n):
                turn = seq(phase, n)
                pe.wait_ge(ln_v, LN_STEPS * (turn + 1))
                for k in range(KC):
                    since(pe, y_rdy, KC * turn + k - 1)
                    for t in range(TT):
                        mm = pe.transpose(PS[:, 6 + k % 2, P * t:P * t + P], XLN[:, t, P * k:P * k + P], ID_F[:])
                    mm.then_inc(t_done, 1)

            pe.wait_ge(gate_evac, 4)
            transpose_x(PA, 0)

            def a_body(phase, n, first, last):
                turn = seq(phase, n)
                nxt = after(phase, n, last)
                if first:
                    pe.wait_ge(w_split, 2 * W_FIRST[PB])
                for u in range(2 * KC):
                    fc = u % KC
                    if u < 4:
                        since(pe, tmp_rdy, TT * (turn - 1) + u + 1)
                    else:
                        pe.wait_ge(a_evac, 12 * n + u - 3)
                    wh, wl = A_W[u // KC]
                    for k in range(KC):
                        if u == 0:
                            pe.wait_ge(xl_rdy, KC * turn + k + 1)
                        cols = slice(P * fc, P * fc + P)
                        mm = product(PS[:, u % 4, :], (wh[:, k, cols], wl[:, k, cols]), (XH[:, k], XL[:, k]), k == 0, k == KC - 1)
                    mm.then_inc(a_qkv, 1)
                for t in range(TT):
                    pe.wait_ge(a_evac, 12 * n + 8 + t - 3)
                    wh, wl = A_W[2]
                    for k in range(KC):
                        cols = slice(P * t, P * t + P)
                        mm = product(PS[:, t, :], (XH[:, k, cols], XL[:, k, cols]), (wh[:, k], wl[:, k]), k == 0, k == KC - 1)
                    mm.then_inc(a_qkv, 1)
                for s in range(TT):
                    pe.wait_ge(a_evac, 12 * n + 8 + s + 1)
                    for k in range(KC):
                        cols = slice(P * s, P * s + P)
                        mm = product(PS[:, s, :], (A_QH[:, k, cols], A_QL[:, k, cols]), (A_KH[:, k], A_KL[:, k]), k == 0, k == KC - 1)
                    mm.then_inc(a_s, 1)
                    if s == 1 and nxt:
                        transpose_x(*nxt)

                def transpose_p(s):
                    pe.wait_ge(a_exp, TT * n + s + 1)
                    since(pe, a_ppe, TT * n + s - 1)
                    for t in range(TT):
                        mm = pe.transpose(PS[:, 4 + s % 2, P * t:P * t + P], A_P[:, s, P * t:P * t + P], ID_F[:])
                    mm.then_inc(a_pp, 1)

                def attend(s):
                    pe.wait_ge(a_ppe, TT * n + s + 1)
                    if s == 0:
                        pe.wait_ge(a_vlo, TT * n + TT)
                    for t in range(TT):
                        cols = slice(P * t, P * t + P)
                        mm = product(PS[:, s, :], (A_PH[:, s, cols], A_PL[:, s, cols]), (A_VH[:, t], A_VL[:, t]), t == 0, t == TT - 1)
                    mm.then_inc(a_pv, 1)

                transpose_p(0)
                transpose_p(1)
                for s in range(TT):
                    attend(s)
                    if s + 2 < TT:
                        transpose_p(s + 2)

            def mlp_body(phase, n, first, last):
                turn = seq(phase, n)
                nxt = after(phase, n, last)

                def up(j):
                    if first:
                        pe.wait_ge(w_split, 2 * (W_FIRST[phase] + j + 1))
                        if j < 2:
                            pe.wait_ge(*((a_ppe, TT * B) if phase == PB else (c_oadd, H * B)))
                    since(pe, m_gelu[phase], FC * n + j - 1)
                    (wh, wl), _ = w_chunk(phase, j)
                    for k in range(KC):
                        if j == 0:
                            pe.wait_ge(xl_rdy, KC * turn + k + 1)
                        mm = product(PS[:, 4 + j % 2, :], (wh[:, k], wl[:, k]), (XH[:, k], XL[:, k]), k == 0, k == KC - 1)
                    mm.then_inc(m_up[phase], 1)

                def down(j):
                    pe.wait_ge(m_lo[phase], FC * n + j + 1)
                    _, w = w_chunk(phase, j)
                    for t in range(TT):
                        if j == 0:
                            pe.wait_ge(tmp_rdy, TT * (turn - 1) + t + 1)
                        cols = slice(P * t, P * t + P)
                        mm = product(PS[:, t, :], (HH[j % 4][:, cols], HL[j % 4][:, cols]), w, j == 0, j == FC - 1)
                    mm.then_inc(m_down[phase], 1)

                up(0)
                for j in range(FC):
                    if j + 1 < FC:
                        up(j + 1)
                    down(j)
                    if j == 9 and nxt:
                        transpose_x(*nxt)

            def c_body(phase, n, first, last):
                turn = seq(phase, n)
                nxt = after(phase, n, last)
                if first:
                    pe.wait_ge(w_split, 2 * W_FIRST[PD])
                def project(n, u):
                    t, turn = u % TT, seq(PC, n)
                    if u >= 4:
                        pe.wait_ge(c_evac, 12 * n + u - 3)
                        if u in (6, 7):
                            pe.wait_ge(tmp_rdy, TT * (turn - 1) + u - 3)
                    elif first:
                        if u < 2:
                            pe.wait_ge(m_gelu[PB], FC * B)
                    elif u == 0:
                        pe.wait_ge(c_exp, 64 * n)
                    elif u == 1:
                        pe.wait_ge(c_oadd, H * n)
                    if u in (2, 3):
                        pe.wait_ge(y_rdy, KC * (turn + 1))
                    wh, wl = C_W[u // TT]
                    for k in range(KC):
                        if u == 0:
                            pe.wait_ge(xl_rdy, KC * turn + k + 1)
                        cols = slice(P * t, P * t + P)
                        mm = product(PS[:, QKV_BANK[u], :], (XH[:, k, cols], XL[:, k, cols]), (wh[:, k], wl[:, k]), k == 0, k == KC - 1)
                    mm.then_inc(c_qkv, 1)

                def transpose_bank(h, what):
                    use = T_USE[h, what]
                    if use < 2:
                        since(pe, y_rdy, KC * (turn + 1))
                    else:
                        pe.wait_ge(t_evac, 48 * n + use - 1)
                    return PS[:, 6 + use % 2, :].bitcast(F32R)

                def transpose_qk(h, what):
                    bank = transpose_bank(h, what)
                    pe.wait_ge(c_stack, 4 * (H * n + h) + what + 3)
                    st = (QS, KS)[what][h % 2]
                    for t in range(TT):
                        mm = pe.transpose(bank[0:96, P * t:P * t + P], st[:, t], ID_R[:])
                    mm.then_inc(t_done, 1)

                def transpose_m(h):
                    bank = transpose_bank(h, 2)
                    pe.wait_ge(c_mm, H * n + h + 1)
                    for t in range(TT):
                        mm = pe.transpose(bank[0:1, P * t:P * t + P], MM[:, h % 3, t:t + 1], ID_R[:])
                    mm.then_inc(t_done, 1)

                def scores(h, s):
                    e = TT * h + s
                    if s == 0:
                        pe.wait_ge(t_evac, 48 * n + T_USE[h, 1] + 1)
                    if e < 2:
                        pe.wait_ge(tmp_rdy, TT * turn)
                    else:
                        pe.wait_ge(c_max, 64 * n + e - 1)
                    pe.matmul(PS[:, e % 2, :], QT[h % 3][0:96, P * s:P * s + P], KT[h % 3][0:96], start=True, stop=True).then_inc(c_s, 1)

                def scores_t(h, t):
                    e = TT * h + t
                    if t == 0:
                        pe.wait_ge(t_evac, 48 * n + T_USE[h, 2] + 1)
                    if e == 0:
                        pe.wait_ge(c_evac, 12 * n + 12)
                    since(pe, c_exp, 64 * n + max(e - 2, 0))
                    pe.matmul(PS[:, 2 + e % 3, :], KT[h % 3][0:97, P * t:P * t + P], QT[h % 3][0:97], start=True, stop=True).then_inc(c_st, 1)

                def attend(h, t):
                    if t == 0:
                        since(pe, c_oadd, H * n + h)
                    pe.wait_ge(c_pl, 64 * n + TT * h + t + 1)
                    v = VS[:, t, 96 * h:96 * h + 96]
                    pe.matmul(PS[0:96, 5, :], v, PTH[h % 2][:, t], start=t == 0, stop=False)
                    mm = pe.matmul(PS[0:96, 5, :], v, PTL[h % 2][:, t], start=False, stop=t == TT - 1)
                    if t == TT - 1:
                        mm.then_inc(c_o, 1)

                if first:
                    for u in range(TT):
                        project(n, u)
                for u in range(TT, 10):
                    project(n, u)
                if first:
                    pe.wait_ge(c_ones, 7)
                transpose_qk(0, 0)
                transpose_qk(0, 1)
                project(n, 10)
                scores(0, 0)
                scores(0, 1)
                project(n, 11)
                scores(0, 2)
                scores(0, 3)
                transpose_m(0)
                transpose_qk(1, 0)
                transpose_qk(1, 1)
                for s in range(TT):
                    scores(1, s)
                def out_product(k, tiles):
                    wh, wl = C_W[3]
                    for t in tiles:
                        if t == 0:
                            pe.wait_ge(c_ol, KC * n + k + 1)
                            pe.wait_ge(c_max, 64 * n + 64)
                        if k == 0 and t == 2:
                            pe.wait_ge(c_exp, 64 * n + 64)
                        cols = slice(P * t, P * t + P)
                        mm = product(PS[:, t, :], (OTH[k][:, cols], OTL[k][:, cols]), (wh[:, k], wl[:, k]), k == 0, k == KC - 1)
                        if k == KC - 1:
                            mm.then_inc(c_wo, 1)
                        elif t == TT - 1:
                            mm.then_inc(c_wok, 1)

                for h in range(H):
                    ahead = h + 2 < H
                    if ahead:
                        transpose_qk(h + 2, 0)
                    scores_t(h, 0)
                    if ahead:
                        transpose_qk(h + 2, 1)
                    scores_t(h, 1)
                    scores_t(h, 2)
                    if h >= 1:
                        attend(h - 1, 0)
                        attend(h - 1, 1)
                    if ahead:
                        scores(h + 2, 0)
                        scores(h + 2, 1)
                    scores_t(h, 3)
                    if h + 1 < H:
                        transpose_m(h + 1)
                    if h >= 1:
                        attend(h - 1, 2)
                        attend(h - 1, 3)
                    if ahead:
                        scores(h + 2, 2)
                        scores(h + 2, 3)
                out_product(0, range(TT))
                attend(H - 1, 0)
                if nxt:
                    pe.wait_ge(t_evac, 48 * n + 48)
                    transpose_x(*nxt)
                attend(H - 1, 1)
                out_product(1, range(2))
                attend(H - 1, 2)
                out_product(1, range(2, TT))
                attend(H - 1, 3)
                out_product(2, range(TT))
                if not last:
                    for u in range(TT):
                        project(n + 1, u)
                out_product(3, range(TT))

            for phase in range(4):
                over_sequences(pe, (a_body, mlp_body, c_body, mlp_body)[phase], phase)


_INS = {
    "x": "x", "fside": "fside_BxS_0", "cond": "cond_1024",
    "Wq0": "L0_cond_Wq", "bq": "L0_cond_bq", "Wk0": "L0_cond_Wk", "bk": "L0_cond_bk", "Wv0": "L0_cond_Wv", "bv": "L0_cond_bv",
    "W1_0": "L0_cond_W1", "b1": "L0_cond_b1", "W2_0": "L0_cond_W2", "b2": "L0_cond_b2", "Wc": "L0_cond_Wc", "bc": "L0_cond_bc",
    "ln1_g": "L0_cond_ln1_g", "ln1_b": "L0_cond_ln1_b", "ln2_g": "L0_cond_ln2_g", "ln2_b": "L0_cond_ln2_b",
    "n1_g": "L1_cond_norm1_g", "n1_b": "L1_cond_norm1_b", "n2_g": "L1_cond_norm2_g", "n2_b": "L1_cond_norm2_b",
    "Wq1": "L1_cond_Wq", "Wk1": "L1_cond_Wk", "Wv1": "L1_cond_Wv", "Wo1": "L1_cond_Wo",
    "W1_1": "L1_cond_W1", "W2_1": "L1_cond_W2", "ada_W": "L1_cond_ada_W", "ada_b": "L1_cond_ada_b",
}


def rope_tables():
    inv = (1.0 / 10000.0 ** (np.arange(0, HD, 2, dtype=np.float32) / np.float32(HD))).astype(np.float32)
    freqs = np.outer(np.arange(S, dtype=np.float32), inv).astype(np.float32)
    emb = np.concatenate([freqs, freqs], -1)
    sign = np.where(np.arange(HD) < HD // 2, -1.0, 1.0).astype(np.float32)
    return np.cos(emb).astype(np.float32), (np.sin(emb).astype(np.float32) * sign).astype(np.float32)


def kernel(**inputs):
    import concourse.bacc as bacc
    from concourse.bass_utils import run_bass_kernel_spmd

    nc = bacc.Bacc("TRN2", target_bir_lowering=False, num_devices=1, dynamic_dma_scratch_size=1024)
    arrays = {f"in_{k}": np.ascontiguousarray(inputs[name]) for k, name in _INS.items()}
    arrays["in_cos"], arrays["in_sin"] = rope_tables()
    a = {n[3:]: nc.dram_tensor(n, v.shape, F32, kind="ExternalInput").ap() for n, v in arrays.items()}
    a["out"] = nc.dram_tensor("out_x", (B, S, D), F32, kind="ExternalOutput").ap()
    build(nc, a)
    r = run_bass_kernel_spmd(nc, [arrays], core_ids=[0])
    return r.results[0]["out_x"]
```

```python
from contextlib import ExitStack

import concourse.bass as bass
import numpy as np
from concourse import mybir

F32 = mybir.dt.float32
F32R = mybir.dt.float32r
ACT = mybir.ActivationFunctionType
ALU = mybir.AluOpType
AX = mybir.AxisListType

B, S, D = 8, 512, 512
P = 128
KC = D // P
TT = S // P
FF = 4 * D
FC = FF // P
H = 16
HD = D // H
HG = P // HD
EPS = 1e-5
SCALE0 = float(D) ** -0.5
SCALE1 = float(HD) ** -0.5
PA, PB, PC, PD = range(4)
TURN_TRANSPOSES = [KC, KC, KC + 3 * H, KC]
W_UNITS = [6, FC, 8, FC]
W_FIRST = [0, 6, 6 + FC, 14 + FC]


def seq(phase, n):
    return n + B * phase


def transposes_before(phase, n):
    return KC + sum([KC * B, KC * B, (KC + 3 * H) * B][:phase]) + TURN_TRANSPOSES[phase] * n


QKV_BANK = [4, 5, 6, 7] + 2 * [4, 5, 2, 3]
N_CONST = 17
LN_STEPS = 14
MOD_LOADS = [(1,), (2,), (0,), (4,), (5,), (3,), (6, 7), (8, 9), (10, 11)]
MOD_SCALE, MOD_SHIFT, MOD_GATE = [1, 4, 7, 10], [2, 5, 6, 9], [0, 3, 8, 11]
MOD_GATE_LOAD = [2, 5, 7, 8]


def mod_vectors(i):
    return sum(len(x) for x in MOD_LOADS[:max(i, 0)])


def mod_bank(i, x):
    return 4 + (i + x) % 2


MOD_LN_AFTER = {1: 0, 4: 1, 6: 2, 8: 3}
T_ORDER = [(0, 0), (0, 1), (1, 0), (1, 1), (0, 2)]
for _h in range(H):
    T_ORDER += [x for x in ((_h + 2, 0), (_h + 2, 1), (_h + 1, 2)) if x[0] < H]
T_USE = {x: i for i, x in enumerate(T_ORDER)}


def build(nc, a):
    ctx = ExitStack()
    with ctx:
        def sb(name, shape, dt=F32):
            return ctx.enter_context(nc.sbuf_tensor(name, shape, dt))

        def sem(name):
            return ctx.enter_context(nc.semaphore(name))

        arena_at = -(-nc.sbuf_base // 32) * 32
        R = sb("pe_operands", [P, 40960], F32R)
        W_SLOT = 2048

        def r(at, *shape):
            ap = R[:, at:at + int(np.prod(shape))]
            return ap if len(shape) == 1 else ap.rearrange("p (a b) -> p a b", b=shape[-1])

        XH, XL = r(32768, KC, S), r(34816, KC, S)
        A_W = [[r(W_SLOT * (2 * w + part), KC, D) for part in range(2)] for w in range(3)]
        A_QH, A_QL, A_KH, A_KL, A_VH, A_VL, A_PH, A_PL = [r(12288 + 2048 * i, 4, 512) for i in range(8)]
        SLOT_OF = {PB: [(j + 14) % FC for j in range(FC)], PD: list(range(FC))}

        def w_chunk(phase, j):
            base = W_SLOT * SLOT_OF[phase][j]
            return (r(base, KC, P), r(base + 1024, KC, P)), (r(base + 512, D), r(base + 1536, D))

        HH = [r(36864 + 1024 * i, 512) for i in range(4)]
        HL = [r(36864 + 1024 * i + 512, 512) for i in range(4)]
        C_W = [[r(W_SLOT * (2 * w + part), KC, D) for part in range(2)] for w in range(4)]
        VS = r(16384, TT, H * 96)
        VSH = VS.rearrange("p t (h c) -> p t h c", c=96)
        QS = [r(22528 + 384 * i, TT, 96) for i in range(2)]
        KS = [r(23296 + 384 * i, TT, 96) for i in range(2)]
        QT = [r(24064 + 1024 * i, S) for i in range(3)]
        KT = [r(24576 + 1024 * i, S) for i in range(3)]
        PTH = [r(at, TT, S) for at in (27136, 36864)]
        PTL = [r(at, TT, S) for at in (29184, 38912)]
        OTH = [XH[:, k] for k in range(KC - 1)] + [r(31232, S)]
        OTL = [XL[:, k] for k in range(KC - 1)] + [r(31744, S)]
        MM = sb("minus_max_r", [P, 3, TT], F32R)
        ID_R = sb("identity_r", [P, P], F32R)

        F = sb("work", [P, 12288])

        def f(at, *shape):
            ap = F[:, at:at + int(np.prod(shape))]
            return ap if len(shape) == 1 else ap.rearrange("p (a b) -> p a b", b=shape[-1])

        XLN, Y, XRES = f(0, TT, D), f(2048, KC, S), f(4096, TT, D)
        TMP = [[f(6144, 512), f(6656, 512)], [f(10240 + 512 * i, 512) for i in range(TT)]]
        GATE = f(7168, 512)
        A_P = f(7680, TT, S)
        A_VT = [f(9728, 512), f(10240, 512)]
        BV = f(10752, 512)
        HID = [f(7680 + 512 * i, 512) for i in range(4)]
        B2 = f(9728, 512)
        KF, QF = XLN, Y
        PE = [f(7680 + 512 * i, 512) for i in range(TT)]
        OA = [f(9728, 512), f(10240, 512)]
        ROT = [f(10752, 512), f(11264, 512)]
        SLD = [F[64 * (i % 2):64 * (i % 2) + 64, 10752 + 512 * (i // 2):11264 + 512 * (i // 2)] for i in range(4)]
        RC = f(11776, 512)
        STAGE = sb("weight_stage", [P, 2, 1024])
        STAGE_W = [nc.alloc_sbuf_tensor_at(f"conditioning_weights_{i}", [P, 4096], F32, offset=arena_at + 4 * at)[:]
                   for i, at in enumerate((28672, 36864))]
        COND_ROWS = F[0:B, 7680:8704]
        VEC_ROWS = F[0:104, 8704:8832]
        MOD_ROWS = [F[0:B, 11264:11776], F[0:B, 11776:12288]]
        GATE_ROWS = sb("gate_rows", [KC * B, P])
        ID_F = sb("identity", [P, P])
        MINUS_HALF = sb("minus_half", [P, TT])
        COS, SIN = sb("cos", [P, TT, HD]), sb("sin", [P, TT, HD])
        CT = sb("cond_T", [P, 8, B])
        ST_ = sb("silu_T", [P, 4, B])
        SE = sb("silu_exp", [P, 4, B])
        VEC = sb("vectors_T", [P, 104])
        MOD = sb("mod_T", [P, 12, KC * B])
        LN_SCALE = sb("ln_scale", [P, 4, KC, B])
        LN_SHIFT = sb("ln_shift", [P, 4, KC, B])
        STATS = sb("bn_stats", [P, TT, 6])
        MV = sb("mean_var", [P, TT, 2])
        VEPS, RSTD = sb("var_eps", [P, TT]), sb("rstd", [P, TT])
        MX, NB, SM, RS = sb("row_max", [P, 4]), sb("minus_scaled_max", [P, 4]), sb("row_sum", [P, 4]), sb("row_sum_inv", [P, 4])
        DEN = sb("denominators", [P, 2, HG, S // P])
        DENI = sb("denominators_inv", [P, 2, HG, S // P])
        MX1 = sb("row_max_heads", [P, 3, TT])

        PS = ctx.enter_context(nc.psum_tensor("psum", [P, 8, 512], F32))
        VECQ, VECK, VECB1 = 80, 84, 88

        x_mid = [nc.dram_tensor(f"x_after_{c}", (B, S, D), F32, kind="Internal").ap() for c in "abc"]
        gates_d = nc.dram_tensor("gates", (4, B, D), F32, kind="Internal").ap()
        den_rows, inv_rows = (nc.dram_tensor(x, (2, HG, S), F32, kind="Internal").ap() for x in ("denominator_rows", "inverse_rows"))
        x_in = [a["x"], *x_mid]
        x_out = [*x_mid, a["out"]]

        def tokens(ap, n):
            return ap[bass.ds(n, 1)].rearrange("o (t p) d -> p (o t) d", p=P)

        const_ld, vec_done, const_evac, consts = sem("const_loaded"), sem("const_transposed"), sem("const_evacuated"), sem("pool_consts")
        idr_rdy, silu_a = sem("identity_r_ready"), sem("silu_steps")
        modw_ld, modw_done = [sem("mod_weights_0"), sem("mod_weights_1")], sem("mod_products")
        mod_rows, mod_t = sem("mod_rows_copied"), sem("mod_transposed")
        mod_evac, mod_steps = sem("mod_evacuated"), sem("scale_shift_steps")
        gate_t, gate_evac, gates_st = sem("gate_transposed"), sem("gate_evacuated"), sem("gates_stored")
        w_ld, w_split = [sem("weights_0"), sem("weights_1")], sem("weights_split")
        xln_ld, ln_v, ln_rstd = sem("ln_input_loaded"), sem("ln_steps"), sem("rstd_ready")
        t_done, t_evac = sem("transposed"), sem("transpose_evacuated")
        y_rdy, xh_rdy, xl_rdy = sem("y_ready"), sem("xh_ready"), sem("xl_ready")
        res_ld, gate_ld, tmp_rdy, res_step, res_done, stored = (
            sem("residual_loaded"), sem("gate_loaded"), sem("branch_ready"), sem("gated"), sem("residual_added"), sem("stored"))
        row_ld = sem("bias_rows_loaded")
        a_qkv, a_qkh, a_evac, a_vhi, a_vlo = sem("a_qkv_done"), sem("a_qk_hi"), sem("a_qkv_evacuated"), sem("a_v_hi"), sem("a_v_lo")
        a_s, a_mx, a_exp, a_pp, a_ppa, a_ppe, a_rs = (sem("a_scores"), sem("a_max"), sem("a_exp"), sem("a_probs_T"),
                                                     sem("a_probs_T_hi"), sem("a_probs_T_lo"), sem("a_row_sum_inv"))
        a_pv = sem("a_attn")
        m_up = {ph: sem(f"up_done_{ph}") for ph in (PB, PD)}
        m_gelu = {ph: sem(f"gelu_{ph}") for ph in (PB, PD)}
        m_hi = {ph: sem(f"hidden_hi_{ph}") for ph in (PB, PD)}
        m_lo = {ph: sem(f"hidden_lo_{ph}") for ph in (PB, PD)}
        m_down = {ph: sem(f"down_done_{ph}") for ph in (PB, PD)}
        b_gelu = sem("b_out_gelu")
        c_ones, c_qkv, c_rot, c_evac, c_rope, c_vhi = sem("c_ones"), sem("c_qkv_done"), sem("c_rot_steps"), sem("c_qkv_evacuated"), sem("c_rope"), sem("c_v_hi")
        c_stack, c_s, c_max, c_mm, c_st, c_exp = sem("c_stacks"), sem("c_scores"), sem("c_max"), sem("c_minus_max"), sem("c_scores_T"), sem("c_exp")
        c_phd, c_pl = sem("c_probs_hi"), sem("c_probs_lo")
        c_o, c_ocp, c_oadd, c_on, c_oh, c_ol = (sem("c_attn"), sem("c_attn_copied"), sem("c_attn_summed"), sem("c_attn_normalised"), sem("c_attn_hi"), sem("c_attn_lo"))
        c_wo, c_wok = sem("c_out_done"), sem("c_out_chunk_done")
        c_den, c_dencp, c_deni, c_denst, c_rcld = ([sem(f"c_denominators_stored_{q}") for q in range(HG)], sem("c_denominators_compact"), sem("c_denominators_inverted"),
                                          sem("c_denominators_inv_stored"), sem("c_denominators_inv_rows"))

        def since(eng, semaphore, value):
            if not isinstance(value, int) or value > 0:
                eng.wait_ge(semaphore, value)

        def operand_free(eng, phase, n, k):
            if phase == PC and k < KC - 1:
                since(eng, c_wok, (KC - 1) * n + k + 1)
            else:
                s, per = [(a_qkv, 12), (m_up[PB], FC), (c_qkv, 12), (m_up[PD], FC)][phase]
                since(eng, s, per * n + per)

        def transposes_c(n, h, what):
            return transposes_before(PC, n) + (T_USE[h, what] + 1 if h >= 0 else 0)

        def after(phase, n, last):
            if not last:
                return phase, n + 1
            return (phase + 1, 0) if phase < PD else None

        def over_sequences(eng, body, phase):
            body(phase, 0, True, False)
            with eng.Fori(1, B - 1) as n:
                body(phase, n, False, False)
            body(phase, B - 1, False, True)

        block = ctx.enter_context(nc.Block())

        @block.sync
        def _(sp):
            sp.dma_start(COND_ROWS[:, 0:512], a["fside"]).then_inc(const_ld, 16)
            sp.dma_start(COND_ROWS[:, 512:1024], a["cond"]).then_inc(const_ld, 16)
            at = 0
            for name in ("bc", "ada_b", "ln1_g", "ln1_b", "ln2_g", "ln2_b", "n1_g", "n1_b", "n2_g", "n2_b", "bq", "bk", "b1"):
                rows = a[name].shape[0] // P
                sp.dma_start(VEC_ROWS[at:at + rows, :], a[name].rearrange("(r c) -> r c", c=P)).then_inc(const_ld, 16)
                at += rows
            sp.dma_start(COS[:], a["cos"].rearrange("(t p) d -> p t d", p=P)).then_inc(const_ld, 16)
            sp.dma_start(SIN[:], a["sin"].rearrange("(t p) d -> p t d", p=P)).then_inc(const_ld, 16)
            def load_unit(u):
                slot = u % 2
                since(sp, w_split, 2 * (u - 1))
                phase = max(p for p in range(4) if W_FIRST[p] <= u)
                j = u - W_FIRST[phase]
                if phase in (PA, PC):
                    w = a[(("Wq0", "Wk0", "Wv0"), ("Wq1", "Wk1", "Wv1", "Wo1"))[phase == PC][j // 2]]
                    src = w.rearrange("(k p) n -> p k n", p=P)[:, 2 * (j % 2):2 * (j % 2) + 2, :]
                    sp.dma_start(STAGE[:, slot, :].rearrange("p (k n) -> p k n", n=D), src).then_inc(w_ld[slot], 16)
                else:
                    w1, w2 = (a["W1_0"], a["W2_0"]) if phase == PB else (a["W1_1"], a["W2_1"])
                    sp.dma_start(STAGE[:, slot, 0:512].rearrange("p (k n) -> p k n", n=P),
                                 w1.rearrange("(k p) n -> p k n", p=P)[:, :, j * P:(j + 1) * P]).then_inc(w_ld[slot], 16)
                    sp.dma_start(STAGE[:, slot, 512:1024], w2[j * P:(j + 1) * P, :]).then_inc(w_ld[slot], 16)

            def load_mod(i):
                since(sp, modw_done, i - 1)
                blk, width = MOD_LOADS[i][0], D * len(MOD_LOADS[i])
                w, k = (a["Wc"], 8) if blk < 6 else (a["ada_W"], 4)
                sp.dma_start(STAGE_W[i % 2].rearrange("p (k n) -> p k n", n=width),
                             w.rearrange("(k p) n -> p k n", p=P)[:, :, (blk % 6) * D:(blk % 6) * D + width]).then_inc(modw_ld[i % 2], 16)

            def store_gate(g):
                sp.wait_ge(gate_evac, g + 1)
                sp.dma_start(gates_d[g].rearrange("b (f c) -> (b f) c", c=P), GATE_ROWS[:]).then_inc(gates_st, 16)
                sp.wait_ge(gates_st, 16 * (g + 1))

            def load_ln(phase, n):
                if phase > PA:
                    since(sp, stored, 16 * (seq(phase - 1, n) + 1))
                first = isinstance(n, int) and n == 0
                if phase == PC and not first:
                    sp.wait_ge(c_stack, 4 * H * n)
                elif phase == PD and first:
                    sp.wait_ge(c_stack, 4 * H * B)
                elif first:
                    sp.wait_ge(t_done, transposes_before(phase - 1, B - 1))
                else:
                    sp.wait_ge(t_done, transposes_before(phase, n) - TURN_TRANSPOSES[phase])
                sp.dma_start(XLN, tokens(x_in[phase], n)).then_inc(xln_ld, 16)

            def load_residual(phase, n):
                turn = seq(phase, n)
                since(sp, stored, 16 * turn)
                sp.dma_start(XRES, tokens(x_in[phase], n)).then_inc(res_ld, 16)
                if not isinstance(turn, int) or turn > 0:
                    load_gate(phase, n)

            def load_gate(phase, n):
                sp.dma_start(GATE, gates_d[phase, bass.ds(n, 1), :].rearrange("o d -> (o d)").partition_broadcast(P)).then_inc(gate_ld, 16)

            sp.dma_start(XLN, tokens(x_in[PA], 0)).then_inc(xln_ld, 16)
            for i in range(2):
                load_mod(i)
            for u in range(4):
                load_unit(u)

            def denominators(n, h):
                g, q = h // HG, h % HG
                sp.wait_ge(c_ocp, H * n + h + 1)
                sp.dma_start(den_rows[g % 2, q:q + 1, :], SLD[h % 4][32:33, :]).then_inc(c_den[q], 16)
                if q == HG - 1:
                    since(sp, c_deni, KC * n + g - 1)
                    for s_ in c_den:
                        sp.wait_ge(s_, 16 * (KC * n + g + 1))
                    sp.dma_start(DEN[:, g % 2], den_rows[g % 2].rearrange("q (p i) -> p q i", i=S // P)).then_inc(c_dencp, 16)
                    sp.wait_ge(c_deni, KC * n + g + 1)
                    sp.dma_start(inv_rows[g % 2].rearrange("q (p i) -> p q i", i=S // P), DENI[:, g % 2]).then_inc(c_denst, 16)
                    sp.wait_ge(c_denst, 16 * (KC * n + g + 1))
                    since(sp, c_on, KC * n + g)
                    for r_ in range(HG):
                        sp.dma_start(RC[HD * r_:HD * r_ + HD], inv_rows[g % 2, r_].partition_broadcast(HD)).then_inc(c_rcld, 16)

            def body(phase, n, first, last):
                if first and phase in (PB, PD):
                    for j in range(4, 6):
                        load_unit(W_FIRST[phase] + j)
                nxt = after(phase, n, last)
                if phase == PC:
                    for h in range(11):
                        denominators(n, h)
                if nxt:
                    load_ln(*nxt)
                if first and phase == PA:
                    for u in range(4, 6):
                        load_unit(u)
                    sp.dma_start(BV, a["bv"].partition_broadcast(P)).then_inc(row_ld, 16)
                    for i in range(2, 4):
                        load_mod(i)
                    load_residual(PA, 0)
                    store_gate(0)
                    load_gate(PA, 0)
                    load_mod(4)
                if last and phase == PA:
                    load_mod(7)
                    load_mod(8)
                    for g in range(1, 4):
                        store_gate(g)
                if phase == PC:
                    for h in range(11, H):
                        denominators(n, h)
                if first and phase in (PB, PD):
                    for j in range(6, FC):
                        load_unit(W_FIRST[phase] + j)
                if last and phase < PD:
                    for j in range(8 if phase == PB else 4):
                        load_unit(W_FIRST[phase + 1] + j)
                sp.wait_ge(res_done, TT * (seq(phase, n) + 1))
                sp.dma_start(tokens(x_out[phase], n), XRES).then_inc(stored, 16)
                if nxt:
                    load_residual(*nxt)
                if first and phase == PA:
                    for i in range(5, 7):
                        load_mod(i)
                if last and phase == PA:
                    sp.dma_start(B2, a["b2"].partition_broadcast(P)).then_inc(row_ld, 16)

            for phase in range(4):
                over_sequences(sp, body, phase)
            sp.wait_ge(stored, 16 * 4 * B)

        @block.gpsimd
        def _(pool):
            pool.memset(ID_F[:], 0.0).then_inc(consts, 1)
            pool.memset(MINUS_HALF[:], -0.5).then_inc(consts, 1)
            pool.wait_ge(consts, 2)
            pool.affine_select(out=ID_F[:], in_=ID_F[:], compare_op=ALU.not_equal, fill=1.0, base=0,
                               pattern=[[-1, P]], channel_multiplier=1).then_inc(consts, 1)

            def rstd(turn):
                pool.wait_ge(ln_v, LN_STEPS * turn + 10)
                pool.tensor_tensor(RSTD[:], VEPS[:], MINUS_HALF[:], ALU.pow).then_inc(ln_rstd, 1)

            def add_residual(phase, n):
                turn = seq(phase, n)
                pool.wait_ge(res_ld, 16 * (turn + 1))
                tmp = TMP[phase % 2]
                for t in range(TT):
                    if phase == PB:
                        pool.wait_ge(gate_ld, 16 * (turn + 1))
                        pool.wait_ge(b_gelu, TT * n + t + 1)
                        pool.tensor_tensor(tmp[t], tmp[t], GATE, ALU.mult).then_inc(res_step, 1)
                        pool.wait_ge(res_step, TT * n + t + 1)
                    else:
                        pool.wait_ge(tmp_rdy, TT * (turn) + t + 1)
                    pool.tensor_tensor(XRES[:, t], XRES[:, t], tmp[t % len(tmp)], ALU.add).then_inc(res_done, 1)

            rstd(0)

            def plain_body(phase, n, first, last):
                nxt = after(phase, n, last)
                if nxt:
                    rstd(seq(*nxt))
                add_residual(phase, n)

            def c_body(phase, n, first, last):
                def rope(n, us):
                    for u in us:
                        dst = (QF, KF)[u // TT][:, u % TT]
                        pool.wait_ge(c_evac, 12 * n + u + 1)
                        pool.tensor_tensor(dst, dst, ROT[u % 2], ALU.add).then_inc(c_rope, 1)

                if first:
                    rope(n, range(TT))
                rope(n, range(TT, 2 * TT))
                for h in range(H):
                    for t in range(TT):
                        if t % 2 == 0:
                            pool.wait_ge(c_exp, 64 * n + TT * h + t + 1)
                        else:
                            pool.wait_ge(c_phd, 32 * n + 2 * h + t // 2 + 1)
                        pool.tensor_tensor(PTL[h % 2][:, t], PE[t], PTH[h % 2][:, t].bitcast(F32), ALU.subtract).then_inc(c_pl, 1)
                    if h == H - 2:
                        nxt = after(phase, n, last)
                        if nxt:
                            rstd(seq(*nxt))
                if not last:
                    rope(n + 1, range(TT))
                add_residual(phase, n)

            for phase in range(4):
                over_sequences(pool, c_body if phase == PC else plain_body, phase)

        @block.vector
        def _(dve):
            dve.wait_ge(consts, 3)
            dve.tensor_copy(ID_R[:], ID_F[:]).then_inc(idr_rdy, 1)
            dve.wait_ge(vec_done, 1)
            dve.tensor_copy(CT[:], PS[:, 0, 0:64].rearrange("p (k b) -> p k b", b=B)).then_inc(const_evac, 1)
            dve.tensor_copy(VEC[:], PS[:, 0, 64:168]).then_inc(const_evac, 1)
            dve.wait_ge(const_evac, 2)
            dve.wait_ge(silu_a, 1)
            dve.tensor_scalar(SE[:], SE[:], 1.0, None, ALU.add).then_inc(silu_a, 1)
            dve.wait_ge(silu_a, 2)
            dve.reciprocal(SE[:], SE[:]).then_inc(silu_a, 1)
            dve.wait_ge(silu_a, 3)
            dve.tensor_tensor(ST_[:], CT[:, 4:8], SE[:], ALU.mult).then_inc(const_evac, 1)

            def split_unit(u, dst_hi, dst_lo, w_count):
                slot = u % 2
                dve.wait_ge(w_ld[slot], w_count)
                dve.tensor_copy(dst_hi, STAGE[:, slot, :]).then_inc(w_split, 1)
                dve.wait_ge(w_split, 2 * u + 1)
                dve.tensor_tensor(dst_lo, STAGE[:, slot, :], dst_hi.bitcast(F32), ALU.subtract).then_inc(w_split, 1)

            arrived = []
            count = [0, 0]
            for u in range(sum(W_UNITS)):
                phase = max(p for p in range(4) if W_FIRST[p] <= u)
                count[u % 2] += 16 if phase in (PA, PC) else 32
                arrived.append(count[u % 2])

            def split_square(phase, j):
                u = W_FIRST[phase] + j
                base = W_SLOT * 2 * (j // 2) + 1024 * (j % 2)
                split_unit(u, R[:, base:base + 1024], R[:, base + W_SLOT:base + W_SLOT + 1024], arrived[u])

            def split_chunk(phase, j):
                u = W_FIRST[phase] + j
                base = W_SLOT * SLOT_OF[phase][j]
                split_unit(u, R[:, base:base + 1024], R[:, base + 1024:base + 2048], arrived[u])


            def copy_mod(i):
                dve.wait_ge(modw_done, i + 1)
                for x in range(len(MOD_LOADS[i])):
                    c = mod_vectors(i) + x
                    since(dve, mod_t, c - 1)
                    dve.tensor_copy(MOD_ROWS[c % 2], PS[0:B, mod_bank(i, x), :]).then_inc(mod_rows, 1)

            def evacuate_mod(i):
                for x, blk in enumerate(MOD_LOADS[i]):
                    dve.wait_ge(mod_t, mod_vectors(i) + x + 1)
                    dst = MOD[:, blk].rearrange("p (b f) -> p f b", f=KC) if blk in MOD_GATE else MOD[:, blk].rearrange("p (f b) -> p f b", b=B)
                    dve.tensor_tensor(dst, PS[:, mod_bank(i, x), 0:KC * B].rearrange("p (f b) -> p f b", b=B),
                                      VEC[:, 4 * blk:4 * blk + 4].unsqueeze(2).broadcast_to([P, KC, B]), ALU.add).then_inc(mod_evac, 1)
                if i in MOD_LN_AFTER:
                    ln = MOD_LN_AFTER[i]
                    m_g, m_b = (MOD[:, m[ln]].rearrange("p (f b) -> p f b", b=B) for m in (MOD_SCALE, MOD_SHIFT))
                    gain = VEC[:, 48 + 8 * ln:52 + 8 * ln].unsqueeze(2).broadcast_to([P, KC, B])
                    offset = VEC[:, 52 + 8 * ln:56 + 8 * ln].unsqueeze(2).broadcast_to([P, KC, B])
                    dve.wait_ge(mod_evac, mod_vectors(i + 1))
                    dve.scalar_tensor_tensor(LN_SCALE[:, ln], m_g, 1.0, gain, ALU.add, ALU.mult).then_inc(mod_steps, 1)
                    dve.scalar_tensor_tensor(LN_SHIFT[:, ln], m_g, 1.0, offset, ALU.add, ALU.mult).then_inc(mod_steps, 1)
                    dve.wait_ge(mod_steps, 3 * ln + 2)
                    dve.tensor_tensor(LN_SHIFT[:, ln], LN_SHIFT[:, ln], m_b, ALU.add).then_inc(mod_steps, 1)

            def evacuate_gate(g):
                dve.wait_ge(gate_t, g + 1)
                since(dve, gates_st, 16 * g)
                i = MOD_GATE_LOAD[g]
                dve.tensor_copy(GATE_ROWS[:], PS[0:KC * B, mod_bank(i, MOD_LOADS[i].index(MOD_GATE[g])), 256:256 + P]).then_inc(gate_evac, 1)

            def ln_moments(turn, tiles):
                if tiles[0] == 0:
                    dve.wait_ge(xln_ld, 16 * (turn + 1))
                    since(dve, ln_v, LN_STEPS * turn)
                for t in tiles:
                    dve.bn_stats(STATS[:, t], XLN[:, t]).then_inc(ln_v, 1)

            def ln_variance(turn):
                dve.wait_ge(ln_v, LN_STEPS * turn + 4)
                dve.memset(VEPS[:], EPS).then_inc(ln_v, 1)
                for t in range(TT):
                    dve.bn_aggr(MV[:, t], STATS[:, t]).then_inc(ln_v, 1)
                dve.wait_ge(ln_v, LN_STEPS * turn + 9)
                dve.tensor_tensor(VEPS[:], MV[:, :, 1], VEPS[:], ALU.add).then_inc(ln_v, 1)

            def ln_stats(turn):
                ln_moments(turn, range(TT))
                ln_variance(turn)

            def ln_norm(turn):
                dve.wait_ge(ln_rstd, turn + 1)
                for t in range(TT):
                    dve.tensor_scalar(XLN[:, t], XLN[:, t], MV[:, t, 0:1], RSTD[:, t:t + 1], ALU.subtract, ALU.mult).then_inc(ln_v, 1)

            def split_x(turn):
                for k in range(KC):
                    dve.wait_ge(xh_rdy, KC * turn + k + 1)
                    dve.tensor_tensor(XL[:, k], Y[:, k], XH[:, k].bitcast(F32), ALU.subtract).then_inc(xl_rdy, 1)

            def tmp_free(phase, turn, t):
                since(dve, res_done, TT * turn + t + 1 - len(TMP[phase % 2]))

            ln_stats(0)
            ln_norm(0)
            for i in range(2):
                copy_mod(i)
                evacuate_mod(i)
            for j in range(2):
                split_square(PA, j)
            split_x(0)
            for j in range(2, 4):
                split_square(PA, j)

            def a_body(phase, n, first, last):
                turn = seq(phase, n)
                nxt = after(phase, n, last)
                for u in range(2 * KC):
                    hi, lo, vec = ((A_QH, A_QL, VECQ), (A_KH, A_KL, VECK))[u // KC]
                    k = u % KC
                    dve.wait_ge(a_qkh, 8 * n + u + 1)
                    dve.scalar_tensor_tensor(lo[:, k], PS[:, u % 4, :], VEC[:, vec + k:vec + k + 1], hi[:, k].bitcast(F32),
                                             ALU.add, ALU.subtract).then_inc(a_evac, 1)
                    if first and u in (3, 5):
                        split_square(PA, (u + 5) // 2)
                    if last and u == 1:
                        copy_mod(5)
                    if last and u == 2:
                        evacuate_mod(5)
                    if last and u == 3:
                        evacuate_gate(1)
                        copy_mod(6)
                    if last and u == 5:
                        evacuate_mod(6)
                    if u == 6 and nxt:
                        ln_stats(seq(*nxt))
                if nxt:
                    ln_norm(seq(*nxt))
                if first:
                    dve.wait_ge(row_ld, 16)
                for t in range(TT + 1):
                    if t < TT:
                        dve.wait_ge(a_qkv, 12 * n + 8 + t + 1)
                        since(dve, a_vlo, TT * n + t - 1)
                        dve.tensor_tensor(A_VT[t % 2], PS[:, t, :], BV, ALU.add).then_inc(a_evac, 1)
                    if last and t == 0:
                        copy_mod(7)
                    if last and t == 1:
                        evacuate_mod(7)
                    if last and t == 2:
                        evacuate_gate(2)
                    if t >= 1:
                        dve.wait_ge(a_vhi, TT * n + t)
                        dve.tensor_tensor(A_VL[:, t - 1], A_VT[(t - 1) % 2], A_VH[:, t - 1].bitcast(F32), ALU.subtract).then_inc(a_vlo, 1)
                if first or last:
                    copy_mod(2 if first else 8)
                since(dve, a_exp, TT * n)
                since(dve, a_mx, 8 * n)
                for s in range(TT):
                    dve.wait_ge(a_s, TT * n + s + 1)
                    dve.reduce_max(MX[:, s:s + 1], PS[:, s, :], AX.X).then_inc(a_mx, 1)
                    dve.wait_ge(a_mx, 8 * n + 2 * s + 1)
                    dve.tensor_scalar(NB[:, s:s + 1], MX[:, s:s + 1], -SCALE0, None, ALU.mult).then_inc(a_mx, 1)
                    if (first or last) and s == 0:
                        evacuate_mod(2 if first else 8)
                    if (first or last) and s == 1:
                        evacuate_gate(0 if first else 3)
                for s in range(TT):
                    dve.wait_ge(a_ppa, TT * n + s + 1)
                    dve.tensor_tensor(A_PL[:, s], PS[:, 4 + s % 2, :], A_PH[:, s].bitcast(F32), ALU.subtract).then_inc(a_ppe, 1)
                dve.wait_ge(a_exp, TT * n + TT)
                since(dve, tmp_rdy, TT * turn)
                dve.reciprocal(RS[:], SM[:]).then_inc(a_rs, 1)
                if last:
                    dve.wait_ge(modw_done, len(MOD_LOADS))
                    for j in range(2):
                        split_chunk(PB, j)
                if nxt:
                    split_x(seq(*nxt))
                dve.wait_ge(gate_ld, 16 * (turn + 1))
                dve.wait_ge(a_rs, n + 1)
                for s in range(TT):
                    dve.wait_ge(a_pv, TT * n + s + 1)
                    tmp_free(phase, turn, s)
                    dve.scalar_tensor_tensor(TMP[0][s % 2], PS[:, s, :], RS[:, s:s + 1], GATE, ALU.mult, ALU.mult).then_inc(tmp_rdy, 1)
                if first:
                    for i in (3, 4):
                        copy_mod(i)
                    for i in (3, 4):
                        evacuate_mod(i)

            def mlp_body(phase, n, first, last):
                turn = seq(phase, n)
                nxt = after(phase, n, last)
                for j in range(FC):
                    dve.wait_ge(m_hi[phase], FC * n + j + 1)
                    dve.tensor_tensor(HL[j % 4], HID[j % 4], HH[j % 4].bitcast(F32), ALU.subtract).then_inc(m_lo[phase], 1)
                    if first and j + 2 < FC:
                        if j == 0:
                            dve.wait_ge(*((a_pv, TT * B) if phase == PB else (c_wo, TT * B)))
                        split_chunk(phase, j + 2)
                    if j == 7 and nxt:
                        ln_stats(seq(*nxt))
                    if j == 8 and nxt:
                        ln_norm(seq(*nxt))
                    if last and phase == PB and j >= 12:
                        if j == 12:
                            dve.wait_ge(m_down[PB], FC * n + 10)
                        for i in range(2):
                            split_square(PC, 2 * (j - 12) + i)
                if nxt:
                    split_x(seq(*nxt))
                if first and phase == PB:
                    dve.wait_ge(row_ld, 32)
                if phase == PD:
                    dve.wait_ge(gate_ld, 16 * (turn + 1))
                dve.wait_ge(m_down[phase], FC * n + FC)
                for t in range(TT):
                    tmp_free(phase, turn, t)
                    if phase == PB:
                        dve.tensor_tensor(TMP[1][t], PS[:, t, :], B2, ALU.add).then_inc(tmp_rdy, 1)
                    else:
                        dve.tensor_tensor(TMP[1][t], PS[:, t, :], GATE, ALU.mult).then_inc(tmp_rdy, 1)

            def c_body(phase, n, first, last):
                turn = seq(phase, n)
                nxt = after(phase, n, last)
                if first:
                    dve.wait_ge(const_ld, 16 * N_CONST)
                    dve.wait_ge(m_down[PB], FC * B)
                    for i in range(3):
                        dve.memset(KT[i][96:97].bitcast(F32), 1.0).then_inc(c_ones, 1)
                    for t in range(TT):
                        dve.memset(VSH[:, t, :, HD:64].bitcast(F32), 1.0).then_inc(c_ones, 1)

                def rope(n, us):
                    for u in us:
                        t = u % TT
                        dst = (QF, KF)[u // TT][:, t].rearrange("p (h d) -> p h d", d=HD)
                        src = PS[:, QKV_BANK[u], :].rearrange("p (h d) -> p h d", d=HD)
                        rot = ROT[u % 2].rearrange("p (h d) -> p h d", d=HD)
                        dve.wait_ge(c_qkv, 12 * n + u + 1)
                        since(dve, c_rope, 8 * n + u - 1)
                        if u == 0:
                            since(dve, c_oadd, H * n)
                        dve.tensor_tensor(dst, src, COS[:, t].unsqueeze(1).broadcast_to([P, H, HD]), ALU.mult).then_inc(c_rot, 1)
                        dve.tensor_tensor(rot[:, :, 0:HD // 2], src[:, :, 1::2],
                                          SIN[:, t, 0:HD // 2].unsqueeze(1).broadcast_to([P, H, HD // 2]), ALU.mult).then_inc(c_rot, 1)
                        dve.wait_ge(c_rot, 16 * n + 2 * u + 2)
                        dve.tensor_tensor(rot[:, :, HD // 2:HD], src[:, :, 0::2],
                                          SIN[:, t, HD // 2:HD].unsqueeze(1).broadcast_to([P, H, HD // 2]), ALU.mult).then_inc(c_evac, 1)

                if first:
                    dve.wait_ge(res_done, TT * turn)
                    rope(n, range(TT))
                rope(n, range(TT, 2 * TT))

                def stack(h):
                    i = h % 2
                    dve.wait_ge(t_done, transposes_c(n, h - 2, 1))
                    cols = slice(h * HD, (h + 1) * HD)
                    halves = ((QF, QS[i], slice(0, 2), slice(64, 96)), (KF, KS[i], slice(0, 3, 2), slice(32, 64)))
                    for src, st, hi2, _ in halves:
                        out = st.rearrange("p t (c d) -> p t c d", d=HD)[:, :, hi2, :]
                        dve.tensor_copy(out, src[:, :, cols].unsqueeze(2).broadcast_to([P, TT, 2, HD])).then_inc(c_stack, 1)
                    for x, (src, st, _, lo) in enumerate(halves):
                        dve.wait_ge(c_stack, 4 * (H * n + h) + x + 1)
                        dve.tensor_tensor(st[:, :, lo], src[:, :, cols], st[:, :, 0:HD].bitcast(F32), ALU.subtract).then_inc(c_stack, 1)

                def maximum(h, s):
                    if s == 0:
                        since(dve, c_mm, H * n + max(h - 2, 0))
                    e = TT * h + s
                    dve.wait_ge(c_s, 64 * n + e + 1)
                    dve.reduce_max(MX1[:, h % 3, s:s + 1], PS[:, e % 2, :], AX.X).then_inc(c_max, 1)

                def minus_max(h):
                    dve.wait_ge(c_max, 64 * n + TT * h + TT)
                    dve.wait_ge(t_done, transposes_c(n, h - 3, 2))
                    dve.tensor_scalar(MM[:, h % 3], MX1[:, h % 3], -1.0, None, ALU.mult).then_inc(c_mm, 1)

                def sum_head(h):
                    g, q = h // HG, h % HG
                    if q == 0:
                        since(dve, c_ol, KC * n + g - 1)
                    dve.wait_ge(c_ocp, H * n + h + 1)
                    dve.tensor_tensor(OA[g % 2][HD * q:HD * (q + 1)], PS[64:96, 5, :], SLD[h % 4][0:HD], ALU.add).then_inc(c_oadd, 1)

                def invert(g):
                    dve.wait_ge(c_dencp, 16 * (KC * n + g + 1))
                    since(dve, c_denst, 16 * (KC * n + g - 1))
                    dve.reciprocal(DENI[:, g % 2], DEN[:, g % 2]).then_inc(c_deni, 1)

                def normalise(g):
                    dve.wait_ge(c_rcld, 64 * (KC * n + g + 1))
                    dve.wait_ge(c_oadd, H * n + HG * (g + 1))
                    dve.tensor_tensor(OA[g % 2], OA[g % 2], RC, ALU.mult).then_inc(c_on, 1)

                def low(g):
                    dve.wait_ge(c_oh, KC * n + g + 1)
                    dve.tensor_tensor(OTL[g], OA[g % 2], OTH[g].bitcast(F32), ALU.subtract).then_inc(c_ol, 1)

                def v_low(t):
                    dve.wait_ge(c_vhi, TT * n + t + 1)
                    dve.tensor_tensor(VSH[:, t, :, 0:HD], PS[:, QKV_BANK[8 + t], :].rearrange("p (h d) -> p h d", d=HD),
                                      VSH[:, t, :, 64:96].bitcast(F32), ALU.subtract).then_inc(c_evac, 1)

                def prob_hi(h, t):
                    dve.wait_ge(c_exp, 64 * n + TT * h + t + 1)
                    if t == 1:
                        since(dve, c_o, H * n + h - 1)
                    dve.tensor_copy(PTH[h % 2][:, t], PE[t]).then_inc(c_phd, 1)

                dve.wait_ge(c_rope, 8 * n + 8)
                stack(0)
                v_low(0)
                stack(1)
                v_low(1)
                maximum(0, 0)
                maximum(0, 1)
                v_low(2)
                maximum(0, 2)
                maximum(0, 3)
                minus_max(0)
                stack(2)
                maximum(1, 0)
                maximum(1, 1)
                v_low(3)
                maximum(1, 2)
                maximum(1, 3)
                minus_max(1)
                for h in range(H + 1):
                    if h + 3 < H:
                        stack(h + 3)
                    if h < H:
                        prob_hi(h, 1)
                    if h in (8, 12, 16):
                        low((h - 8) // HG)
                    if h == H - 2 and nxt:
                        ln_moments(seq(*nxt), range(2))
                    if h + 2 < H:
                        maximum(h + 2, 0)
                        maximum(h + 2, 1)
                    if h in (7, 11, 15):
                        normalise((h - 7) // HG)
                    if h < H:
                        prob_hi(h, 3)
                    if h + 2 < H:
                        maximum(h + 2, 2)
                    if h >= 1:
                        sum_head(h - 1)
                    if h + 2 < H:
                        maximum(h + 2, 3)
                        minus_max(h + 2)
                    if h in (5, 9, 13):
                        invert((h - 5) // HG)
                    if h == H - 2 and nxt:
                        ln_moments(seq(*nxt), range(2, TT))
                        ln_variance(seq(*nxt))
                    if h == H - 1 and nxt:
                        ln_norm(seq(*nxt))
                if nxt:
                    split_x(seq(*nxt))
                invert(KC - 1)
                if not last:
                    rope(n + 1, range(2))
                normalise(KC - 1)
                low(KC - 1)
                if last:
                    for j in range(2):
                        split_chunk(PD, j)
                if not last:
                    rope(n + 1, range(2, TT))
                dve.wait_ge(gate_ld, 16 * (turn + 1))
                for t in range(TT):
                    dve.wait_ge(c_wo, TT * n + t + 1)
                    tmp_free(phase, turn, t)
                    dve.tensor_tensor(TMP[0][t % 2], PS[:, t, :], GATE, ALU.mult).then_inc(tmp_rdy, 1)

            for phase in range(4):
                over_sequences(dve, (a_body, mlp_body, c_body, mlp_body)[phase], phase)

        @block.scalar
        def _(act):
            act.wait_ge(const_evac, 1)
            act.activation(SE[:], CT[:, 4:8], ACT.Exp, scale=-1.0).then_inc(silu_a, 1)

            def evacuate_y(phase, n):
                turn = seq(phase, n)
                since(act, xl_rdy, KC * turn)
                if isinstance(n, int) and n == 0:
                    act.wait_ge(mod_steps, 3 * phase + 3)
                for k in range(KC):
                    act.wait_ge(t_done, transposes_before(phase, n) - KC + k + 1)
                    act.activation(Y[:, k], PS[:, 6 + k % 2, :], ACT.Identity,
                                   scale=LN_SCALE[:, phase, k, bass.ds(n, 1)], bias=LN_SHIFT[:, phase, k, bass.ds(n, 1)]).then_inc(y_rdy, 1)

            def split_x(phase, n, prev):
                turn = seq(phase, n)
                for k in range(KC):
                    if prev:
                        operand_free(act, *prev, k)
                    act.wait_ge(y_rdy, KC * turn + k + 1)
                    act.activation(XH[:, k], Y[:, k], ACT.Identity).then_inc(xh_rdy, 1)

            evacuate_y(PA, 0)
            split_x(PA, 0, None)

            def a_body(phase, n, first, last):
                nxt = after(phase, n, last)
                since(act, a_s, TT * n)
                for u in range(2 * KC):
                    hi, vec = ((A_QH, VECQ), (A_KH, VECK))[u // KC]
                    k = u % KC
                    act.wait_ge(a_qkv, 12 * n + u + 1)
                    act.activation(hi[:, k], PS[:, u % 4, :], ACT.Identity, bias=VEC[:, vec + k:vec + k + 1]).then_inc(a_qkh, 1)
                since(act, a_pv, TT * n)
                for t in range(TT):
                    act.wait_ge(a_evac, 12 * n + 8 + t + 1)
                    act.activation(A_VH[:, t], A_VT[t % 2], ACT.Identity).then_inc(a_vhi, 1)
                since(act, a_rs, n)

                def exponential(s):
                    act.wait_ge(a_mx, 8 * n + 2 * s + 2)
                    act.activation(A_P[:, s], PS[:, s, :], ACT.Exp, bias=NB[:, s:s + 1], scale=SCALE0,
                                   accum_out=SM[:, s:s + 1]).then_inc(a_exp, 1)

                def probs_hi(s):
                    act.wait_ge(a_pp, TT * n + s + 1)
                    act.activation(A_PH[:, s], PS[:, 4 + s % 2, :], ACT.Identity).then_inc(a_ppa, 1)

                for s in range(3):
                    exponential(s)
                probs_hi(0)
                exponential(3)
                probs_hi(1)
                if nxt:
                    evacuate_y(*nxt)
                probs_hi(2)
                probs_hi(3)
                if nxt:
                    split_x(*nxt, (phase, n))

            def mlp_body(phase, n, first, last):
                nxt = after(phase, n, last)
                for j in range(FC):
                    act.wait_ge(m_up[phase], FC * n + j + 1)
                    since(act, m_lo[phase], FC * n + j - 3)
                    if first and phase == PD and j == 0:
                        act.wait_ge(c_pl, 64 * B)
                    bias = VEC[:, VECB1 + j:VECB1 + j + 1] if phase == PB else 0.0
                    act.activation(HID[j % 4], PS[:, 4 + j % 2, :], ACT.Gelu, bias=bias).then_inc(m_gelu[phase], 1)
                    act.wait_ge(m_gelu[phase], FC * n + j + 1)
                    since(act, m_down[phase], FC * n + j - 3)
                    act.activation(HH[j % 4], HID[j % 4], ACT.Identity).then_inc(m_hi[phase], 1)
                    if j == 10 and nxt:
                        evacuate_y(*nxt)
                if nxt:
                    split_x(*nxt, (phase, n))
                if phase == PB:
                    for t in range(TT):
                        act.wait_ge(tmp_rdy, TT * seq(phase, n) + t + 1)
                        act.activation(TMP[1][t], TMP[1][t], ACT.Gelu).then_inc(b_gelu, 1)

            def c_body(phase, n, first, last):
                nxt = after(phase, n, last)
                if first:
                    act.wait_ge(m_down[PB], FC * B)
                since(act, c_o, H * n)

                def v_hi(t):
                    act.wait_ge(c_qkv, 12 * n + 8 + t + 1)
                    act.activation(VSH[:, t, :, 64:96], PS[:, QKV_BANK[8 + t], :].rearrange("p (h d) -> p h d", d=HD), ACT.Identity).then_inc(c_vhi, 1)

                def evacuate(h, what, rows, dst):
                    act.wait_ge(t_done, transposes_c(n, h, what))
                    act.activation(dst, PS[0:rows, 6 + T_USE[h, what] % 2, :], ACT.Identity).then_inc(t_evac, 1)

                def evacuate_q(h):
                    since(act, c_st, 64 * n + TT * max(h - 2, 0))
                    evacuate(h, 0, 96, QT[h % 3][0:96])

                def evacuate_k(h):
                    evacuate(h, 1, 96, KT[h % 3][0:96])

                def evacuate_m(h):
                    evacuate(h, 2, 1, QT[h % 3][96:97])

                def copy_out(h):
                    act.wait_ge(c_o, H * n + h + 1)
                    since(act, c_oadd, H * n + h - 3)
                    since(act, c_den[h % HG], 16 * (KC * n + h // HG))
                    if h == 0:
                        act.wait_ge(c_rope, 8 * n + 8)
                    act.activation(SLD[h % 4], PS[0:64, 5, :], ACT.Identity).then_inc(c_ocp, 1)

                def normalised_hi(g):
                    act.wait_ge(c_on, KC * n + g + 1)
                    act.activation(OTH[g], OA[g % 2], ACT.Identity).then_inc(c_oh, 1)

                def exponential(h, t):
                    e = TT * h + t
                    act.wait_ge(c_st, 64 * n + e + 1)
                    since(act, c_pl, 64 * n + e - 3)
                    if h == 0 and t == 0 and first:
                        act.wait_ge(m_lo[PB], FC * B)
                    if t == 0:
                        since(act, c_o, H * n + h - 1)
                    if t % 2 == 0:
                        act.activation(PTH[h % 2][:, t], PS[:, 2 + e % 3, :], ACT.Exp, scale=SCALE1)
                    act.activation(PE[t], PS[:, 2 + e % 3, :], ACT.Exp, scale=SCALE1).then_inc(c_exp, 1)

                v_hi(0)
                v_hi(1)
                evacuate_q(0)
                evacuate_k(0)
                v_hi(2)
                evacuate_q(1)
                evacuate_k(1)
                v_hi(3)
                evacuate_m(0)
                for h in range(H + 1):
                    if h + 2 < H:
                        evacuate_q(h + 2)
                    if h < H:
                        exponential(h, 0)
                    if h + 2 < H:
                        evacuate_k(h + 2)
                    if h < H:
                        exponential(h, 1)
                        exponential(h, 2)
                        exponential(h, 3)
                    if h == H and nxt:
                        evacuate_y(*nxt)
                    if h + 1 < H:
                        evacuate_m(h + 1)
                    if h >= 1:
                        copy_out(h - 1)
                    if h in (7, 11, 15):
                        normalised_hi((h - 7) // HG)
                if nxt:
                    split_x(*nxt, (phase, n))
                normalised_hi(KC - 1)

            for phase in range(4):
                over_sequences(act, (a_body, mlp_body, c_body, mlp_body)[phase], phase)

        @block.tensor
        def _(pe):
            def product(out, x, w, start, stop):
                (xh, xl), (wh, wl) = x, w
                pe.matmul(out, xh, wh, start=start, stop=False)
                pe.matmul(out, xh, wl, start=False, stop=False)
                return pe.matmul(out, xl, wh, start=False, stop=stop)

            pe.wait_ge(const_ld, 16 * N_CONST)
            pe.wait_ge(consts, 3)
            for k in range(8):
                pe.transpose(PS[:, 0, B * k:B * k + B], COND_ROWS[:, P * k:P * k + P], ID_F[0:B, 0:B])
            pe.transpose(PS[:, 0, 64:168], VEC_ROWS, ID_F[0:104, 0:104]).then_inc(vec_done, 1)
            pe.wait_ge(const_evac, 3)

            def mod_products(i):
                pe.wait_ge(modw_ld[i % 2], 16 * (i // 2 + 1))
                before = i - 1 if len(MOD_LOADS[i]) == 1 else i
                since(pe, mod_evac, mod_vectors(before))
                since(pe, gate_evac, sum(x < before for x in MOD_GATE_LOAD))
                vectors, kn = len(MOD_LOADS[i]), (8, 4)[i > 5]
                w = STAGE_W[i % 2].rearrange("p (k x n) -> p k x n", x=vectors, n=D)
                for x in range(vectors):
                    for k in range(kn):
                        mm = pe.matmul(PS[0:B, mod_bank(i, x), :], (CT if i < 6 else ST_)[:, k, :], w[:, k, x, :], start=k == 0, stop=k == kn - 1)
                mm.then_inc(modw_done, 1)

            def transpose_mod(i):
                for x in range(len(MOD_LOADS[i])):
                    c = mod_vectors(i) + x
                    pe.wait_ge(mod_rows, c + 1)
                    for f in range(KC):
                        mm = pe.transpose(PS[:, mod_bank(i, x), B * f:B * f + B], MOD_ROWS[c % 2][:, P * f:P * f + P], ID_F[0:B, 0:B])
                    mm.then_inc(mod_t, 1)

            def transpose_gate(g):
                i = MOD_GATE_LOAD[g]
                pe.wait_ge(mod_evac, mod_vectors(i + 1))
                pe.transpose(PS[0:KC * B, mod_bank(i, MOD_LOADS[i].index(MOD_GATE[g])), 256:256 + P], MOD[:, MOD_GATE[g]], ID_F[:]).then_inc(gate_t, 1)

            def transpose_x(phase, n, chunks=range(KC)):
                turn = seq(phase, n)
                if chunks[0] == 0:
                    pe.wait_ge(ln_v, LN_STEPS * (turn + 1))
                for k in chunks:
                    since(pe, y_rdy, KC * turn + k - 1)
                    for t in range(TT):
                        mm = pe.transpose(PS[:, 6 + k % 2, P * t:P * t + P], XLN[:, t, P * k:P * k + P], ID_F[:])
                    mm.then_inc(t_done, 1)

            for i in range(2):
                mod_products(i)
                transpose_mod(i)
            transpose_x(PA, 0)

            def a_body(phase, n, first, last):
                turn = seq(phase, n)
                nxt = after(phase, n, last)
                for u in range(2 * KC):
                    if first and u in (0, 4):
                        pe.wait_ge(w_split, u + 4)
                    if last and u == 2:
                        mod_products(5)
                    if last and u == 3:
                        transpose_mod(5)
                    if last and u == 4:
                        transpose_gate(1)
                        mod_products(6)
                    if last and u == 6:
                        transpose_mod(6)
                    fc = u % KC
                    if u < 4:
                        since(pe, tmp_rdy, TT * (turn - 1) + u + 1)
                    else:
                        pe.wait_ge(a_evac, 12 * n + u - 3)
                    wh, wl = A_W[u // KC]
                    for k in range(KC):
                        if u == 0:
                            pe.wait_ge(xl_rdy, KC * turn + k + 1)
                        cols = slice(P * fc, P * fc + P)
                        mm = product(PS[:, u % 4, :], (wh[:, k, cols], wl[:, k, cols]), (XH[:, k], XL[:, k]), k == 0, k == KC - 1)
                    mm.then_inc(a_qkv, 1)
                if first:
                    pe.wait_ge(w_split, 2 * W_FIRST[PB])
                for t in range(TT):
                    if last and t == 1:
                        mod_products(7)
                    if last and t == 2:
                        transpose_mod(7)
                    if last and t == 3:
                        transpose_gate(2)
                    pe.wait_ge(a_evac, 12 * n + 8 + t - 3)
                    wh, wl = A_W[2]
                    for k in range(KC):
                        cols = slice(P * t, P * t + P)
                        mm = product(PS[:, t, :], (XH[:, k, cols], XL[:, k, cols]), (wh[:, k], wl[:, k]), k == 0, k == KC - 1)
                    mm.then_inc(a_qkv, 1)
                if first or last:
                    mod_products(2 if first else 8)
                def transpose_p(s):
                    pe.wait_ge(a_exp, TT * n + s + 1)
                    since(pe, a_ppe, TT * n + s - 1)
                    if s == 0 and (first or last):
                        pe.wait_ge(gate_evac, 1 if first else 4)
                    for t in range(TT):
                        mm = pe.transpose(PS[:, 4 + s % 2, P * t:P * t + P], A_P[:, s, P * t:P * t + P], ID_F[:])
                    mm.then_inc(a_pp, 1)

                for s in range(TT):
                    if s == 3:
                        transpose_p(0)
                    pe.wait_ge(a_evac, 12 * n + 8 + s + 1)
                    for k in range(KC):
                        cols = slice(P * s, P * s + P)
                        mm = product(PS[:, s, :], (A_QH[:, k, cols], A_QL[:, k, cols]), (A_KH[:, k], A_KL[:, k]), k == 0, k == KC - 1)
                    mm.then_inc(a_s, 1)
                    if (first or last) and s == 0:
                        transpose_mod(2 if first else 8)
                    if (first or last) and s == 1:
                        transpose_gate(0 if first else 3)

                def attend(s):
                    pe.wait_ge(a_ppe, TT * n + s + 1)
                    if s == 0:
                        pe.wait_ge(a_vlo, TT * n + TT)
                    for t in range(TT):
                        cols = slice(P * t, P * t + P)
                        mm = product(PS[:, s, :], (A_PH[:, s, cols], A_PL[:, s, cols]), (A_VH[:, t], A_VL[:, t]), t == 0, t == TT - 1)
                    mm.then_inc(a_pv, 1)

                transpose_p(1)
                if nxt:
                    transpose_x(*nxt, range(2))
                for s in range(TT):
                    attend(s)
                    if s == 0 and nxt:
                        transpose_x(*nxt, range(2, KC))
                    if s + 2 < TT:
                        transpose_p(s + 2)
                if first:
                    for i in (3, 4):
                        mod_products(i)
                    for i in (3, 4):
                        transpose_mod(i)

            def mlp_body(phase, n, first, last):
                turn = seq(phase, n)
                nxt = after(phase, n, last)

                def up(j):
                    if first:
                        pe.wait_ge(w_split, 2 * (W_FIRST[phase] + j + 1))
                        if j < 2:
                            pe.wait_ge(*((a_ppe, TT * B) if phase == PB else (c_oadd, H * B)))
                    since(pe, m_gelu[phase], FC * n + j - 1)
                    (wh, wl), _ = w_chunk(phase, j)
                    for k in range(KC):
                        if j == 0:
                            pe.wait_ge(xl_rdy, KC * turn + k + 1)
                        mm = product(PS[:, 4 + j % 2, :], (wh[:, k], wl[:, k]), (XH[:, k], XL[:, k]), k == 0, k == KC - 1)
                    mm.then_inc(m_up[phase], 1)

                def down(j):
                    pe.wait_ge(m_lo[phase], FC * n + j + 1)
                    _, w = w_chunk(phase, j)
                    for t in range(TT):
                        if j == 0:
                            pe.wait_ge(tmp_rdy, TT * (turn - 1) + t + 1)
                        cols = slice(P * t, P * t + P)
                        mm = product(PS[:, t, :], (HH[j % 4][:, cols], HL[j % 4][:, cols]), w, j == 0, j == FC - 1)
                    mm.then_inc(m_down[phase], 1)

                up(0)
                for j in range(FC):
                    if j + 1 < FC:
                        up(j + 1)
                    down(j)
                    if j in (9, 10) and nxt:
                        transpose_x(*nxt, range(2 * (j - 9), 2 * (j - 8)))

            def c_body(phase, n, first, last):
                turn = seq(phase, n)
                nxt = after(phase, n, last)
                if first:
                    pe.wait_ge(w_split, 2 * W_FIRST[PD])
                def project(n, u, chunks=range(KC)):
                    t, turn = u % TT, seq(PC, n)
                    if chunks[0] > 0:
                        pass
                    elif u >= 4:
                        pe.wait_ge(c_evac, 12 * n + u - 3)
                        if u in (6, 7):
                            pe.wait_ge(tmp_rdy, TT * (turn - 1) + u - 3)
                    elif first:
                        if u < 2:
                            pe.wait_ge(m_gelu[PB], FC * B)
                    elif u == 0:
                        pe.wait_ge(c_exp, 64 * n)
                    elif u == 1:
                        pe.wait_ge(c_oadd, H * n)
                    if u in (2, 3):
                        pe.wait_ge(y_rdy, KC * (turn + 1))
                    wh, wl = C_W[u // TT]
                    for k in chunks:
                        if u == 0:
                            pe.wait_ge(xl_rdy, KC * turn + k + 1)
                        cols = slice(P * t, P * t + P)
                        mm = product(PS[:, QKV_BANK[u], :], (XH[:, k, cols], XL[:, k, cols]), (wh[:, k], wl[:, k]), k == 0, k == KC - 1)
                    if chunks[-1] == KC - 1:
                        mm.then_inc(c_qkv, 1)

                def transpose_bank(h, what):
                    use = T_USE[h, what]
                    if use < 2:
                        since(pe, y_rdy, KC * (turn + 1))
                    else:
                        pe.wait_ge(t_evac, 48 * n + use - 1)
                    return PS[:, 6 + use % 2, :].bitcast(F32R)

                def transpose_qk(h, what):
                    bank = transpose_bank(h, what)
                    pe.wait_ge(c_stack, 4 * (H * n + h) + what + 3)
                    st = (QS, KS)[what][h % 2]
                    for t in range(TT):
                        mm = pe.transpose(bank[0:96, P * t:P * t + P], st[:, t], ID_R[:])
                    mm.then_inc(t_done, 1)

                def transpose_m(h):
                    bank = transpose_bank(h, 2)
                    pe.wait_ge(c_mm, H * n + h + 1)
                    for t in range(TT):
                        mm = pe.transpose(bank[0:1, P * t:P * t + P], MM[:, h % 3, t:t + 1], ID_R[:])
                    mm.then_inc(t_done, 1)

                def scores(h, s):
                    e = TT * h + s
                    if s == 0:
                        pe.wait_ge(t_evac, 48 * n + T_USE[h, 1] + 1)
                    if e < 2:
                        pe.wait_ge(tmp_rdy, TT * turn)
                    else:
                        pe.wait_ge(c_max, 64 * n + e - 1)
                    pe.matmul(PS[:, e % 2, :], QT[h % 3][0:96, P * s:P * s + P], KT[h % 3][0:96], start=True, stop=True).then_inc(c_s, 1)

                def scores_t(h, t):
                    e = TT * h + t
                    if t == 0:
                        pe.wait_ge(t_evac, 48 * n + T_USE[h, 2] + 1)
                    if e == 0:
                        pe.wait_ge(c_evac, 12 * n + 12)
                    since(pe, c_exp, 64 * n + max(e - 2, 0))
                    pe.matmul(PS[:, 2 + e % 3, :], KT[h % 3][0:97, P * t:P * t + P], QT[h % 3][0:97], start=True, stop=True).then_inc(c_st, 1)

                def attend(h, t):
                    if t == 0:
                        since(pe, c_oadd, H * n + h)
                    pe.wait_ge(c_pl, 64 * n + TT * h + t + 1)
                    v = VS[:, t, 96 * h:96 * h + 96]
                    pe.matmul(PS[0:96, 5, :], v, PTH[h % 2][:, t], start=t == 0, stop=False)
                    mm = pe.matmul(PS[0:96, 5, :], v, PTL[h % 2][:, t], start=False, stop=t == TT - 1)
                    if t == TT - 1:
                        mm.then_inc(c_o, 1)

                if first:
                    for u in range(TT):
                        project(n, u)
                for u in range(TT, 10):
                    project(n, u)
                if first:
                    pe.wait_ge(c_ones, 7)
                transpose_qk(0, 0)
                transpose_qk(0, 1)
                project(n, 10, range(2))
                scores(0, 0)
                scores(0, 1)
                project(n, 10, range(2, KC))
                transpose_qk(1, 0)
                transpose_qk(1, 1)
                scores(0, 2)
                scores(0, 3)
                project(n, 11, range(2))
                scores(1, 0)
                scores(1, 1)
                project(n, 11, range(2, KC))
                transpose_m(0)
                scores(1, 2)
                scores(1, 3)
                def out_product(k, tiles):
                    wh, wl = C_W[3]
                    for t in tiles:
                        if t == 0:
                            pe.wait_ge(c_ol, KC * n + k + 1)
                            pe.wait_ge(c_max, 64 * n + 64)
                        if k == 0 and t == 2:
                            pe.wait_ge(c_exp, 64 * n + 64)
                        cols = slice(P * t, P * t + P)
                        mm = product(PS[:, t, :], (OTH[k][:, cols], OTL[k][:, cols]), (wh[:, k], wl[:, k]), k == 0, k == KC - 1)
                        if k == KC - 1:
                            mm.then_inc(c_wo, 1)
                        elif t == TT - 1:
                            mm.then_inc(c_wok, 1)

                for h in range(H):
                    ahead = h + 2 < H
                    if ahead:
                        transpose_qk(h + 2, 0)
                    scores_t(h, 0)
                    if ahead:
                        transpose_qk(h + 2, 1)
                    scores_t(h, 1)
                    scores_t(h, 2)
                    if h >= 1:
                        attend(h - 1, 0)
                        attend(h - 1, 1)
                    if ahead:
                        scores(h + 2, 0)
                        scores(h + 2, 1)
                    scores_t(h, 3)
                    if h + 1 < H:
                        transpose_m(h + 1)
                    if h >= 1:
                        attend(h - 1, 2)
                        attend(h - 1, 3)
                    if ahead:
                        scores(h + 2, 2)
                        scores(h + 2, 3)
                out_product(0, range(TT))
                attend(H - 1, 0)
                if nxt:
                    pe.wait_ge(t_evac, 48 * n + 48)
                    transpose_x(*nxt, range(2))
                attend(H - 1, 1)
                out_product(1, range(2))
                if nxt:
                    transpose_x(*nxt, range(2, KC))
                attend(H - 1, 2)
                out_product(1, range(2, TT))
                attend(H - 1, 3)
                out_product(2, range(TT))
                if not last:
                    for u in range(TT):
                        project(n + 1, u)
                out_product(3, range(TT))

            for phase in range(4):
                over_sequences(pe, (a_body, mlp_body, c_body, mlp_body)[phase], phase)


_INS = {
    "x": "x", "fside": "fside_BxS_0", "cond": "cond_1024",
    "Wq0": "L0_cond_Wq", "bq": "L0_cond_bq", "Wk0": "L0_cond_Wk", "bk": "L0_cond_bk", "Wv0": "L0_cond_Wv", "bv": "L0_cond_bv",
    "W1_0": "L0_cond_W1", "b1": "L0_cond_b1", "W2_0": "L0_cond_W2", "b2": "L0_cond_b2", "Wc": "L0_cond_Wc", "bc": "L0_cond_bc",
    "ln1_g": "L0_cond_ln1_g", "ln1_b": "L0_cond_ln1_b", "ln2_g": "L0_cond_ln2_g", "ln2_b": "L0_cond_ln2_b",
    "n1_g": "L1_cond_norm1_g", "n1_b": "L1_cond_norm1_b", "n2_g": "L1_cond_norm2_g", "n2_b": "L1_cond_norm2_b",
    "Wq1": "L1_cond_Wq", "Wk1": "L1_cond_Wk", "Wv1": "L1_cond_Wv", "Wo1": "L1_cond_Wo",
    "W1_1": "L1_cond_W1", "W2_1": "L1_cond_W2", "ada_W": "L1_cond_ada_W", "ada_b": "L1_cond_ada_b",
}


def rope_tables():
    inv = (1.0 / 10000.0 ** (np.arange(0, HD, 2, dtype=np.float32) / np.float32(HD))).astype(np.float32)
    freqs = np.outer(np.arange(S, dtype=np.float32), inv).astype(np.float32)
    emb = np.concatenate([freqs, freqs], -1)
    sign = np.where(np.arange(HD) < HD // 2, -1.0, 1.0).astype(np.float32)
    return np.cos(emb).astype(np.float32), (np.sin(emb).astype(np.float32) * sign).astype(np.float32)


def kernel(**inputs):
    import concourse.bacc as bacc
    from concourse.bass_utils import run_bass_kernel_spmd

    nc = bacc.Bacc("TRN2", target_bir_lowering=False, num_devices=1, dynamic_dma_scratch_size=1024)
    arrays = {f"in_{k}": np.ascontiguousarray(inputs[name]) for k, name in _INS.items()}
    arrays["in_cos"], arrays["in_sin"] = rope_tables()
    a = {n[3:]: nc.dram_tensor(n, v.shape, F32, kind="ExternalInput").ap() for n, v in arrays.items()}
    a["out"] = nc.dram_tensor("out_x", (B, S, D), F32, kind="ExternalOutput").ap()
    build(nc, a)
    r = run_bass_kernel_spmd(nc, [arrays], core_ids=[0])
    return r.results[0]["out_x"]
```
